# Optimizing a Trainium2 kernel written in Bass

```python
import numpy as np
import jax
import jax.numpy as jnp

def _softmax(x, axis=-1):
    return jax.nn.softmax(x, axis=axis)

def _gelu(x):
    return jax.nn.gelu(x, approximate=True)

def _silu(x):
    return jax.nn.silu(x)

def _sigmoid(x):
    return jax.nn.sigmoid(x)

def _layernorm(x, axis=-1, eps=1e-05):
    m = jnp.mean(x, axis=axis, keepdims=True)
    v = jnp.var(x, axis=axis, keepdims=True)
    return (x - m) / jnp.sqrt(v + eps)

def _scatter_add(tgt, idx, src, axis=0):
    return tgt.at[idx].add(src)

def _segment_sum(src, seg, n):
    return jax.ops.segment_sum(src, seg, n)
kernel_name = 'mk_gnn_resnorm_d2_gnn_r8_84562c'

def setup_inputs(seed: int=0):
    np.random.seed(seed)
    _w = jnp.asarray

    def _rec_inputs():
        import jax
        import jax.numpy as jnp
        _gk = jax.random.key(seed)
        x = -6.415e-05 + 1 * jax.random.normal(jax.random.fold_in(_gk, 1), (1250, 512), jnp.float32)
        _s = jax.random.randint(jax.random.fold_in(_gk, 2), (20000,), 0, 1250, jnp.int32)
        _d = jax.random.randint(jax.random.fold_in(_gk, 3), (20000,), 0, 1250, jnp.int32)
        _loop = jnp.arange(1250, dtype=jnp.int32)
        src = jnp.concatenate([_s, _d, _loop])
        dst = jnp.concatenate([_d, _s, _loop])
        _o = jnp.argsort(dst, stable=True)
        src = src[_o]
        dst = dst[_o]
        return (x, src, dst)
    x, src, dst = _rec_inputs()

    def _L0_gnn_setup():
        import jax, jax.numpy as jnp
        import numpy as np
        NEG_SLOPE = 0.2
        HEADS = 8

        def gat_conv(x, src, dst, W, att_src, att_dst, bias, heads, out_ch):
            N = x.shape[0]
            h = (x @ W).reshape(N, heads, out_ch)
            a_src = jnp.einsum('nhc,hc->nh', h, att_src)
            a_dst = jnp.einsum('nhc,hc->nh', h, att_dst)
            e = jax.nn.leaky_relu(a_src[src] + a_dst[dst], NEG_SLOPE)
            m = jax.ops.segment_max(e, dst, num_segments=N)
            m = jnp.where(jnp.isfinite(m), m, jnp.zeros_like(m))
            ex = jnp.exp(e - m[dst])
            s = jax.ops.segment_sum(ex, dst, num_segments=N)
            alpha = ex / (s[dst] + 1e-16)
            msg = h[src] * alpha[:, :, None]
            out = jax.ops.segment_sum(msg, dst, num_segments=N)
            return out.reshape(N, heads * out_ch) + bias
        key = jax.random.key(seed)
        ks = jax.random.split(key, 12)
        N, F_in, nhid, heads, ncls, E = (2500, 512, 128, HEADS, 64, 25000)
        x = jax.random.normal(ks[0], (N, F_in), dtype=jnp.float32)
        edge_index = jax.random.randint(ks[1], (2, E), 0, N, dtype=jnp.int32)

        def lin(k, fi, fo):
            return jax.random.normal(k, (fi, fo), dtype=jnp.float32) / np.sqrt(fi)
        W1 = lin(ks[2], F_in, heads * nhid)
        att_src1 = jax.random.normal(ks[3], (heads, nhid), dtype=jnp.float32) / np.sqrt(nhid)
        att_dst1 = jax.random.normal(ks[4], (heads, nhid), dtype=jnp.float32) / np.sqrt(nhid)
        b1 = jnp.zeros((heads * nhid,), dtype=jnp.float32)
        W2 = lin(ks[5], heads * nhid, heads * ncls)
        att_src2 = jax.random.normal(ks[6], (heads, ncls), dtype=jnp.float32) / np.sqrt(ncls)
        att_dst2 = jax.random.normal(ks[7], (heads, ncls), dtype=jnp.float32) / np.sqrt(ncls)
        b2 = jnp.zeros((heads * ncls,), dtype=jnp.float32)
        return {'x': x, 'edge_index': edge_index, 'W1': W1, 'att_src1': att_src1, 'att_dst1': att_dst1, 'b1': b1, 'W2': W2, 'att_src2': att_src2, 'att_dst2': att_dst2, 'b2': b2}
    _L0_gnn_all = _L0_gnn_setup()
    _L0_gnn_in = {k: v for k, v in _L0_gnn_all.items() if k in ('W1', 'att_src1', 'att_dst1', 'b1', 'W2', 'att_src2', 'att_dst2', 'b2')}
    del _L0_gnn_all

    def _L1_gnn_setup():
        import jax, jax.numpy as jnp
        import numpy as np
        D = 512
        H = 8
        DH = D // H
        F = 256
        L = 2
        N = 2500
        E = 40000
        EPS = 1e-05

        def _xavier(key, shape):
            fan_out, fan_in = (shape[-2], shape[-1])
            lim = float(np.sqrt(6.0 / (fan_in + fan_out)))
            return jax.random.uniform(key, shape, jnp.float32, -lim, lim)

        def _batchnorm(x, g, b):
            mu = jnp.mean(x, axis=0)
            var = jnp.mean(jnp.square(x - mu), axis=0)
            return (x - mu) * jax.lax.rsqrt(var + EPS) * g + b

        def _layernorm(x, g, b):
            mu = jnp.mean(x, axis=-1, keepdims=True)
            var = jnp.mean(jnp.square(x - mu), axis=-1, keepdims=True)
            return (x - mu) * jax.lax.rsqrt(var + EPS) * g + b
        key = jax.random.key(seed)
        ks = jax.random.split(key, 12)
        src = jax.random.normal(ks[0], (N, D), jnp.float32)
        edge_index = jax.random.randint(ks[1], (2, E), 0, N)
        return {'src': src, 'edge_index': edge_index, 'Wq': _xavier(ks[2], (L, D, D)), 'bq': jnp.zeros((L, D), jnp.float32), 'Wk': _xavier(ks[3], (L, D, D)), 'Wv': _xavier(ks[4], (L, D, D)), 'Wo': _xavier(ks[5], (L, D, D)), 'bo': jnp.zeros((L, D), jnp.float32), 'W1': _xavier(ks[6], (L, F, D)), 'b1': jnp.zeros((L, F), jnp.float32), 'W2': _xavier(ks[7], (L, D, F)), 'b2': jnp.zeros((L, D), jnp.float32), 'g1': jnp.ones((L, D), jnp.float32), 'beta1': jnp.zeros((L, D), jnp.float32), 'g2': jnp.ones((L, D), jnp.float32), 'beta2': jnp.zeros((L, D), jnp.float32), 'ln_g': jnp.ones((D,), jnp.float32), 'ln_b': jnp.zeros((D,), jnp.float32)}
    _L1_gnn_all = _L1_gnn_setup()
    _L1_gnn_in = {k: v for k, v in _L1_gnn_all.items() if k in ('Wq', 'bq', 'Wk', 'Wv', 'Wo', 'bo', 'W1', 'b1', 'W2', 'b2', 'g1', 'beta1', 'g2', 'beta2', 'ln_g', 'ln_b')}
    del _L1_gnn_all
    return {'x': x, 'src': src, 'dst': dst, 'L0_gnn_W1': _L0_gnn_in['W1'], 'L0_gnn_att_src1': _L0_gnn_in['att_src1'], 'L0_gnn_att_dst1': _L0_gnn_in['att_dst1'], 'L0_gnn_b1': _L0_gnn_in['b1'], 'L0_gnn_W2': _L0_gnn_in['W2'], 'L0_gnn_att_src2': _L0_gnn_in['att_src2'], 'L0_gnn_att_dst2': _L0_gnn_in['att_dst2'], 'L0_gnn_b2': _L0_gnn_in['b2'], 'L1_gnn_Wq': _L1_gnn_in['Wq'], 'L1_gnn_bq': _L1_gnn_in['bq'], 'L1_gnn_Wk': _L1_gnn_in['Wk'], 'L1_gnn_Wv': _L1_gnn_in['Wv'], 'L1_gnn_Wo': _L1_gnn_in['Wo'], 'L1_gnn_bo': _L1_gnn_in['bo'], 'L1_gnn_W1': _L1_gnn_in['W1'], 'L1_gnn_b1': _L1_gnn_in['b1'], 'L1_gnn_W2': _L1_gnn_in['W2'], 'L1_gnn_b2': _L1_gnn_in['b2'], 'L1_gnn_g1': _L1_gnn_in['g1'], 'L1_gnn_beta1': _L1_gnn_in['beta1'], 'L1_gnn_g2': _L1_gnn_in['g2'], 'L1_gnn_beta2': _L1_gnn_in['beta2'], 'L1_gnn_ln_g': _L1_gnn_in['ln_g'], 'L1_gnn_ln_b': _L1_gnn_in['ln_b']}

def reference(x, src, dst, L0_gnn_W1, L0_gnn_att_src1, L0_gnn_att_dst1, L0_gnn_b1, L0_gnn_W2, L0_gnn_att_src2, L0_gnn_att_dst2, L0_gnn_b2, L1_gnn_Wq, L1_gnn_bq, L1_gnn_Wk, L1_gnn_Wv, L1_gnn_Wo, L1_gnn_bo, L1_gnn_W1, L1_gnn_b1, L1_gnn_W2, L1_gnn_b2, L1_gnn_g1, L1_gnn_beta1, L1_gnn_g2, L1_gnn_beta2, L1_gnn_ln_g, L1_gnn_ln_b):
    import jax
    import jax.numpy as jnp

    def _L0_gnn_ref(x, edge_index, W1, att_src1, att_dst1, b1, W2, att_src2, att_dst2, b2):
        import jax, jax.numpy as jnp
        import numpy as np
        NEG_SLOPE = 0.2
        HEADS = 8

        def gat_conv(x, src, dst, W, att_src, att_dst, bias, heads, out_ch):
            N = x.shape[0]
            h = (x @ W).reshape(N, heads, out_ch)
            a_src = jnp.einsum('nhc,hc->nh', h, att_src)
            a_dst = jnp.einsum('nhc,hc->nh', h, att_dst)
            e = jax.nn.leaky_relu(a_src[src] + a_dst[dst], NEG_SLOPE)
            m = jax.ops.segment_max(e, dst, num_segments=N)
            m = jnp.where(jnp.isfinite(m), m, jnp.zeros_like(m))
            ex = jnp.exp(e - m[dst])
            s = jax.ops.segment_sum(ex, dst, num_segments=N)
            alpha = ex / (s[dst] + 1e-16)
            msg = h[src] * alpha[:, :, None]
            out = jax.ops.segment_sum(msg, dst, num_segments=N)
            return out.reshape(N, heads * out_ch) + bias
        N = x.shape[0]
        nhid = att_src1.shape[1]
        ncls = att_src2.shape[1]
        loop = jnp.arange(N, dtype=edge_index.dtype)
        src = jnp.concatenate([edge_index[0], loop])
        dst = jnp.concatenate([edge_index[1], loop])
        h = gat_conv(x, src, dst, W1, att_src1, att_dst1, b1, HEADS, nhid)
        h = jax.nn.relu(h)
        out = gat_conv(h, src, dst, W2, att_src2, att_dst2, b2, HEADS, ncls)
        return jax.nn.log_softmax(out, axis=1)

    def _L1_gnn_ref(src, edge_index, Wq, bq, Wk, Wv, Wo, bo, W1, b1, W2, b2, g1, beta1, g2, beta2, ln_g, ln_b):
        import jax, jax.numpy as jnp
        import numpy as np
        D = 512
        H = 8
        DH = D // H
        F = 256
        L = 2
        N = 2500
        E = 40000
        EPS = 1e-05

        def _xavier(key, shape):
            fan_out, fan_in = (shape[-2], shape[-1])
            lim = float(np.sqrt(6.0 / (fan_in + fan_out)))
            return jax.random.uniform(key, shape, jnp.float32, -lim, lim)

        def _batchnorm(x, g, b):
            mu = jnp.mean(x, axis=0)
            var = jnp.mean(jnp.square(x - mu), axis=0)
            return (x - mu) * jax.lax.rsqrt(var + EPS) * g + b

        def _layernorm(x, g, b):
            mu = jnp.mean(x, axis=-1, keepdims=True)
            var = jnp.mean(jnp.square(x - mu), axis=-1, keepdims=True)
            return (x - mu) * jax.lax.rsqrt(var + EPS) * g + b
        n = src.shape[0]
        scaling = float(DH) ** (-0.5)
        tgt = edge_index[1]
        srcidx = edge_index[0]
        x = src
        for l in range(L):
            q = ((x @ Wq[l].T + bq[l]) * scaling).reshape(n, H, DH)
            k = (x @ Wk[l].T).reshape(n, H, DH)
            v = (x @ Wv[l].T).reshape(n, H, DH)
            scores = jnp.einsum('ehd,ehd->eh', q[tgt], k[srcidx])
            m = jax.ops.segment_max(scores, tgt, num_segments=n)
            p = jnp.exp(scores - m[tgt])
            s = jax.ops.segment_sum(p, tgt, num_segments=n)
            w = p / (s[tgt] + 1e-16)
            agg = jax.ops.segment_sum(w[:, :, None] * v[srcidx], tgt, num_segments=n)
            attn = agg.reshape(n, D) @ Wo[l].T + bo[l]
            x = _batchnorm(x + attn, g1[l], beta1[l])
            ff = jax.nn.relu(x @ W1[l].T + b1[l]) @ W2[l].T + b2[l]
            x = _batchnorm(x + ff, g2[l], beta2[l])
        return _layernorm(x, ln_g, ln_b)
    edge_index = jnp.stack([src, dst])
    x = _layernorm(x + _L0_gnn_ref(x, edge_index, L0_gnn_W1, L0_gnn_att_src1, L0_gnn_att_dst1, L0_gnn_b1, L0_gnn_W2, L0_gnn_att_src2, L0_gnn_att_dst2, L0_gnn_b2), axis=-1)
    x = _layernorm(x + _L1_gnn_ref(x, edge_index, L1_gnn_Wq, L1_gnn_bq, L1_gnn_Wk, L1_gnn_Wv, L1_gnn_Wo, L1_gnn_bo, L1_gnn_W1, L1_gnn_b1, L1_gnn_W2, L1_gnn_b2, L1_gnn_g1, L1_gnn_beta1, L1_gnn_g2, L1_gnn_beta2, L1_gnn_ln_g, L1_gnn_ln_b), axis=-1)
    return x

_drawn_inputs = setup_inputs


def setup_inputs(seed=0):
    import zlib

    import numpy as np

    out = dict(_drawn_inputs(seed))
    spreads = {'L0_gnn_b1': (0.0, 0.1),
     'L0_gnn_b2': (0.0, 0.1),
     'L1_gnn_bq': (0.0, 0.363),
     'L1_gnn_bo': (0.0, 0.8),
     'L1_gnn_b1': (0.0, 0.267),
     'L1_gnn_b2': (0.0, 0.8),
     'L1_gnn_g1': (1.0, 0.2),
     'L1_gnn_beta1': (0.0, 0.1),
     'L1_gnn_g2': (1.0, 0.2),
     'L1_gnn_beta2': (0.0, 0.1),
     'L1_gnn_ln_g': (1.0, 0.2),
     'L1_gnn_ln_b': (0.0, 0.1)}
    factors = {'L0_gnn_att_dst1': 8.0, 'L0_gnn_att_src2': 8.0, 'L0_gnn_att_dst2': 8.0}
    for name, (base, spread) in spreads.items():
        noise = np.random.default_rng([zlib.crc32(name.encode()), seed]).standard_normal(out[name].shape)
        drawn = base * np.exp(spread * noise) if base else spread * noise
        out[name] = jnp.asarray(drawn.astype(out[name].dtype))
    for name, factor in factors.items():
        out[name] = (out[name] * factor).astype(out[name].dtype)
    return out
```

```python
from contextlib import ExitStack, contextmanager

import concourse.bass as bass
from concourse import mybir

ALU = mybir.AluOpType
ACT = mybir.ActivationFunctionType
AX_X = mybir.AxisListType.X
F32 = mybir.dt.float32
F32R = mybir.dt.float32r
F16 = mybir.dt.float16
BF16 = mybir.dt.bfloat16
I32 = mybir.dt.int32

BANK = 512
NEG_SLOPE = 0.2
GAIN = 1 / NEG_SLOPE
EPS = 1e-5
TINY = 1e-16
NO_EDGE = -1e30
FLOOR = -1e29
LEAST_COUNT = 2.0 ** -64
EXP_LN = "natural_log_exp_and_others"


def pieces(width):
    return [(a, min(BANK, width - a)) for a in range(0, width, BANK)]


def divisor(n, limit=128):
    return max(p for p in range(1, limit + 1) if n % p == 0)


class Step:

    def __init__(self, item, slot, turn, total):
        self.item, self.slot, self.turn, self.total = item, slot, turn, total

    def back(self, d):
        return Step(self.item - d, (self.slot - d) % 2, self.turn + (self.slot - d) // 2, self.total)

    def live(self):
        return not isinstance(self.item, int) or 0 <= self.item < self.total

    def first(self):
        return isinstance(self.item, int) and self.item == 0


def run_steps(eng, total, lag, emit):
    head = 2 * ((lag + 1) // 2) + 2
    for s in range(head):
        emit(Step(s, s % 2, s // 2, total))
    pairs = (total - head) // 2
    with eng.Fori(0, pairs) as i:
        for slot in range(2):
            emit(Step(i * 2 + (head + slot), slot, i + head // 2, total))
    for s in range(head + 2 * pairs, total + lag):
        emit(Step(s, s % 2, s // 2, total))


def wait_item(eng, sem, step, ago=0):
    count = step.item - ago + 1
    if not isinstance(count, int) or count > 0:
        eng.wait_ge(sem, count)


def wait_loaded(eng, sems, step):
    eng.wait_ge(sems[step.slot], (step.turn + 1) * 16)


def wait_stored(eng, sems, step, dmas=1):
    last = step.back(2)
    if last.live():
        eng.wait_ge(sems[step.slot], (last.turn + 1) * (16 * dmas))


class Unit:

    def __init__(self, head, tile, heads, tiles):
        self.head, self.tile, self.heads, self.tiles = head, tile, heads, tiles

    def shift(self, d):
        v = self.tile + d
        return Unit(self.head + v // self.tiles, v % self.tiles, self.heads, self.tiles)

    def live(self):
        return not isinstance(self.head, int) or 0 <= self.head < self.heads

    def number(self):
        return self.head * self.tiles + self.tile

    def starts(self, head):
        return isinstance(self.head, int) and self.head == head and self.tile == 0


def run_units(eng, heads, tiles, emit):
    for t in range(tiles):
        emit(Unit(0, t, heads, tiles))
    with eng.Fori(1, heads - 1) as h:
        for t in range(tiles):
            emit(Unit(h, t, heads, tiles))
    for h in (heads - 1, heads):
        for t in range(tiles):
            emit(Unit(h, t, heads, tiles))


def wait_unit(eng, sem, unit, ago=0):
    count = unit.number() - ago + 1
    if not isinstance(count, int) or count > 0:
        eng.wait_ge(sem, count)


class Kernel:

    def __init__(self, nc, x, src):
        self.nc = nc
        self.N, self.D = x.shape
        self.P = divisor(self.N)
        self.T = self.N // self.P
        self.H = 8
        self.E = src.shape[0]
        self.chunks = self.E // self.P
        self.chunk_rows = divisor(self.chunks)
        self.ctx = ExitStack()

    def sb(self, name, shape, dt=F32):
        return self.ctx.enter_context(self.nc.sbuf_tensor(name, shape, dt))

    def sem(self, name):
        self.stage_sems.append(self.nc.alloc_semaphore(name))
        return self.stage_sems[-1]

    @contextmanager
    def stage(self, name):
        self.stage_sems = []
        with ExitStack() as buffers:
            yield buffers
        self.nc.clear_and_free_semaphores(self.stage_sems)
        self.nc.all_engine_barrier()

    def dram(self, name, shape, dt=F32):
        return self.nc.dram_tensor(name, shape, dt, kind="Internal").ap()




def stage_edges(k, src, dst):
    nc, P, N = k.nc, k.P, k.N
    rows, parts = k.chunk_rows, k.chunks // k.chunk_rows
    with k.stage("stage_edges") as ctx:
        ends_int = ctx.enter_context(nc.sbuf_tensor("ends_int", [rows, 2, parts, P], I32))
        ends_f32 = ctx.enter_context(nc.sbuf_tensor("ends_f32", [rows, 2, parts, P], F32))
        ends_loaded = k.sem("ends_loaded")
        ends_cast = k.sem("ends_cast")
        ends_turned = k.sem("ends_turned")
        zeroed = k.sem("zeroed")
        padded = k.sem("padded")
        ident_made = k.sem("ident_made")
        block = ctx.enter_context(nc.Block("edges"))

        @block.sync
        def _(sp):
            for i, ends in enumerate((src, dst)):
                sp.dma_start(ends_int[:, i], ends.rearrange("(a p e) -> p a e", a=parts, p=rows)).then_inc(ends_loaded, 16)

        @block.gpsimd
        def _(pool):
            pool.memset(k.ident[:], 0.0).then_inc(zeroed, 1)
            pool.wait_ge(zeroed, 1)
            pool.affine_select(out=k.ident[:], in_=k.ident[:], compare_op=ALU.not_equal, fill=1.0,
                               base=0, pattern=[[-1, 128]], channel_multiplier=1).then_inc(ident_made, 1)
            pool.iota(k.node_row[:], [[1, N]], base=0, channel_multiplier=0,
                      allow_small_or_imprecise_dtypes=True)
            pool.memset(k.ones[:], 1.0)

        @block.vector
        def _(dve):
            dve.memset(k.end_cols[:], -1.0).then_inc(padded, 1)
            dve.wait_ge(ends_loaded, 32)
            dve.tensor_copy(ends_f32[:], ends_int[:]).then_inc(ends_cast, 1)
            dve.wait_ge(padded, 1)
            for i in range(2):
                dve.wait_ge(ends_turned, i + 1)
                dve.tensor_copy(k.end_cols[:, i, k.pad_left:k.pad_left + k.chunks],
                                k.psum[0:P, i * BANK:i * BANK + k.chunks])

        @block.tensor
        def _(pe):
            pe.wait_ge(ident_made, 1)
            pe.wait_ge(ends_cast, 1)
            for i in range(2):
                for a in range(parts):
                    turned = pe.transpose(k.psum[0:P, i * BANK + a * rows:i * BANK + (a + 1) * rows],
                                          ends_f32[:, i, a], k.ident[0:rows, 0:rows])
                turned.then_inc(ends_turned, 1)


def stage_count(k, name, first_chunk, chunks, verify):
    nc, P, T, N = k.nc, k.P, k.T, k.N
    R = 6
    groups = chunks // R
    with k.stage("stage_count") as ctx:
        src_hot = ctx.enter_context(nc.sbuf_tensor(f"src_hot_{name}", [P, R, N], BF16))
        dst_hot = ctx.enter_context(nc.sbuf_tensor(f"dst_hot_{name}", [P, R, P], BF16))
        row_total = ctx.enter_context(nc.sbuf_tensor(f"row_total_{name}", [P, T], F32))
        col_total = ctx.enter_context(nc.sbuf_tensor(f"col_total_{name}", [P, 1], F32))
        hot_ready = k.sem(f"hot_ready_{name}")
        hot_free = k.sem(f"hot_free_{name}")
        sums_free = k.sem(f"sums_free_{name}")
        total_step = k.sem(f"total_step_{name}")
        block = ctx.enter_context(nc.Block(name))
        assert chunks % R == 0

        def sums(slot, a, n):
            return k.psum[0:P, 3 * BANK * slot + a:3 * BANK * slot + a + n]

        @block.vector
        def _(dve):
            dve.sem_inc(hot_free, R)
            with dve.Fori(0, T) as t:
                with dve.Fori(0, groups) as g:
                    for r in range(R):
                        c = first_chunk(t) + g * R + r
                        dve.wait_ge(hot_free, (t * groups + g) * R + r + 1)
                        dve.tensor_scalar(src_hot[:, r], k.node_row[0:P, :], k.end_cols[:, 0, bass.ds(c, 1)], None, ALU.is_equal)
                        dve.tensor_scalar(dst_hot[:, r], k.node_row[0:P, bass.ds(t * P, P)],
                                          k.end_cols[:, 1, bass.ds(c, 1)], None, ALU.is_equal).then_inc(hot_ready, 1)
            if verify:
                dve.wait_ge(sums_free, T + 2)
                dve.tensor_reduce(col_total[:], row_total[:], AX_X, ALU.add).then_inc(total_step, 1)
                dve.wait_ge(total_step, 2)
                dve.tensor_copy(k.edges_found[:], k.psum[0:1, 6 * BANK:6 * BANK + 1])

        @block.tensor
        def _(pe):
            def group(t, slot, g, first, last):
                for r in range(R):
                    pe.wait_ge(hot_ready, (t * groups + g) * R + r + 1)
                    for a, n in pieces(N):
                        product = pe.matmul(sums(slot, a, n), dst_hot[:, r], src_hot[:, r, a:a + n],
                                            start=first and r == 0, stop=last and r == R - 1)
                    product.then_inc(hot_free, 1)

            def tile(t, slot):
                pe.wait_ge(sums_free, t + 1)
                group(t, slot, 0, True, False)
                with pe.Fori(1, groups - 1) as g:
                    group(t, slot, g, False, False)
                group(t, slot, groups - 1, False, True)

            with pe.Fori(0, T // 2) as i:
                tile(i * 2, 0)
                tile(i * 2 + 1, 1)
            if verify:
                pe.wait_ge(total_step, 1)
                pe.matmul(k.psum[0:1, 6 * BANK:6 * BANK + 1], col_total[:], k.ones[0:P, 0:1],
                          start=True, stop=True).then_inc(total_step, 1)

        @block.scalar
        def _(act):
            act.sem_inc(sums_free, 2)
            with act.Fori(0, T // 2) as i:
                for slot in range(2):
                    t = i * 2 + slot
                    act.wait_ge(hot_free, (t + 1) * groups * R + R)
                    act.activation(k.log_counts[:, t, :], sums(slot, 0, N), ACT.Copy,
                                   accum_out=row_total[:, bass.ds(t, 1)]).then_inc(sums_free, 1)


def stage_logs(k):
    nc, P, T, N = k.nc, k.P, k.T, k.N
    with k.stage("stage_logs") as ctx:
        logs = ctx.enter_context(nc.sbuf_tensor("logs", [P, 2, N], F32))
        fence = ctx.enter_context(nc.sbuf_tensor("fence", [P, 2, N], F32))
        loop_counts = ctx.enter_context(nc.sbuf_tensor("loop_counts", [P, 2, P], F32))
        loop_logs = ctx.enter_context(nc.sbuf_tensor("loop_logs", [P, 2, P], F32))
        loop_fence = ctx.enter_context(nc.sbuf_tensor("loop_fence", [P, 2, P], F32))
        least = ctx.enter_context(nc.sbuf_tensor("least", [P, 1], F32))
        least_set = k.sem("least_set")
        loops_added = k.sem("loops_added")
        fences_ready = k.sem("fences_ready")
        logs_ready = k.sem("logs_ready")
        tile_done = k.sem("tile_done")
        rows_done = k.sem("rows_done")
        block = ctx.enter_context(nc.Block("logs"))

        def diag(t):
            return k.log_counts[:, t, bass.ds(t * P, P)]

        @block.gpsimd
        def _(pool):
            pool.memset(least[:], LEAST_COUNT).then_inc(least_set, 1)
            pool.sem_inc(tile_done, 2)
            with pool.Fori(0, T // 2) as i:
                for slot in range(2):
                    t = i * 2 + slot
                    pool.wait_ge(tile_done, t + 1)
                    pool.tensor_tensor(loop_counts[:, slot], diag(t), k.ident[0:P, 0:P], ALU.add).then_inc(loops_added, 1)

        @block.scalar
        def _(act):
            act.preload_act_table_set(EXP_LN)
            act.wait_ge(least_set, 1)
            with act.Fori(0, T // 2) as i:
                for slot in range(2):
                    t = i * 2 + slot
                    act.wait_ge(tile_done, t + 1)
                    act.activation(logs[:, slot], k.log_counts[:, t, :], ACT.Ln, bias=least[:])
                    act.wait_ge(loops_added, t + 1)
                    act.activation(loop_logs[:, slot], loop_counts[:, slot], ACT.Ln, bias=least[:]).then_inc(logs_ready, 1)

        @block.vector
        def _(dve):
            with dve.Fori(0, T // 2) as i:
                for slot in range(2):
                    t = i * 2 + slot
                    dve.wait_ge(loops_added, t + 1)
                    dve.tensor_scalar(fence[:, slot], k.log_counts[:, t, :], -0.5, -2 * NO_EDGE, ALU.add, ALU.mult)
                    dve.tensor_scalar(loop_fence[:, slot], loop_counts[:, slot], -0.5, -2 * NO_EDGE, ALU.add, ALU.mult
                                      ).then_inc(fences_ready, 1)
                    dve.wait_ge(fences_ready, t + 1)
                    dve.wait_ge(logs_ready, t + 1)
                    block_at = bass.ds(t * P, P)
                    dve.tensor_tensor(k.plain_diag[:, t, :], logs[:, slot, block_at], fence[:, slot, block_at], ALU.min)
                    dve.scalar_tensor_tensor(k.log_counts[:, t, :], logs[:, slot], GAIN, fence[:, slot],
                                             ALU.mult, ALU.min).then_inc(rows_done, 1)
                    dve.wait_ge(rows_done, t + 1)
                    dve.scalar_tensor_tensor(diag(t), loop_logs[:, slot], GAIN, loop_fence[:, slot],
                                             ALU.mult, ALU.min).then_inc(tile_done, 1)


def stage_gat_project(k, name, rows, row_bias, w, att_src, att_dst, h_sb, a_dst, a_src_rows):
    nc, P, T, N, H = k.nc, k.P, k.T, k.N, k.H
    relu = row_bias is not None
    K = w.shape[0] // 128
    M = w.shape[1]
    CH = M // H
    KB = -(-K // 4)
    MB = M // BANK
    with k.stage("stage_gat_project") as ctx:
        def sb(what, shape, dt=F32):
            return ctx.enter_context(nc.sbuf_tensor(f"{what}_{name}", shape, dt))

        w_f32 = sb("w_f32", [128, K, M])
        w_high = sb("w_high", [128, K, M], F32R)
        w_low = sb("w_low", [128, K, M], F32R)
        att = sb("att", [P, 2, M])
        x_rows = sb("x_rows", [P, 2, K * 128])
        x_high = sb("x_high", [128, 2, K, P], F32R)
        x_low = sb("x_low", [128, 2, K, P], F32R)
        h_att = sb("h_att", [P, 2, 2, M])
        a_src = sb("a_src", [P, 2, H])
        a_src_t = sb("a_src_t", [H, N])
        if relu:
            bias_rows = sb("bias_rows", [P, K * 128])
            bias_loaded = k.sem(f"bias_loaded_{name}")
            x_biased = k.sem(f"x_biased_{name}")
        w_loaded = k.sem(f"w_loaded_{name}")
        att_loaded = k.sem(f"att_loaded_{name}")
        x_loaded = [k.sem(f"x_loaded{i}_{name}") for i in range(2)]
        w_high_done = k.sem(f"w_high_done_{name}")
        w_low_done = k.sem(f"w_low_done_{name}")
        x_turned = k.sem(f"x_turned_{name}")
        x_high_done = k.sem(f"x_high_done_{name}")
        x_low_done = k.sem(f"x_low_done_{name}")
        h_summed = k.sem(f"h_summed_{name}")
        h_saved = k.sem(f"h_saved_{name}")
        att_multiplied = k.sem(f"att_multiplied_{name}")
        a_reduced = k.sem(f"a_reduced_{name}")
        a_turned = k.sem(f"a_turned_{name}")
        a_saved = k.sem(f"a_saved_{name}")
        a_stored = k.sem(f"a_stored_{name}")
        block = ctx.enter_context(nc.Block(f"project_{name}"))

        def turned(slot):
            at = slot * KB * BANK
            return k.psum[:, at:at + KB * BANK].rearrange("p (b c) -> p b c", b=KB)[:, :, 0:4 * P]

        def halves(x, slot):
            return x[:, slot].rearrange("p (b c) n -> p b (c n)", b=KB)

        def h_bank(slot, m):
            at = (2 * KB + slot * MB + m) * BANK
            return k.psum[0:P, at:at + BANK]

        a_bank = k.psum[0:H, 7 * BANK:7 * BANK + P]

        @block.sync
        def _(sp):
            if relu:
                sp.dma_start(bias_rows[:], row_bias.rearrange("(o c) -> o c", o=1).to_broadcast([P, K * 128])
                             ).then_inc(bias_loaded, 16)
            sp.dma_start(w_f32[:], w.rearrange("(c p) m -> p c m", p=128)).then_inc(w_loaded, 16)

            def step(s):
                if not s.live():
                    return
                wait_item(sp, x_turned, s, ago=2)
                sp.dma_start(x_rows[:, s.slot], rows[bass.ds(s.item * P, P), :]).then_inc(x_loaded[s.slot], 16)
                if s.first():
                    for i, v in enumerate((att_src, att_dst)):
                        sp.dma_start(att[:, i], v.rearrange("(o h) c -> o (h c)", o=1).to_broadcast([P, M])
                                     ).then_inc(att_loaded, 16)

            run_steps(sp, T, 0, step)
            sp.wait_ge(a_saved, T)
            sp.dma_start(a_src_rows, a_src_t[:]).then_inc(a_stored, 16)
            sp.wait_ge(a_stored, 16)

        @block.tensor
        def _(pe):
            def step(s):
                if s.live():
                    if relu:
                        wait_item(pe, x_biased, s)
                    else:
                        wait_loaded(pe, x_loaded, s)
                    wait_item(pe, x_low_done, s, ago=2)
                    for c in range(K):
                        block_t = pe.transpose(turned(s.slot)[:, c // 4, (c % 4) * P:(c % 4 + 1) * P],
                                               x_rows[:, s.slot, c * 128:(c + 1) * 128], k.ident[0:P, 0:P])
                    block_t.then_inc(x_turned, 1)
                s = s.back(1)
                if s.live():
                    if s.first():
                        pe.wait_ge(w_low_done, 1)
                    wait_item(pe, x_low_done, s)
                    wait_item(pe, h_saved, s, ago=2)
                    for m in range(MB):
                        cols = slice(m * BANK, (m + 1) * BANK)
                        for c in range(K):
                            for i, (x, v) in enumerate(((x_high, w_high), (x_high, w_low), (x_low, w_high))):
                                product = pe.matmul(h_bank(s.slot, m), x[:, s.slot, c], v[:, c, cols],
                                                    start=c == 0 and i == 0, stop=c == K - 1 and i == 2)
                    product.then_inc(h_summed, 1)
                s = s.back(2)
                if s.live():
                    wait_item(pe, a_reduced, s)
                    wait_item(pe, a_saved, s, ago=1)
                    pe.transpose(a_bank, a_src[:, s.slot], k.ident[0:P, 0:P]).then_inc(a_turned, 1)

            run_steps(pe, T, 3, step)

        @block.scalar
        def _(act):
            act.wait_ge(w_loaded, 16)
            act.copy(w_high[:], w_f32[:]).then_inc(w_high_done, 1)

            def step(s):
                if s.live():
                    wait_item(act, x_turned, s)
                    wait_item(act, h_summed, s, ago=2)
                    act.activation(halves(x_high, s.slot), turned(s.slot), ACT.Relu if relu else ACT.Copy).then_inc(x_high_done, 1)
                s = s.back(1)
                if s.live():
                    wait_item(act, h_summed, s)
                    for m in range(MB):
                        saved = act.copy(h_sb[:, s.item, m * BANK:(m + 1) * BANK], h_bank(s.slot, m))
                    saved.then_inc(h_saved, 1)

            run_steps(act, T, 1, step)

        @block.gpsimd
        def _(pool):
            pool.wait_ge(att_loaded, 32)
            if relu:
                pool.wait_ge(bias_loaded, 16)

            def step(s):
                if s.live() and relu:
                    wait_loaded(pool, x_loaded, s)
                    pool.tensor_tensor(x_rows[:, s.slot], x_rows[:, s.slot], bias_rows[:], ALU.add).then_inc(x_biased, 1)
                s = s.back(2)
                if s.live():
                    wait_item(pool, h_saved, s)
                    wait_item(pool, a_reduced, s, ago=2)
                    for i in range(2):
                        made = pool.tensor_tensor(h_att[:, s.slot, i], h_sb[:, s.item, :], att[:, i], ALU.mult)
                    made.then_inc(att_multiplied, 1)

            run_steps(pool, T, 2, step)

        @block.vector
        def _(dve):
            dve.wait_ge(w_high_done, 1)
            dve.tensor_tensor(w_low[:], w_f32[:], w_high[:].bitcast(F32), ALU.subtract).then_inc(w_low_done, 1)

            def step(s):
                if s.live():
                    wait_item(dve, x_high_done, s)
                    if relu:
                        cut = dve.scalar_tensor_tensor(halves(x_low, s.slot), turned(s.slot), 0.0,
                                                       halves(x_high, s.slot).bitcast(F32), ALU.max, ALU.subtract)
                    else:
                        cut = dve.tensor_tensor(halves(x_low, s.slot), turned(s.slot), halves(x_high, s.slot).bitcast(F32),
                                                ALU.subtract)
                    cut.then_inc(x_low_done, 1)
                s = s.back(2)
                if s.live():
                    wait_item(dve, att_multiplied, s)
                    wait_item(dve, a_turned, s, ago=2)
                    for i, a in enumerate((a_src[:, s.slot], a_dst[:, s.item, :])):
                        total = dve.tensor_reduce(a, h_att[:, s.slot, i].rearrange("p (h c) -> p h c", h=H), AX_X, ALU.add)
                    total.then_inc(a_reduced, 1)
                s = s.back(1)
                if s.live():
                    wait_item(dve, a_turned, s)
                    dve.tensor_copy(a_src_t[:, bass.ds(s.item * P, P)], a_bank).then_inc(a_saved, 1)

            run_steps(dve, T, 3, step)


def stage_gat_attend(k, name, h_sb, a_dst, a_src_rows, out_rows):
    nc, P, T, N, H = k.nc, k.P, k.T, k.N, k.H
    CH = h_sb.shape[2] // H
    B = T // 2
    HALF = BANK // 2
    with k.stage("stage_gat_attend") as ctx:
        def sb(what, shape, dt=F32):
            return ctx.enter_context(nc.sbuf_tensor(f"{what}_{name}", shape, dt))

        a_src = sb("a_src_all", [P, H, N])
        probs = sb("probs", [P, B, N])
        probs_t = sb("probs_t", [P, 2, T, P])
        neg_max, sums, sums_safe, inverse = (sb(what, [P, T]) for what in ("neg_max", "sums", "sums_safe", "inverse"))
        final = sb("final", [P, 2, T // 2, CH])
        a_loaded = k.sem(f"a_loaded_{name}")
        a_rest_loaded = k.sem(f"a_rest_loaded_{name}")
        ramp_done = k.sem(f"ramp_done_{name}")
        logits_done = k.sem(f"logits_done_{name}")
        masked = k.sem(f"masked_{name}")
        exp_done = k.sem(f"exp_done_{name}")
        sum_safe = k.sem(f"sum_safe_{name}")
        inverted = k.sem(f"inverted_{name}")
        probs_turned = k.sem(f"probs_turned_{name}")
        probs_saved = k.sem(f"probs_saved_{name}")
        summed = k.sem(f"summed_{name}")
        final_done = k.sem(f"final_done_{name}")
        stored = [k.sem(f"stored{i}_{name}") for i in range(2)]
        block = ctx.enter_context(nc.Block(f"attend_{name}"))

        def turned(u):
            at = (u % 2) * 3 * BANK
            return k.psum[0:P, at:at + T // 2 * HALF].rearrange("p (b c) -> p b c", c=HALF)[:, :, 0:2 * P]

        def out_bank(u):
            at = (6 + u % 2) * BANK
            return k.psum[0:P, at:at + CH]

        @block.sync
        def _(sp):
            for h in range(H):
                sp.dma_start(a_src[:, h], a_src_rows[h:h + 1, :].to_broadcast([P, N])
                             ).then_inc(a_rest_loaded if h else a_loaded, 16)

            def step(n):
                if n.live() and n.tile % B == B - 1:
                    half = n.tile // B
                    wait_unit(sp, final_done, n)
                    sp.dma_start(out_rows.rearrange("(t p) m -> p t m", p=P)[:, half * B:(half + 1) * B, bass.ds(n.head * CH, CH)],
                                 final[:, half]).then_inc(stored[half], 16)

            run_units(sp, H, T, step)
            for half in range(2):
                sp.wait_ge(stored[half], 16 * H)

        @block.scalar
        def _(act):
            act.preload_act_table_set(EXP_LN)

            def step(n):
                if n.live():
                    wait_unit(act, masked, n)
                    act.activation(probs[:, n.tile % B], probs[:, n.tile % B], ACT.Exp, scale=-1.0,
                                   bias=neg_max[:, n.tile:n.tile + 1],
                                   accum_out=sums[:, n.tile:n.tile + 1]).then_inc(exp_done, 1)
                n = n.shift(-1)
                if n.live():
                    wait_unit(act, probs_turned, n)
                    wait_unit(act, summed, n, ago=2)
                    act.copy(probs_t[:, n.tile % 2].rearrange("p (b c) n -> p b (c n)", c=2), turned(n.tile)
                             ).then_inc(probs_saved, 1)
                n = n.shift(-2)
                if n.live():
                    wait_unit(act, summed, n)
                    wait_unit(act, inverted, n)
                    half, t = n.tile // B, n.tile % B
                    if t == 0 and not (isinstance(n.head, int) and n.head == 0):
                        act.wait_ge(stored[half], n.head * 16)
                    act.activation(final[:, half, t], out_bank(n.tile), ACT.Copy,
                                   scale=inverse[:, n.tile:n.tile + 1]).then_inc(final_done, 1)

            run_units(act, H, T, step)

        @block.vector
        def _(dve):
            def ramp(n):
                if n.live():
                    if n.starts(0):
                        dve.wait_ge(a_loaded, 16)
                    if n.starts(1):
                        dve.wait_ge(a_rest_loaded, 16 * (H - 1))
                    wait_unit(dve, probs_turned, n, ago=B)
                    dve.tensor_scalar(probs[:, n.tile % B], a_src[:, n.head, :], a_dst[:, n.tile, bass.ds(n.head, 1)],
                                      0.0, ALU.add, ALU.max).then_inc(ramp_done, 1)

            def logits(n):
                if n.live():
                    wait_unit(dve, ramp_done, n)
                    dve.scalar_tensor_tensor(probs[:, n.tile % B], probs[:, n.tile % B], GAIN - 1, a_src[:, n.head, :],
                                             ALU.mult, ALU.add).then_inc(logits_done, 1)

            def mask(n):
                if n.live():
                    dve.tensor_tensor_reduce(probs[:, n.tile % B], probs[:, n.tile % B], k.log_counts[:, n.tile, :],
                                             -NEG_SLOPE, -FLOOR, ALU.add, ALU.min,
                                             neg_max[:, n.tile:n.tile + 1]).then_inc(masked, 1)

            def step(n):
                ramp(n.shift(2))
                if n.shift(1).live():
                    wait_unit(dve, logits_done, n.shift(1))
                last = n.shift(-1)
                if last.live():
                    wait_unit(dve, exp_done, last)
                    dve.tensor_scalar(sums_safe[:, last.tile:last.tile + 1], sums[:, last.tile:last.tile + 1],
                                      TINY, None, ALU.add).then_inc(sum_safe, 1)
                mask(n.shift(1))
                logits(n.shift(2))
                n = last
                if n.live():
                    wait_unit(dve, sum_safe, n)
                    dve.reciprocal(inverse[:, n.tile:n.tile + 1], sums_safe[:, n.tile:n.tile + 1]
                                   ).then_inc(inverted, 1)

            for u in range(2):
                ramp(Unit(0, u, H, T))
                logits(Unit(0, u, H, T))
            dve.wait_ge(logits_done, 1)
            mask(Unit(0, 0, H, T))
            run_units(dve, H, T, step)

        @block.tensor
        def _(pe):
            def step(n):
                if n.live():
                    wait_unit(pe, exp_done, n)
                    wait_unit(pe, probs_saved, n, ago=2)
                    for i in range(T):
                        block_t = pe.transpose(turned(n.tile)[:, i // 2, (i % 2) * P:(i % 2 + 1) * P],
                                               probs[:, n.tile % B, i * P:(i + 1) * P], k.ident[0:P, 0:P])
                    block_t.then_inc(probs_turned, 1)
                n = n.shift(-1)
                if n.live():
                    wait_unit(pe, probs_saved, n)
                    wait_unit(pe, final_done, n, ago=2)
                    for i in range(T):
                        total = pe.matmul(out_bank(n.tile), probs_t[:, n.tile % 2, i],
                                          h_sb[:, i, bass.ds(n.head * CH, CH)], start=i == 0, stop=i == T - 1)
                    total.then_inc(summed, 1)

            run_units(pe, H, T, step)


def stage_gat_finish(k, gat_rows, bias, x, x_rows, x_cols):
    nc, P, T, N, D = k.nc, k.P, k.T, k.N, k.D
    C = D // 128
    with k.stage("stage_gat_finish") as ctx:
        def sb(what, shape, dt=F32):
            return ctx.enter_context(nc.sbuf_tensor(f"{what}_gf", shape, dt))

        g = sb("g", [P, T, D])
        y = sb("y", [P, T, D])
        e = sb("e", [P, 2, D])
        normal = sb("normal", [P, 2, D])
        cols = sb("cols", [128, 2, C, P])
        neg_max, sums, shift = sb("neg_max", [P, T]), sb("sums", [P, T]), sb("shift", [P, T])
        logs = sb("logs", [P, T])
        stats = sb("stats", [P, T, 6])
        moments = sb("moments", [P, T, 2])
        spread, deviation, inverse = sb("spread", [P, T]), sb("deviation", [P, T]), sb("inverse", [P, T])
        bias_rows = sb("bias_rows", [P, D])
        bias_loaded, g_biased = k.sem("bias_loaded_gf"), k.sem("g_biased_gf")
        g_loaded, x_loaded = k.sem("g_loaded"), k.sem("x_loaded_gf")
        max_done, exp_done, logs_done = k.sem("max_done_gf"), k.sem("exp_done_gf"), k.sem("logs_done_gf")
        shift_done, added, stats_done = k.sem("shift_done_gf"), k.sem("added_gf"), k.sem("stats_done_gf")
        moments_done, spread_done = k.sem("moments_done_gf"), k.sem("spread_done_gf")
        deviation_done, inverse_done = k.sem("deviation_done_gf"), k.sem("inverse_done_gf")
        normed, turned, cols_saved = k.sem("normed_gf"), k.sem("turned_gf"), k.sem("cols_saved_gf")
        rows_stored = [k.sem(f"rows_stored{i}_gf") for i in range(2)]
        cols_stored = [k.sem(f"cols_stored{i}_gf") for i in range(2)]
        block = ctx.enter_context(nc.Block("gat_finish"))

        def bank(slot):
            return k.psum[:, slot * BANK:slot * BANK + C * P]

        @block.sync
        def _(sp):
            sp.dma_start(bias_rows[:], bias.rearrange("(o c) -> o c", o=1).to_broadcast([P, D])).then_inc(bias_loaded, 16)
            sp.dma_start(g[:], gat_rows.rearrange("(t p) d -> p t d", p=P)).then_inc(g_loaded, 16)
            sp.dma_start(y[:], x.rearrange("(t p) d -> p t d", p=P)).then_inc(x_loaded, 16)

            def step(s):
                wait_item(sp, normed, s)
                sp.dma_start(x_rows[bass.ds(s.item * P, P), :], normal[:, s.slot]).then_inc(rows_stored[s.slot], 16)

            run_steps(sp, T, 0, step)
            for i in range(2):
                sp.wait_ge(rows_stored[i], 16 * T // 2)
                sp.wait_ge(cols_stored[i], 16 * T // 2)

        @block.gpsimd
        def _(pool):
            pool.wait_ge(bias_loaded, 16)
            pool.wait_ge(g_loaded, 16)
            with pool.Fori(0, T) as t:
                pool.tensor_tensor(g[:, t, :], g[:, t, :], bias_rows[:], ALU.add).then_inc(g_biased, 1)

        @block.vector
        def _(dve):
            with dve.Fori(0, T) as t:
                dve.wait_ge(g_biased, t + 1)
                dve.tensor_reduce(neg_max[:, bass.ds(t, 1)], g[:, t, :], AX_X, ALU.max, negate=True).then_inc(max_done, 1)
            dve.wait_ge(logs_done, 1)
            dve.wait_ge(max_done, T)
            dve.tensor_tensor(shift[:], neg_max[:], logs[:], ALU.subtract).then_inc(shift_done, 1)
            dve.wait_ge(shift_done, 1)
            dve.wait_ge(x_loaded, 16)
            with dve.Fori(0, T) as t:
                dve.scalar_tensor_tensor(y[:, t, :], g[:, t, :], shift[:, bass.ds(t, 1)], y[:, t, :],
                                         ALU.add, ALU.add).then_inc(added, 1)
                dve.wait_ge(added, t + 1)
                dve.bn_stats(stats[:, t, :], y[:, t, :]).then_inc(stats_done, 1)
            dve.wait_ge(stats_done, T)
            for t in range(T):
                dve.bn_aggr(moments[:, t], stats[:, t]).then_inc(moments_done, 1)
            dve.wait_ge(moments_done, T)
            dve.tensor_scalar(spread[:], moments[:, :, 1], EPS, None, ALU.add).then_inc(spread_done, 1)
            dve.wait_ge(deviation_done, 1)
            dve.reciprocal(inverse[:], deviation[:]).then_inc(inverse_done, 1)
            dve.wait_ge(inverse_done, 1)

            def norm(s):
                wait_stored(dve, rows_stored, s)
                wait_item(dve, turned, s, ago=2)
                dve.tensor_scalar(normal[:, s.slot], y[:, s.item, :], moments[:, s.item, 0:1],
                                  inverse[:, bass.ds(s.item, 1)], ALU.subtract, ALU.mult).then_inc(normed, 1)

            run_steps(dve, T, 0, norm)

        @block.scalar
        def _(act):
            act.preload_act_table_set(EXP_LN)

            def softmax(s):
                wait_item(act, max_done, s)
                wait_item(act, exp_done, s, ago=2)
                act.activation(e[:, s.slot], g[:, s.item, :], ACT.Exp, bias=neg_max[:, bass.ds(s.item, 1)],
                               accum_out=sums[:, bass.ds(s.item, 1)]).then_inc(exp_done, 1)

            run_steps(act, T, 0, softmax)
            act.wait_ge(exp_done, T)
            act.activation(logs[:], sums[:], ACT.Ln).then_inc(logs_done, 1)
            act.wait_ge(spread_done, 1)
            act.activation(deviation[:], spread[:], ACT.Sqrt).then_inc(deviation_done, 1)

            def save(s):
                wait_item(act, turned, s)
                wait_stored(act, cols_stored, s)
                act.copy(cols[:, s.slot].rearrange("p c n -> p (c n)"), bank(s.slot)).then_inc(cols_saved, 1)
                wait_item(act, cols_saved, s)
                act.dma_start(x_cols.rearrange("(c p) n -> p c n", p=128)[:, :, bass.ds(s.item * P, P)],
                             cols[:, s.slot]).then_inc(cols_stored[s.slot], 16)

            run_steps(act, T, 0, save)

        @block.tensor
        def _(pe):
            def step(s):
                wait_item(pe, normed, s)
                wait_item(pe, cols_saved, s, ago=2)
                for c in range(C):
                    block_t = pe.transpose(bank(s.slot)[:, c * P:(c + 1) * P], normal[:, s.slot, c * 128:(c + 1) * 128],
                                           k.ident[0:P, 0:P])
                block_t.then_inc(turned, 1)

            run_steps(pe, T, 0, step)


def stage_plain_counts(k):
    nc, P, T = k.nc, k.P, k.T
    with k.stage("stage_plain_counts") as ctx:
        scaled = k.sem("mask_scaled")
        block = ctx.enter_context(nc.Block("plain_counts"))

        @block.vector
        def _(dve):
            with dve.Fori(0, T) as t:
                dve.tensor_scalar(k.log_counts[:, t, :], k.log_counts[:, t, :], NEG_SLOPE, None, ALU.mult).then_inc(scaled, 1)
                dve.wait_ge(scaled, t + 1)
                dve.tensor_copy(k.log_counts[:, t, bass.ds(t * P, P)], k.plain_diag[:, t, :])


def stage_turn_weights(k, name, jobs):
    nc = k.nc
    parts = [(w, high, low, o) for w, high, low in jobs for o in range(w.shape[0] // 128)]
    widest = max(w.shape[1] for w, _, _ in jobs)
    total = len(parts)
    assert total % 2 == 0
    with k.stage("stage_turn_weights") as ctx:
        rows = ctx.enter_context(nc.sbuf_tensor(f"w_rows_{name}", [128, total, widest], F32))
        loaded = [k.sem(f"w_rows_loaded{i}_{name}") for i in range(2)]
        turned, high_done, low_done = (k.sem(f"w_{what}_{name}") for what in ("turned", "high_done", "low_done"))
        block = ctx.enter_context(nc.Block(f"weights_{name}"))

        def bank(j, width):
            return k.psum[:, (j % 4) * BANK:(j % 4) * BANK + width]

        def part_of(j, half):
            w, high, low, o = parts[j]
            return (low if half else high)[:, :, o * 128:(o + 1) * 128]

        def blocks(j, width):
            return bank(j, width).rearrange("p (c o) -> p c o", o=128)

        @block.sync
        def _(sp):
            for j, (w, _, _, o) in enumerate(parts):
                sp.dma_start(rows[:, j, 0:w.shape[1]], w[o * 128:(o + 1) * 128, :]).then_inc(loaded[j * 2 // total], 16)

        @block.tensor
        def _(pe):
            for j, (w, _, _, o) in enumerate(parts):
                if j * 2 % total == 0:
                    pe.wait_ge(loaded[j * 2 // total], 8 * total)
                if j >= 4:
                    pe.wait_ge(low_done, j - 3)
                for c in range(w.shape[1] // 128):
                    block_t = pe.transpose(bank(j, w.shape[1])[:, c * 128:(c + 1) * 128],
                                           rows[:, j, c * 128:(c + 1) * 128], k.ident[:])
                block_t.then_inc(turned, 1)

        @block.scalar
        def _(act):
            for j, (w, _, _, o) in enumerate(parts):
                act.wait_ge(turned, j + 1)
                act.copy(part_of(j, 0), blocks(j, w.shape[1])).then_inc(high_done, 1)

        @block.vector
        def _(dve):
            for j, (w, _, _, o) in enumerate(parts):
                dve.wait_ge(high_done, j + 1)
                dve.tensor_tensor(part_of(j, 1), blocks(j, w.shape[1]), part_of(j, 0).bitcast(F32), ALU.subtract
                                  ).then_inc(low_done, 1)


def halves(nc, ctx, name, ins, outs):
    return [ctx.enter_context(nc.sbuf_tensor(f"{name}_{half}", [128, ins, outs], F32R)) for half in ("high", "low")]


def three_passes(pe, out, x_high, x_low, w_high, w_low, first, last):
    pe.matmul(out, w_high, x_high, start=first, stop=False)
    pe.matmul(out, w_high, x_low, start=False, stop=False)
    return pe.matmul(out, w_low, x_high, start=False, stop=last)


def stage_qkv(k, x_cols, wq, wk, wv, bq, q_halves, k_halves, v_halves):
    nc, P, T, N, D, H = k.nc, k.P, k.T, k.N, k.D, k.H
    C, CH = D // 128, D // H
    W = P + P % 2
    SCALE = float(CH) ** -0.5
    with k.stage("stage_qkv") as ctx:
        def sb(what, shape, dt=F32):
            return ctx.enter_context(nc.sbuf_tensor(f"{what}_qkv", shape, dt))

        x = sb("x", [128, 2, C, W])
        x_high, x_low = sb("x_high", [128, 2, C, W], F32R), sb("x_low", [128, 2, C, W], F32R)
        q = sb("q", [128, C, P])
        q_out = sb("q_out", [128, 2, 2, C, P], F32R)
        k_out = sb("k_out", [128, 2, 2, C, P], F32R)
        bias, scaled_bias = sb("bias", [128, C]), sb("scaled_bias", [128, C])
        bias_loaded, bias_scaled, padded, high_done, low_done, q_summed, k_summed, v_summed, q_saved, q_high_done, \
            q_low_done, k_high_done, k_low_done, v_high_done, v_low_done = (
                k.sem(f"{what}_qkv") for what in ("bias_loaded", "bias_scaled", "padded", "high_done", "low_done", "q_summed",
                                                  "k_summed", "v_summed", "q_saved", "q_high_done", "q_low_done",
                                                  "k_high_done", "k_low_done", "v_high_done", "v_low_done"))
        x_loaded, q_stored, k_stored = (
            [k.sem(f"{what}{slot}_qkv") for slot in range(2)] for what in ("x_loaded", "q_stored", "k_stored"))
        block = ctx.enter_context(nc.Block("qkv"))

        def bank(slot, i):
            return k.psum[:, (slot * 3 + i) * BANK:(slot * 3 + i + 1) * BANK]

        def by_feature(slot, i):
            return bank(slot, i)[:, 0:C * W].rearrange("p (c n) -> p c n", n=W)

        def v_bank(slot):
            return bank(slot, 2)[0:P].rearrange("p (h c) -> p h c", h=H)

        @block.sync
        def _(sp):
            sp.dma_start(bias[:], bq.rearrange("(c p) -> p c", p=128), allow_slow_non_contiguous=True).then_inc(bias_loaded, 16)
            sp.wait_ge(padded, 1)

            def step(s):
                if s.live():
                    wait_item(sp, low_done, s, ago=2)
                    sp.dma_start(x[:, s.slot, :, 0:P],
                                 x_cols.rearrange("(c p) n -> p c n", p=128)[:, :, bass.ds(s.item * P, P)]
                                 ).then_inc(x_loaded[s.slot], 16)
                s = s.back(2)
                if s.live():
                    nodes = bass.ds(s.item * P, P)
                    wait_item(sp, k_low_done, s)
                    wait_item(sp, q_low_done, s)
                    for odd in range(2):
                        for copy in range(2):
                            for half in range(2):
                                to = q_halves.rearrange("(c odd) (copy p) half n -> odd copy half p c n", odd=2, copy=2)
                                sp.dma_start(to[odd, copy, half][:, :, nodes],
                                             q_out[odd * CH:(odd + 1) * CH, s.slot, half].bitcast(F32)).then_inc(q_stored[s.slot], 16)
                    for odd in range(2):
                        for half in range(2):
                            to = k_halves[half * CH:(half + 1) * CH].rearrange("p (c odd) n -> p odd c n", odd=2)
                            sp.dma_start(to[:, odd][:, :, nodes].bitcast(F32),
                                         k_out[odd * CH:(odd + 1) * CH, s.slot, half].bitcast(F32)).then_inc(k_stored[s.slot], 16)

            run_steps(sp, T, 2, step)
            for i in range(2):
                sp.wait_ge(q_stored[i], (16 * 8 * T // 2))
                sp.wait_ge(k_stored[i], (16 * 4 * T // 2))

        @block.tensor
        def _(pe):
            def step(s):
                wait_item(pe, low_done, s)
                wait_item(pe, q_saved, s, ago=2)
                wait_item(pe, k_low_done, s, ago=2)
                wait_item(pe, v_low_done, s, ago=2)
                for i, (w, summed) in enumerate(((wq, q_summed), (wk, k_summed))):
                    for o in range(C):
                        for c in range(C):
                            total = three_passes(pe, by_feature(s.slot, i)[:, o], x_high[:, s.slot, c], x_low[:, s.slot, c],
                                                 w[0][:, c, o * 128:(o + 1) * 128], w[1][:, c, o * 128:(o + 1) * 128],
                                                 c == 0, c == C - 1)
                    total.then_inc(summed, 1)
                for c in range(C):
                    xh, xl = x_high[:, s.slot, c, 0:P], x_low[:, s.slot, c, 0:P]
                    for i, (v, w) in enumerate(((xh, wv[0]), (xh, wv[1]), (xl, wv[0]))):
                        total = pe.matmul(bank(s.slot, 2)[0:P], v, w[:, c, :], start=c == 0 and i == 0,
                                          stop=c == C - 1 and i == 2)
                total.then_inc(v_summed, 1)

            run_steps(pe, T, 0, step)

        @block.scalar
        def _(act):
            act.wait_ge(bias_scaled, 1)

            def step(s):
                if s.live():
                    wait_loaded(act, x_loaded, s)
                    wait_item(act, v_summed, s, ago=2)
                    act.copy(x_high[:, s.slot], x[:, s.slot]).then_inc(high_done, 1)
                s = s.back(1)
                if s.live():
                    wait_item(act, q_summed, s)
                    wait_item(act, q_low_done, s, ago=1)
                    for c in range(C):
                        saved = act.activation(q[:, c], by_feature(s.slot, 0)[:, c, 0:P], ACT.Identity,
                                               bias=scaled_bias[:, c:c + 1], scale=SCALE)
                    saved.then_inc(q_saved, 1)
                    wait_item(act, q_saved, s)
                    wait_stored(act, q_stored, s, 8)
                    act.copy(q_out[:, s.slot, 0], q[:]).then_inc(q_high_done, 1)
                    wait_item(act, k_summed, s)
                    wait_stored(act, k_stored, s, 4)
                    act.copy(k_out[:, s.slot, 0], by_feature(s.slot, 1)[:, :, 0:P]).then_inc(k_high_done, 1)
                    wait_item(act, v_summed, s)
                    act.copy(v_halves[:, s.item, :, 0:CH], v_bank(s.slot)).then_inc(v_high_done, 1)

            run_steps(act, T, 1, step)

        @block.vector
        def _(dve):
            dve.memset(x[:, :, :, P:W], 0.0).then_inc(padded, 1)
            dve.wait_ge(bias_loaded, 16)
            dve.tensor_scalar(scaled_bias[:], bias[:], SCALE, None, ALU.mult).then_inc(bias_scaled, 1)

            def step(s):
                if s.live():
                    wait_item(dve, high_done, s)
                    dve.tensor_tensor(x_low[:, s.slot], x[:, s.slot], x_high[:, s.slot].bitcast(F32), ALU.subtract
                                      ).then_inc(low_done, 1)
                s = s.back(1)
                if s.live():
                    wait_item(dve, k_high_done, s)
                    dve.tensor_tensor(k_out[:, s.slot, 1], by_feature(s.slot, 1)[:, :, 0:P],
                                      k_out[:, s.slot, 0].bitcast(F32), ALU.subtract).then_inc(k_low_done, 1)
                    wait_item(dve, v_high_done, s)
                    dve.tensor_tensor(v_halves[:, s.item, :, CH:2 * CH], v_bank(s.slot),
                                      v_halves[:, s.item, :, 0:CH].bitcast(F32), ALU.subtract).then_inc(v_low_done, 1)

            run_steps(dve, T, 1, step)

        @block.gpsimd
        def _(pool):
            def step(s):
                wait_item(pool, q_high_done, s)
                pool.tensor_tensor(q_out[:, s.slot, 1], q[:], q_out[:, s.slot, 0].bitcast(F32), ALU.subtract
                                   ).then_inc(q_low_done, 1)

            run_steps(pool, T, 0, step)


def stage_attend(k, q_halves, k_halves, v_halves, out_rows):
    nc, P, T, N, D, H = k.nc, k.P, k.T, k.N, k.D, k.H
    CH = D // H
    B = T // 2
    HALF = BANK // 2
    with k.stage("stage_attend") as ctx:
        def sb(what, shape, dt=F32):
            return ctx.enter_context(nc.sbuf_tensor(f"{what}_att", shape, dt))

        q = sb("q", [128, T, 2, P], F32R)
        probs = sb("probs", [P, B, N])
        probs_high, probs_low = sb("probs_high", [P, 2, T, P], F32R), sb("probs_low", [P, 2, T, P], F32R)
        neg_max, sums, sums_safe, inverse = (sb(what, [P, T]) for what in ("neg_max", "sums", "sums_safe", "inverse"))
        scaled, final = sb("scaled", [P, B, 2 * CH]), sb("final", [P, 2, B, CH])
        q_loaded = [k.sem(f"q_loaded{t}_att") for t in range(T)]
        stored = [k.sem(f"stored{i}_att") for i in range(2)]
        scored, masked, exp_done, sum_safe, inverted, turned_done, high_done, low_done, summed, scaled_done, final_done = (
            k.sem(f"{what}_att") for what in ("scored", "masked", "exp_done", "sum_safe", "inverted", "turned_done",
                                              "high_done", "low_done", "summed", "scaled_done", "final_done"))
        block = ctx.enter_context(nc.Block("attend"))

        scores = k.psum[0:P, 0:N]

        def turned():
            return k.psum[0:P, 3 * BANK:3 * BANK + T // 2 * HALF].rearrange("p (b c) -> p b c", c=HALF)[:, :, 0:2 * P]

        def pairs(x, u):
            return x[:, u % 2].rearrange("p (b c) n -> p b (c n)", c=2)

        def out_bank(u):
            at = (6 + u % 2) * BANK
            return k.psum[0:P, at:at + 2 * CH]

        def units(eng, emit):
            run_units(eng, H, T, emit)

        @block.sync
        def _(sp):
            def load(n):
                if n.live():
                    wait_unit(sp, scored, n, ago=T)
                    sp.dma_start(q[:, n.tile].bitcast(F32),
                                 q_halves[bass.ds(n.head, 1), :, :, n.tile * P:(n.tile + 1) * P].rearrange("o p f n -> (o p) f n")
                                 ).then_inc(q_loaded[n.tile], 16)

            def step(n):
                load(n.shift(6))
                if n.tile % B == 1:
                    n = n.shift(-2)
                    if n.live():
                        half = n.tile // B
                        wait_unit(sp, final_done, n)
                        sp.dma_start(out_rows.rearrange("(t p) m -> p t m", p=P)[:, half * B:(half + 1) * B, bass.ds(n.head * CH, CH)],
                                     final[:, half]).then_inc(stored[half], 16)

            for u in range(6):
                load(Unit(0, u, H, T))
            units(sp, step)
            for half in range(2):
                sp.wait_ge(stored[half], 16 * H)

        @block.tensor
        def _(pe):
            def score(n):
                if n.live():
                    pe.wait_ge(q_loaded[n.tile], (n.head + 1) * 16)
                    wait_unit(pe, masked, n, ago=1)
                    for a, width in pieces(N):
                        for half in range(2):
                            total = pe.matmul(scores[:, a:a + width], q[:, n.tile, half], k_halves[:, n.head, a:a + width],
                                              start=half == 0, stop=half == 1)
                    total.then_inc(scored, 1)

            def step(n):
                if n.live():
                    wait_unit(pe, exp_done, n)
                    wait_unit(pe, low_done, n, ago=1)
                    for i in range(T):
                        block_t = pe.transpose(turned()[:, i // 2, (i % 2) * P:(i % 2 + 1) * P],
                                               probs[:, n.tile % B, i * P:(i + 1) * P], k.ident[0:P, 0:P])
                    block_t.then_inc(turned_done, 1)
                m = n.shift(-1)
                if m.live():
                    wait_unit(pe, low_done, m)
                    wait_unit(pe, scaled_done, m, ago=2)
                    for i in range(T):
                        for x in (probs_high, probs_low):
                            total = pe.matmul(out_bank(m.tile), x[:, m.tile % 2, i], v_halves[:, i, m.head, :],
                                              start=i == 0 and x is probs_high, stop=i == T - 1 and x is probs_low)
                    total.then_inc(summed, 1)
                score(n.shift(2))

            for u in range(2):
                score(Unit(0, u, H, T))
            units(pe, step)

        @block.scalar
        def _(act):
            act.preload_act_table_set(EXP_LN)

            def exponential(n):
                if n.live():
                    wait_unit(act, masked, n)
                    act.activation(probs[:, n.tile % B], probs[:, n.tile % B], ACT.Exp, scale=-1.0,
                                   bias=neg_max[:, n.tile:n.tile + 1],
                                   accum_out=sums[:, n.tile:n.tile + 1]).then_inc(exp_done, 1)

            def step(n):
                if n.live():
                    wait_unit(act, turned_done, n)
                    wait_unit(act, summed, n, ago=2)
                    act.copy(pairs(probs_high, n.tile), turned()).then_inc(high_done, 1)
                exponential(n.shift(1))
                n = n.shift(-2)
                if n.live():
                    wait_unit(act, summed, n)
                    wait_unit(act, inverted, n)
                    wait_unit(act, final_done, n, ago=B)
                    act.activation(scaled[:, n.tile % B], out_bank(n.tile), ACT.Copy,
                                   scale=inverse[:, n.tile:n.tile + 1]).then_inc(scaled_done, 1)

            exponential(Unit(0, 0, H, T))
            units(act, step)

        @block.vector
        def _(dve):
            def invert(n):
                if n.live():
                    wait_unit(dve, sum_safe, n)
                    dve.reciprocal(inverse[:, n.tile:n.tile + 1], sums_safe[:, n.tile:n.tile + 1]).then_inc(inverted, 1)

            def wait_mask(n):
                if n.live():
                    wait_unit(dve, scored, n)
                    wait_unit(dve, turned_done, n, ago=B)

            def mask(n):
                if n.live():
                    dve.tensor_tensor_reduce(probs[:, n.tile % B], scores, k.log_counts[:, n.tile, :],
                                             -1.0, -FLOOR, ALU.add, ALU.min, neg_max[:, n.tile:n.tile + 1]).then_inc(masked, 1)

            def step(n):
                wait_mask(n.shift(1))
                invert(n.shift(-1))
                mask(n.shift(1))
                if n.live():
                    wait_unit(dve, exp_done, n)
                    dve.tensor_scalar(sums_safe[:, n.tile:n.tile + 1], sums[:, n.tile:n.tile + 1],
                                      TINY, None, ALU.add).then_inc(sum_safe, 1)
                    wait_unit(dve, high_done, n)
                    dve.tensor_tensor(pairs(probs_low, n.tile), turned(), pairs(probs_high, n.tile).bitcast(F32),
                                      ALU.subtract).then_inc(low_done, 1)

            wait_mask(Unit(0, 0, H, T))
            mask(Unit(0, 0, H, T))
            units(dve, step)

        @block.gpsimd
        def _(pool):
            def step(n):
                if n.live():
                    wait_unit(pool, scaled_done, n)
                    half, t = n.tile // B, n.tile % B
                    if t == 0 and not (isinstance(n.head, int) and n.head == 0):
                        pool.wait_ge(stored[half], n.head * 16)
                    pool.tensor_tensor(final[:, half, t], scaled[:, n.tile % B, 0:CH], scaled[:, n.tile % B, CH:2 * CH],
                                       ALU.add).then_inc(final_done, 1)

            units(pool, step)


def stage_out(k, rows, x_cols, w, bo, y):
    nc, P, T, N, D = k.nc, k.P, k.T, k.N, k.D
    C = D // 128
    W = P + P % 2
    with k.stage("stage_out") as ctx:
        def sb(what, shape, dt=F32):
            return ctx.enter_context(nc.sbuf_tensor(f"{what}_out", shape, dt))

        a_rows, x = sb("a_rows", [P, 2, D]), sb("x", [128, 2, C, P])
        a_high, a_low = sb("a_high", [128, 2, C, W], F32R), sb("a_low", [128, 2, C, W], F32R)
        zeros, bias = sb("zeros", [128, 2, C]), sb("bias", [128, C])
        bias_loaded, zeroed, padded, turned_done, high_done, low_done, summed, added = (
            k.sem(f"{what}_out") for what in ("bias_loaded", "zeroed", "padded", "turned_done", "high_done", "low_done",
                                              "summed", "added"))
        a_loaded, x_loaded = ([k.sem(f"{what}{slot}_out") for slot in range(2)] for what in ("a_loaded", "x_loaded"))
        block = ctx.enter_context(nc.Block("out"))

        def turned(slot):
            return k.psum[:, slot * BANK:slot * BANK + C * P].rearrange("p (c n) -> p c n", n=P)

        def result(slot):
            return k.psum[:, (2 + slot) * BANK:(2 + slot) * BANK + C * W].rearrange("p (c n) -> p c n", n=W)

        @block.sync
        def _(sp):
            sp.dma_start(bias[:], bo.rearrange("(c p) -> p c", p=128), allow_slow_non_contiguous=True).then_inc(bias_loaded, 16)

            def step(s):
                nodes = bass.ds(s.item * P, P)
                wait_item(sp, added, s, ago=2)
                sp.dma_start(a_rows[:, s.slot], rows[nodes, :]).then_inc(a_loaded[s.slot], 16)
                sp.dma_start(x[:, s.slot], x_cols.rearrange("(c p) n -> p c n", p=128)[:, :, nodes]
                             ).then_inc(x_loaded[s.slot], 16)

            run_steps(sp, T, 0, step)

        @block.gpsimd
        def _(pool):
            pool.memset(zeros[:], 0.0).then_inc(zeroed, 1)
            pool.wait_ge(zeroed, 1)
            for v in (a_high, a_low):
                made = pool.tensor_copy(v[:, :, :, P:W].rearrange("p s c o -> p (s c) o"),
                                        zeros[:].rearrange("p s (c o) -> p (s c) o", o=1))
            made.then_inc(padded, 1)

        @block.tensor
        def _(pe):
            pe.wait_ge(padded, 1)

            def step(s):
                if s.live():
                    wait_loaded(pe, a_loaded, s)
                    wait_item(pe, low_done, s, ago=2)
                    for c in range(C):
                        block_t = pe.transpose(turned(s.slot)[:, c], a_rows[:, s.slot, c * 128:(c + 1) * 128], k.ident[0:P, 0:P])
                    block_t.then_inc(turned_done, 1)
                s = s.back(1)
                if s.live():
                    wait_item(pe, low_done, s)
                    wait_item(pe, added, s, ago=2)
                    for o in range(C):
                        for c in range(C):
                            total = three_passes(pe, result(s.slot)[:, o], a_high[:, s.slot, c], a_low[:, s.slot, c],
                                                 w[0][:, c, o * 128:(o + 1) * 128], w[1][:, c, o * 128:(o + 1) * 128],
                                                 c == 0, c == C - 1)
                    total.then_inc(summed, 1)

            run_steps(pe, T, 1, step)

        @block.scalar
        def _(act):
            def step(s):
                wait_item(act, turned_done, s)
                wait_item(act, summed, s, ago=2)
                act.copy(a_high[:, s.slot, :, 0:P], turned(s.slot)).then_inc(high_done, 1)

            run_steps(act, T, 0, step)

        @block.vector
        def _(dve):
            dve.wait_ge(bias_loaded, 16)

            def step(s):
                if s.live():
                    wait_item(dve, high_done, s)
                    dve.tensor_tensor(a_low[:, s.slot, :, 0:P], turned(s.slot), a_high[:, s.slot, :, 0:P].bitcast(F32),
                                      ALU.subtract).then_inc(low_done, 1)
                s = s.back(1)
                if s.live():
                    wait_item(dve, summed, s)
                    wait_loaded(dve, x_loaded, s)
                    for c in range(C):
                        made = dve.scalar_tensor_tensor(y[:, c, bass.ds(s.item * P, P)], result(s.slot)[:, c, 0:P],
                                                        bias[:, c:c + 1], x[:, s.slot, c], ALU.add, ALU.add)
                    made.then_inc(added, 1)

            run_steps(dve, T, 1, step)


def stage_feed_forward(k, w1, b1, w2, b2, y):
    nc, P, T, N, D = k.nc, k.P, k.T, k.N, k.D
    C, F = D // 128, b1.shape[0] // 128
    W = P + P % 2
    with k.stage("stage_feed_forward") as ctx:
        def sb(what, shape, dt=F32):
            return ctx.enter_context(nc.sbuf_tensor(f"{what}_ff", shape, dt))

        x_high, x_low = sb("x_high", [128, 2, C, W], F32R), sb("x_low", [128, 2, C, W], F32R)
        f, f_high, f_low = sb("f", [128, 2, F, W]), sb("f_high", [128, 2, F, W], F32R), sb("f_low", [128, 2, F, W], F32R)
        zeros = sb("zeros", [128, 2, C])
        bias1, bias2 = sb("bias1", [128, F]), sb("bias2", [128, C])
        bias_loaded, zeroed, padded, x_high_done, x_low_done, f_summed, f_saved, f_high_done, f_low_done, summed, added = (
            k.sem(f"{what}_ff") for what in ("bias_loaded", "zeroed", "padded", "x_high_done", "x_low_done", "f_summed",
                                             "f_saved", "f_high_done", "f_low_done", "summed", "added"))
        block = ctx.enter_context(nc.Block("feed_forward"))

        def hidden(slot):
            return k.psum[:, slot * BANK:slot * BANK + F * W].rearrange("p (c n) -> p c n", n=W)

        def result(slot):
            return k.psum[:, (2 + slot) * BANK:(2 + slot) * BANK + C * W].rearrange("p (c n) -> p c n", n=W)

        @block.sync
        def _(sp):
            sp.dma_start(bias1[:], b1.rearrange("(c p) -> p c", p=128), allow_slow_non_contiguous=True).then_inc(bias_loaded, 16)
            sp.dma_start(bias2[:], b2.rearrange("(c p) -> p c", p=128), allow_slow_non_contiguous=True).then_inc(bias_loaded, 16)

        @block.gpsimd
        def _(pool):
            pool.memset(zeros[:], 0.0).then_inc(zeroed, 1)
            pool.wait_ge(zeroed, 1)
            for v in (x_high, x_low):
                made = pool.tensor_copy(v[:, :, :, P:W].rearrange("p s c o -> p (s c) o"),
                                        zeros[:].rearrange("p s (c o) -> p (s c) o", o=1))
            made.then_inc(padded, 1)

            def step(s):
                wait_item(pool, f_high_done, s)
                pool.tensor_tensor(f_low[:, s.slot], f[:, s.slot], f_high[:, s.slot].bitcast(F32), ALU.subtract
                                   ).then_inc(f_low_done, 1)

            run_steps(pool, T, 0, step)

        @block.tensor
        def _(pe):
            pe.wait_ge(padded, 1)

            def step(s):
                if s.live():
                    wait_item(pe, x_low_done, s)
                    wait_item(pe, f_saved, s, ago=2)
                    for o in range(F):
                        for c in range(C):
                            total = three_passes(pe, hidden(s.slot)[:, o], x_high[:, s.slot, c], x_low[:, s.slot, c],
                                                 w1[0][:, c, o * 128:(o + 1) * 128], w1[1][:, c, o * 128:(o + 1) * 128],
                                                 c == 0, c == C - 1)
                    total.then_inc(f_summed, 1)
                s = s.back(1)
                if s.live():
                    wait_item(pe, f_low_done, s)
                    wait_item(pe, added, s, ago=2)
                    for o in range(C):
                        for c in range(F):
                            total = three_passes(pe, result(s.slot)[:, o], f_high[:, s.slot, c], f_low[:, s.slot, c],
                                                 w2[0][:, c, o * 128:(o + 1) * 128], w2[1][:, c, o * 128:(o + 1) * 128],
                                                 c == 0, c == F - 1)
                    total.then_inc(summed, 1)

            run_steps(pe, T, 1, step)

        @block.scalar
        def _(act):
            act.wait_ge(bias_loaded, 32)

            def step(s):
                if s.live():
                    wait_item(act, f_summed, s, ago=2)
                    act.copy(x_high[:, s.slot, :, 0:P], y[:, :, bass.ds(s.item * P, P)]).then_inc(x_high_done, 1)
                s = s.back(1)
                if s.live():
                    wait_item(act, f_summed, s)
                    wait_item(act, f_low_done, s, ago=2)
                    for c in range(F):
                        saved = act.activation(f[:, s.slot, c], hidden(s.slot)[:, c], ACT.Relu, bias=bias1[:, c:c + 1])
                    saved.then_inc(f_saved, 1)
                    wait_item(act, f_saved, s)
                    wait_item(act, summed, s, ago=2)
                    act.copy(f_high[:, s.slot], f[:, s.slot]).then_inc(f_high_done, 1)

            run_steps(act, T, 1, step)

        @block.vector
        def _(dve):
            dve.wait_ge(bias_loaded, 32)

            def step(s):
                if s.live():
                    wait_item(dve, x_high_done, s)
                    dve.tensor_tensor(x_low[:, s.slot, :, 0:P], y[:, :, bass.ds(s.item * P, P)],
                                      x_high[:, s.slot, :, 0:P].bitcast(F32), ALU.subtract).then_inc(x_low_done, 1)
                s = s.back(2)
                if s.live():
                    wait_item(dve, summed, s)
                    for c in range(C):
                        cols = y[:, c, bass.ds(s.item * P, P)]
                        made = dve.scalar_tensor_tensor(cols, result(s.slot)[:, c, 0:P], bias2[:, c:c + 1], cols,
                                                        ALU.add, ALU.add)
                    made.then_inc(added, 1)

            run_steps(dve, T, 2, step)


def stage_batch_norm(k, name, gamma, beta, y, x_cols):
    nc, N, D = k.nc, k.N, k.D
    C = D // 128
    parts = -(-N // BANK)
    cuts = [N * i // parts for i in range(parts + 1)]
    with k.stage("stage_batch_norm") as ctx:
        def sb(what, shape, dt=F32):
            return ctx.enter_context(nc.sbuf_tensor(f"{what}_{name}", shape, dt))

        g, b = sb("g", [128, C]), sb("b", [128, C])
        stats, moments = sb("stats", [128, C, parts * 6]), sb("moments", [128, C, 2])
        spread, deviation, inverse = sb("spread", [128, C]), sb("deviation", [128, C]), sb("inverse", [128, C])
        scale, moved, shift = sb("scale", [128, C]), sb("moved", [128, C]), sb("shift", [128, C])
        loaded, stats_done, moments_done, spread_done, deviation_done, inverse_done, scale_done, moved_done, shift_done, \
            normed, stored = (
                k.sem(f"{what}_{name}") for what in ("loaded", "stats_done", "moments_done", "spread_done", "deviation_done",
                                                     "inverse_done", "scale_done", "moved_done", "shift_done", "normed",
                                                     "stored"))
        block = ctx.enter_context(nc.Block(name))

        @block.sync
        def _(sp):
            sp.dma_start(g[:], gamma.rearrange("(c p) -> p c", p=128), allow_slow_non_contiguous=True).then_inc(loaded, 16)
            sp.dma_start(b[:], beta.rearrange("(c p) -> p c", p=128), allow_slow_non_contiguous=True).then_inc(loaded, 16)
            if x_cols is not None:
                for c in range(C):
                    sp.wait_ge(normed, c + 1)
                    sp.dma_start(x_cols[c * 128:(c + 1) * 128, :], y[:, c]).then_inc(stored, 16)
                sp.wait_ge(stored, (16 * C))

        @block.vector
        def _(dve):
            for c in range(C):
                for i in range(parts):
                    done = dve.bn_stats(stats[:, c, 6 * i:6 * i + 6], y[:, c, cuts[i]:cuts[i + 1]])
            done.then_inc(stats_done, 1)
            dve.wait_ge(stats_done, 1)
            for c in range(C):
                done = dve.bn_aggr(moments[:, c], stats[:, c])
            done.then_inc(moments_done, 1)
            dve.wait_ge(moments_done, 1)
            dve.tensor_scalar(spread[:], moments[:, :, 1], EPS, None, ALU.add).then_inc(spread_done, 1)
            dve.wait_ge(deviation_done, 1)
            dve.reciprocal(inverse[:], deviation[:]).then_inc(inverse_done, 1)
            dve.wait_ge(inverse_done, 1)
            dve.wait_ge(loaded, 32)
            dve.tensor_tensor(scale[:], inverse[:], g[:], ALU.mult).then_inc(scale_done, 1)
            dve.wait_ge(scale_done, 1)
            dve.tensor_tensor(moved[:], moments[:, :, 0], scale[:], ALU.mult).then_inc(moved_done, 1)
            dve.wait_ge(moved_done, 1)
            dve.tensor_tensor(shift[:], b[:], moved[:], ALU.subtract).then_inc(shift_done, 1)
            dve.wait_ge(shift_done, 1)
            for c in range(C):
                dve.tensor_scalar(y[:, c], y[:, c], scale[:, c:c + 1], shift[:, c:c + 1], ALU.mult, ALU.add
                                  ).then_inc(normed, 1)

        @block.scalar
        def _(act):
            act.wait_ge(spread_done, 1)
            act.activation(deviation[:], spread[:], ACT.Sqrt).then_inc(deviation_done, 1)


def stage_final(k, x_cols, ln_g, ln_b, x_rows, out):
    nc, P, T, N, D = k.nc, k.P, k.T, k.N, k.D
    C = D // 128
    with k.stage("stage_final") as ctx:
        def sb(what, shape, dt=F32):
            return ctx.enter_context(nc.sbuf_tensor(f"{what}_fin", shape, dt))

        cols = sb("cols", [128, 2, C, P])
        z, x1 = sb("z", [P, T, D]), sb("x1", [P, T, D])
        g, b = sb("g", [P, D]), sb("b", [P, D])
        stats, moments = sb("stats", [P, T, 6]), [sb(f"moments{r}", [P, T, 2]) for r in range(2)]
        spread, deviation = [[sb(f"{what}{r}", [P, T]) for r in range(2)] for what in ("spread", "deviation")]
        inverse = [sb(f"inverse{r}", [P, T]) for r in range(2)]
        cols_loaded = [k.sem(f"cols_loaded{i}_fin") for i in range(2)]
        x1_loaded, gb_loaded, turned, saved, stats_done, moments_done, spread_done, deviation_done, \
            inverse_done, normed, gained, shifted, added, out_stored = (
                k.sem(f"{what}_fin") for what in ("x1_loaded", "gb_loaded", "turned", "saved", "stats_done",
                                                  "moments_done", "spread_done", "deviation_done", "inverse_done",
                                                  "normed", "gained", "shifted", "added", "out_stored"))
        block = ctx.enter_context(nc.Block("final"))

        def bank(slot):
            return k.psum[0:P, slot * BANK:(slot + 1) * BANK]

        @block.sync
        def _(sp):
            def load(s):
                wait_item(sp, turned, s, ago=2)
                sp.dma_start(cols[:, s.slot], x_cols.rearrange("(c p) n -> p c n", p=128)[:, :, bass.ds(s.item * P, P)]
                             ).then_inc(cols_loaded[s.slot], 16)

            run_steps(sp, T, 0, load)
            sp.dma_start(x1[:], x_rows.rearrange("(t p) d -> p t d", p=P)).then_inc(x1_loaded, 16)
            for v, w in ((g, ln_g), (b, ln_b)):
                sp.dma_start(v[:], w.rearrange("(o d) -> o d", o=1).to_broadcast([P, D])).then_inc(gb_loaded, 16)
            with sp.Fori(0, T) as t:
                sp.wait_ge(normed, T + t + 1)
                sp.dma_start(out[bass.ds(t * P, P), :], z[:, t, :]).then_inc(out_stored, 16)
            sp.wait_ge(out_stored, 16 * T)

        @block.tensor
        def _(pe):
            def step(s):
                wait_loaded(pe, cols_loaded, s)
                wait_item(pe, saved, s, ago=2)
                for c in range(C):
                    block_t = pe.transpose(bank(s.slot)[:, c * 128:(c + 1) * 128], cols[:, s.slot, c], k.ident[:])
                block_t.then_inc(turned, 1)

            run_steps(pe, T, 0, step)

        @block.scalar
        def _(act):
            def step(s):
                wait_item(act, turned, s)
                act.copy(z[:, s.item, :], bank(s.slot)).then_inc(saved, 1)

            run_steps(act, T, 0, step)
            for r in range(2):
                act.wait_ge(spread_done, r + 1)
                act.activation(deviation[r][:], spread[r][:], ACT.Sqrt).then_inc(deviation_done, 1)

        @block.gpsimd
        def _(pool):
            pool.wait_ge(gb_loaded, 32)
            with pool.Fori(0, T) as t:
                pool.wait_ge(gained, t + 1)
                pool.tensor_tensor(z[:, t, :], z[:, t, :], b[:], ALU.add).then_inc(shifted, 1)

        @block.vector
        def _(dve):
            def stats_of(t):
                dve.bn_stats(stats[:, t, :], z[:, t, :]).then_inc(stats_done, 1)

            def invert(r):
                dve.wait_ge(stats_done, (r + 1) * T)
                for t in range(T):
                    dve.bn_aggr(moments[r][:, t], stats[:, t]).then_inc(moments_done, 1)
                dve.wait_ge(moments_done, (r + 1) * T)
                dve.tensor_scalar(spread[r][:], moments[r][:, :, 1], EPS, None, ALU.add).then_inc(spread_done, 1)
                dve.wait_ge(deviation_done, r + 1)
                dve.reciprocal(inverse[r][:], deviation[r][:]).then_inc(inverse_done, 1)
                dve.wait_ge(inverse_done, r + 1)

            def norm(r, t):
                return dve.tensor_scalar(z[:, t, :], z[:, t, :], moments[r][:, t, 0:1], inverse[r][:, bass.ds(t, 1)],
                                         ALU.subtract, ALU.mult).then_inc(normed, 1)

            with dve.Fori(0, T) as t:
                dve.wait_ge(saved, t + 1)
                stats_of(t)
            invert(0)
            dve.wait_ge(gb_loaded, 32)
            with dve.Fori(0, T) as t:
                norm(0, t)
                dve.wait_ge(normed, t + 1)
                dve.tensor_tensor(z[:, t, :], z[:, t, :], g[:], ALU.mult).then_inc(gained, 1)
            dve.wait_ge(x1_loaded, 16)
            with dve.Fori(0, T) as t:
                dve.wait_ge(shifted, t + 1)
                dve.tensor_tensor(z[:, t, :], z[:, t, :], x1[:, t, :], ALU.add).then_inc(added, 1)
                dve.wait_ge(added, t + 1)
                stats_of(t)
            invert(1)
            with dve.Fori(0, T) as t:
                norm(1, t)


def build(nc, **a):
    src, dst, x = a["src"], a["dst"], a["x"]
    k = Kernel(nc, x, src)
    P, T, N, D, H = k.P, k.T, k.N, k.D, k.H
    with k.ctx:
        k.psum = k.ctx.enter_context(nc.psum_tensor("banks", [128, 8 * BANK], F32))
        k.ident = k.sb("ident", [128, 128])
        k.ones = k.sb("ones", [128, 1])
        k.edges_found = k.sb("edges_found", [1, 1], I32)
        k.log_counts = k.sb("log_counts", [P, T, N])
        diag_ctx = k.ctx.enter_context(ExitStack())
        k.plain_diag = diag_ctx.enter_context(nc.sbuf_tensor("plain_diag", [P, T, P], F32))

        with ExitStack() as edge_ctx:
            share = k.chunks // T
            window = -(-(share + 8) // 6) * 6
            k.pad_left = (window - share) // 2
            k.node_row = edge_ctx.enter_context(nc.sbuf_tensor("node_row", [128, N], F16))
            k.end_cols = edge_ctx.enter_context(
                nc.sbuf_tensor("end_cols", [P, 2, k.chunks + window - share], F32))
            stage_edges(k, src, dst)
            stage_count(k, "count_windows", lambda t: t * share, window, verify=True)
            found = nc.values_load(k.edges_found[0:1, 0:1], min_val=0, max_val=k.E)
            with nc.If(found < k.E):
                nc.gpsimd.nop()
                nc.sync.nop()
                stage_count(k, "count_all", lambda t: k.pad_left, k.chunks, verify=False)
            stage_logs(k)
        hidden = H * a["L0_gnn_att_src1"].shape[1]
        classes = H * a["L0_gnn_att_src2"].shape[1]
        gat1_rows = k.dram("gat1_rows", [N, hidden])
        gat2_rows = k.dram("gat2_rows", [N, classes])
        a_src_rows = k.dram("a_src_rows", [H, N])
        for name, rows, width, w, att_src, att_dst, row_bias, out_rows in (
                ("gat1", x, hidden, a["L0_gnn_W1"], a["L0_gnn_att_src1"], a["L0_gnn_att_dst1"], None, gat1_rows),
                ("gat2", gat1_rows, classes, a["L0_gnn_W2"], a["L0_gnn_att_src2"], a["L0_gnn_att_dst2"], a["L0_gnn_b1"], gat2_rows)):
            with ExitStack() as gat_ctx:
                h_sb = gat_ctx.enter_context(nc.sbuf_tensor(f"h_{name}", [P, T, width], F32))
                a_dst = gat_ctx.enter_context(nc.sbuf_tensor(f"a_dst_{name}", [P, T, H], F32))
                stage_gat_project(k, name, rows, row_bias, w, att_src, att_dst, h_sb, a_dst, a_src_rows)
                stage_gat_attend(k, name, h_sb, a_dst, a_src_rows, out_rows)
        x_rows = k.dram("x_rows", [N, D])
        x_cols = k.dram("x_cols", [D, N])
        stage_gat_finish(k, gat2_rows, a["L0_gnn_b2"], x, x_rows, x_cols)
        stage_plain_counts(k)
        diag_ctx.close()
        w = {name: a[f"L1_gnn_{name}"] for name in ("Wq", "Wk", "Wv", "Wo", "W1", "W2", "bq", "bo", "b1", "b2",
                                                    "g1", "beta1", "g2", "beta2")}
        C, F, CH = D // 128, w["W1"].shape[1] // 128, D // H
        q_halves = k.dram("q_halves", [H, 2 * CH, 2, N])
        att_rows = k.dram("att_rows", [N, D])
        with nc.Fori(0, w["Wq"].shape[0]) as layer:
            with ExitStack() as ctx:
                k_halves = ctx.enter_context(nc.sbuf_tensor("k_halves", [2 * CH, H, N], F32R))
                v_halves = ctx.enter_context(nc.sbuf_tensor("v_halves", [P, T, H, 2 * CH], F32R))
                with ExitStack() as w_ctx:
                    wq, wk, wv = (halves(nc, w_ctx, name, C, D) for name in ("wq", "wk", "wv"))
                    stage_turn_weights(k, "qkv", [(w["Wq"][layer], *wq), (w["Wk"][layer], *wk), (w["Wv"][layer], *wv)])
                    stage_qkv(k, x_cols, wq, wk, wv, w["bq"][layer], q_halves, k_halves, v_halves)
                stage_attend(k, q_halves, k_halves, v_halves, att_rows)
            with ExitStack() as w_ctx:
                y = w_ctx.enter_context(nc.sbuf_tensor("y", [128, C, N], F32))
                wo, w1, w2 = (halves(nc, w_ctx, *v) for v in (("wo", C, D), ("w1", C, F * 128), ("w2", F, D)))
                stage_turn_weights(k, "rest", [(w["Wo"][layer], *wo), (w["W1"][layer], *w1), (w["W2"][layer], *w2)])
                stage_out(k, att_rows, x_cols, wo, w["bo"][layer], y)
                stage_batch_norm(k, "norm1", w["g1"][layer], w["beta1"][layer], y, None)
                stage_feed_forward(k, w1, w["b1"][layer], w2, w["b2"][layer], y)
                stage_batch_norm(k, "norm2", w["g2"][layer], w["beta2"][layer], y, x_cols)
        stage_final(k, x_cols, a["L1_gnn_ln_g"], a["L1_gnn_ln_b"], x_rows, a["out"])



INPUTS = ("x", "src", "dst") + tuple(f"L0_gnn_{name}" for name in (
    "W1", "att_src1", "att_dst1", "b1", "W2", "att_src2", "att_dst2", "b2")) + tuple(f"L1_gnn_{name}" for name in (
        "Wq", "bq", "Wk", "Wv", "Wo", "bo", "W1", "b1", "W2", "b2", "g1", "beta1", "g2", "beta2", "ln_g", "ln_b"))


def kernel(**inputs):
    import numpy as np
    import concourse.bacc as bacc
    from concourse.bass_utils import run_bass_kernel_spmd

    nc = bacc.Bacc("TRN2", target_bir_lowering=False, num_devices=1)
    arrays, args = {}, {}
    for name in INPUTS:
        array = np.ascontiguousarray(inputs[name])
        arrays[f"in_{name}_dram"] = array
        args[name] = nc.dram_tensor(f"in_{name}_dram", array.shape, mybir.dt.from_np(array.dtype), kind="ExternalInput").ap()
    args["out"] = nc.dram_tensor("out_0_dram", inputs["x"].shape, F32, kind="ExternalOutput").ap()
    build(nc, **args)
    result = run_bass_kernel_spmd(nc, [arrays], core_ids=[0])
    return result.results[0]["out_0_dram"]
```

```python
from contextlib import ExitStack, contextmanager

import concourse.bass as bass
from concourse import mybir

ALU = mybir.AluOpType
ACT = mybir.ActivationFunctionType
AX_X = mybir.AxisListType.X
F32 = mybir.dt.float32
F32R = mybir.dt.float32r
F16 = mybir.dt.float16
BF16 = mybir.dt.bfloat16
I32 = mybir.dt.int32

BANK = 512
NEG_SLOPE = 0.2
GAIN = 1 / NEG_SLOPE
EPS = 1e-5
TINY = 1e-16
NO_EDGE = -1e30
FLOOR = -1e29
LEAST_COUNT = 2.0 ** -64
EXP_LN = "natural_log_exp_and_others"


def pieces(width):
    return [(a, min(BANK, width - a)) for a in range(0, width, BANK)]


def divisor(n, limit=128):
    return max(p for p in range(1, limit + 1) if n % p == 0)


class Step:

    def __init__(self, item, slot, turn, total):
        self.item, self.slot, self.turn, self.total = item, slot, turn, total

    def back(self, d):
        return Step(self.item - d, (self.slot - d) % 2, self.turn + (self.slot - d) // 2, self.total)

    def live(self):
        return not isinstance(self.item, int) or 0 <= self.item < self.total

    def first(self):
        return isinstance(self.item, int) and self.item == 0


def run_steps(eng, total, lag, emit):
    head = 2 * ((lag + 1) // 2) + 2
    if (total - head) // 2 < 2:
        head = total + lag
    for s in range(head):
        emit(Step(s, s % 2, s // 2, total))
    pairs = max(0, (total - head) // 2)
    if pairs > 0:
        with eng.Fori(0, pairs) as i:
            for slot in range(2):
                emit(Step(i * 2 + (head + slot), slot, i + head // 2, total))
    for s in range(head + 2 * pairs, total + lag):
        emit(Step(s, s % 2, s // 2, total))


def wait_item(eng, sem, step, ago=0):
    count = step.item - ago + 1
    if not isinstance(count, int) or count > 0:
        eng.wait_ge(sem, count)


def wait_loaded(eng, sems, step):
    eng.wait_ge(sems[step.slot], (step.turn + 1) * 16)


def wait_stored(eng, sems, step, dmas=1):
    last = step.back(2)
    if last.live():
        eng.wait_ge(sems[step.slot], (last.turn + 1) * (16 * dmas))


class Unit:

    def __init__(self, head, tile, heads, tiles):
        self.head, self.tile, self.heads, self.tiles = head, tile, heads, tiles

    def shift(self, d):
        v = self.tile + d
        return Unit(self.head + v // self.tiles, v % self.tiles, self.heads, self.tiles)

    def live(self):
        return not isinstance(self.head, int) or 0 <= self.head < self.heads

    def number(self):
        return self.head * self.tiles + self.tile

    def starts(self, head):
        return isinstance(self.head, int) and self.head == head and self.tile == 0


def run_units(eng, heads, tiles, emit):
    for t in range(tiles):
        emit(Unit(0, t, heads, tiles))
    with eng.Fori(1, heads - 1) as h:
        for t in range(tiles):
            emit(Unit(h, t, heads, tiles))
    for h in (heads - 1, heads):
        for t in range(tiles):
            emit(Unit(h, t, heads, tiles))


def wait_unit(eng, sem, unit, ago=0):
    count = unit.number() - ago + 1
    if not isinstance(count, int) or count > 0:
        eng.wait_ge(sem, count)


class Kernel:

    def __init__(self, nc, x, src):
        self.nc = nc
        self.N, self.D = x.shape
        self.P = divisor(self.N)
        self.T = self.N // self.P
        self.H = 8
        self.E = src.shape[0]
        self.chunks = self.E // self.P
        self.chunk_rows = divisor(self.chunks)
        self.ctx = ExitStack()

    def sb(self, name, shape, dt=F32):
        return self.ctx.enter_context(self.nc.sbuf_tensor(name, shape, dt))

    def sem(self, name):
        self.stage_sems.append(self.nc.alloc_semaphore(name))
        return self.stage_sems[-1]

    @contextmanager
    def stage(self, name):
        self.stage_sems = []
        with ExitStack() as buffers:
            yield buffers
        self.nc.clear_and_free_semaphores(self.stage_sems)
        self.nc.all_engine_barrier()

    def dram(self, name, shape, dt=F32):
        return self.nc.dram_tensor(name, shape, dt, kind="Internal").ap()




def stage_edges(k, src, dst):
    nc, P, N = k.nc, k.P, k.N
    rows, parts = k.chunk_rows, k.chunks // k.chunk_rows
    with k.stage("stage_edges") as ctx:
        ends_int = ctx.enter_context(nc.sbuf_tensor("ends_int", [rows, 2, parts, P], I32))
        ends_f32 = ctx.enter_context(nc.sbuf_tensor("ends_f32", [rows, 2, parts, P], F32))
        ends_loaded = k.sem("ends_loaded")
        ends_cast = k.sem("ends_cast")
        ends_turned = k.sem("ends_turned")
        zeroed = k.sem("zeroed")
        padded = k.sem("padded")
        ident_made = k.sem("ident_made")
        block = ctx.enter_context(nc.Block("edges"))

        @block.sync
        def _(sp):
            for i, ends in enumerate((src, dst)):
                sp.dma_start(ends_int[:, i], ends.rearrange("(a p e) -> p a e", a=parts, p=rows)).then_inc(ends_loaded, 16)

        @block.gpsimd
        def _(pool):
            pool.memset(k.ident[:], 0.0).then_inc(zeroed, 1)
            pool.wait_ge(zeroed, 1)
            pool.affine_select(out=k.ident[:], in_=k.ident[:], compare_op=ALU.not_equal, fill=1.0,
                               base=0, pattern=[[-1, 128]], channel_multiplier=1).then_inc(ident_made, 1)
            pool.iota(k.node_row[:], [[1, N]], base=0, channel_multiplier=0,
                      allow_small_or_imprecise_dtypes=True)
            pool.memset(k.ones[:], 1.0)

        @block.vector
        def _(dve):
            dve.memset(k.end_cols[:], -1.0).then_inc(padded, 1)
            dve.wait_ge(ends_loaded, 32)
            dve.tensor_copy(ends_f32[:], ends_int[:]).then_inc(ends_cast, 1)
            dve.wait_ge(padded, 1)
            for i in range(2):
                dve.wait_ge(ends_turned, i + 1)
                dve.tensor_copy(k.end_cols[:, i, k.pad_left:k.pad_left + k.chunks],
                                k.psum[0:P, i * BANK:i * BANK + k.chunks])

        @block.tensor
        def _(pe):
            pe.wait_ge(ident_made, 1)
            pe.wait_ge(ends_cast, 1)
            for i in range(2):
                for a in range(parts):
                    turned = pe.transpose(k.psum[0:P, i * BANK + a * rows:i * BANK + (a + 1) * rows],
                                          ends_f32[:, i, a], k.ident[0:rows, 0:rows])
                turned.then_inc(ends_turned, 1)


def stage_count(k, name, first_chunk, chunks, R, verify):
    nc, P, T, N = k.nc, k.P, k.T, k.N
    groups = chunks // R
    with k.stage("stage_count") as ctx:
        src_hot = ctx.enter_context(nc.sbuf_tensor(f"src_hot_{name}", [P, R, N], BF16))
        dst_hot = ctx.enter_context(nc.sbuf_tensor(f"dst_hot_{name}", [P, R, P], BF16))
        row_total = ctx.enter_context(nc.sbuf_tensor(f"row_total_{name}", [P, T], F32))
        col_total = ctx.enter_context(nc.sbuf_tensor(f"col_total_{name}", [P, 1], F32))
        hot_ready = k.sem(f"hot_ready_{name}")
        hot_free = k.sem(f"hot_free_{name}")
        sums_free = k.sem(f"sums_free_{name}")
        total_step = k.sem(f"total_step_{name}")
        block = ctx.enter_context(nc.Block(name))
        assert chunks % R == 0

        def sums(slot, a, n):
            return k.psum[0:P, 3 * BANK * slot + a:3 * BANK * slot + a + n]

        @block.vector
        def _(dve):
            dve.sem_inc(hot_free, R)
            with dve.Fori(0, T) as t:
                with dve.Fori(0, groups) as g:
                    for r in range(R):
                        c = first_chunk(t) + g * R + r
                        dve.wait_ge(hot_free, (t * groups + g) * R + r + 1)
                        dve.tensor_scalar(src_hot[:, r], k.node_row[0:P, :], k.end_cols[:, 0, bass.ds(c, 1)], None, ALU.is_equal)
                        dve.tensor_scalar(dst_hot[:, r], k.node_row[0:P, bass.ds(t * P, P)],
                                          k.end_cols[:, 1, bass.ds(c, 1)], None, ALU.is_equal).then_inc(hot_ready, 1)
            if verify:
                dve.wait_ge(sums_free, T + 2)
                dve.tensor_reduce(col_total[:], row_total[:], AX_X, ALU.add).then_inc(total_step, 1)
                dve.wait_ge(total_step, 2)
                dve.tensor_copy(k.edges_found[:], k.psum[0:1, 6 * BANK:6 * BANK + 1])

        @block.tensor
        def _(pe):
            def group(t, slot, g, first, last):
                for r in range(R):
                    pe.wait_ge(hot_ready, (t * groups + g) * R + r + 1)
                    for a, n in pieces(N):
                        product = pe.matmul(sums(slot, a, n), dst_hot[:, r], src_hot[:, r, a:a + n],
                                            start=first and r == 0, stop=last and r == R - 1)
                    product.then_inc(hot_free, 1)

            def tile(t, slot):
                pe.wait_ge(sums_free, t + 1)
                group(t, slot, 0, True, False)
                with pe.Fori(1, groups - 1) as g:
                    group(t, slot, g, False, False)
                group(t, slot, groups - 1, False, True)

            with pe.Fori(0, T // 2) as i:
                tile(i * 2, 0)
                tile(i * 2 + 1, 1)
            if verify:
                pe.wait_ge(total_step, 1)
                pe.matmul(k.psum[0:1, 6 * BANK:6 * BANK + 1], col_total[:], k.ones[0:P, 0:1],
                          start=True, stop=True).then_inc(total_step, 1)

        @block.scalar
        def _(act):
            act.sem_inc(sums_free, 2)
            with act.Fori(0, T // 2) as i:
                for slot in range(2):
                    t = i * 2 + slot
                    act.wait_ge(hot_free, (t + 1) * groups * R + R)
                    act.activation(k.log_counts[:, t, :], sums(slot, 0, N), ACT.Copy,
                                   accum_out=row_total[:, bass.ds(t, 1)]).then_inc(sums_free, 1)


def stage_logs(k):
    nc, P, T, N = k.nc, k.P, k.T, k.N
    with k.stage("stage_logs") as ctx:
        logs = ctx.enter_context(nc.sbuf_tensor("logs", [P, 2, N], F32))
        fence = ctx.enter_context(nc.sbuf_tensor("fence", [P, 2, N], F32))
        loop_counts = ctx.enter_context(nc.sbuf_tensor("loop_counts", [P, 2, P], F32))
        loop_logs = ctx.enter_context(nc.sbuf_tensor("loop_logs", [P, 2, P], F32))
        loop_fence = ctx.enter_context(nc.sbuf_tensor("loop_fence", [P, 2, P], F32))
        least = ctx.enter_context(nc.sbuf_tensor("least", [P, 1], F32))
        least_set = k.sem("least_set")
        loops_added = k.sem("loops_added")
        fences_ready = k.sem("fences_ready")
        logs_ready = k.sem("logs_ready")
        tile_done = k.sem("tile_done")
        rows_done = k.sem("rows_done")
        block = ctx.enter_context(nc.Block("logs"))

        def diag(t):
            return k.log_counts[:, t, bass.ds(t * P, P)]

        @block.gpsimd
        def _(pool):
            pool.memset(least[:], LEAST_COUNT).then_inc(least_set, 1)
            pool.sem_inc(tile_done, 2)
            with pool.Fori(0, T // 2) as i:
                for slot in range(2):
                    t = i * 2 + slot
                    pool.wait_ge(tile_done, t + 1)
                    pool.tensor_tensor(loop_counts[:, slot], diag(t), k.ident[0:P, 0:P], ALU.add).then_inc(loops_added, 1)

        @block.scalar
        def _(act):
            act.preload_act_table_set(EXP_LN)
            act.wait_ge(least_set, 1)
            with act.Fori(0, T // 2) as i:
                for slot in range(2):
                    t = i * 2 + slot
                    act.wait_ge(tile_done, t + 1)
                    act.activation(logs[:, slot], k.log_counts[:, t, :], ACT.Ln, bias=least[:])
                    act.wait_ge(loops_added, t + 1)
                    act.activation(loop_logs[:, slot], loop_counts[:, slot], ACT.Ln, bias=least[:]).then_inc(logs_ready, 1)

        @block.vector
        def _(dve):
            with dve.Fori(0, T // 2) as i:
                for slot in range(2):
                    t = i * 2 + slot
                    dve.wait_ge(loops_added, t + 1)
                    dve.tensor_scalar(fence[:, slot], k.log_counts[:, t, :], -0.5, -2 * NO_EDGE, ALU.add, ALU.mult)
                    dve.tensor_scalar(loop_fence[:, slot], loop_counts[:, slot], -0.5, -2 * NO_EDGE, ALU.add, ALU.mult
                                      ).then_inc(fences_ready, 1)
                    dve.wait_ge(fences_ready, t + 1)
                    dve.wait_ge(logs_ready, t + 1)
                    block_at = bass.ds(t * P, P)
                    dve.tensor_tensor(k.plain_diag[:, t, :], logs[:, slot, block_at], fence[:, slot, block_at], ALU.min)
                    dve.scalar_tensor_tensor(k.log_counts[:, t, :], logs[:, slot], GAIN, fence[:, slot],
                                             ALU.mult, ALU.min).then_inc(rows_done, 1)
                    dve.wait_ge(rows_done, t + 1)
                    dve.scalar_tensor_tensor(diag(t), loop_logs[:, slot], GAIN, loop_fence[:, slot],
                                             ALU.mult, ALU.min).then_inc(tile_done, 1)


def stage_gat_project(k, name, rows, row_bias, w, att_src, att_dst, h_sb, a_dst, a_src_rows):
    nc, P, T, N, H = k.nc, k.P, k.T, k.N, k.H
    relu = row_bias is not None
    K = w.shape[0] // 128
    M = w.shape[1]
    CH = M // H
    KB = -(-K // 4)
    MB = M // BANK
    with k.stage("stage_gat_project") as ctx:
        def sb(what, shape, dt=F32):
            return ctx.enter_context(nc.sbuf_tensor(f"{what}_{name}", shape, dt))

        w_f32 = sb("w_f32", [128, K, M])
        w_high = sb("w_high", [128, K, M], F32R)
        w_low = sb("w_low", [128, K, M], F32R)
        att = sb("att", [P, 2, M])
        x_rows = sb("x_rows", [P, 2, K * 128])
        x_high = sb("x_high", [128, 2, K, P], F32R)
        x_low = sb("x_low", [128, 2, K, P], F32R)
        h_att = sb("h_att", [P, 2, 2, M])
        a_src = sb("a_src", [P, 2, H])
        a_src_t = sb("a_src_t", [H, N])
        if relu:
            bias_rows = sb("bias_rows", [P, K * 128])
            bias_loaded = k.sem(f"bias_loaded_{name}")
            x_biased = k.sem(f"x_biased_{name}")
        w_loaded = k.sem(f"w_loaded_{name}")
        att_loaded = k.sem(f"att_loaded_{name}")
        x_loaded = [k.sem(f"x_loaded{i}_{name}") for i in range(2)]
        w_high_done = k.sem(f"w_high_done_{name}")
        w_low_done = k.sem(f"w_low_done_{name}")
        x_turned = k.sem(f"x_turned_{name}")
        x_high_done = k.sem(f"x_high_done_{name}")
        x_low_done = k.sem(f"x_low_done_{name}")
        h_summed = k.sem(f"h_summed_{name}")
        h_saved = k.sem(f"h_saved_{name}")
        att_multiplied = k.sem(f"att_multiplied_{name}")
        a_reduced = k.sem(f"a_reduced_{name}")
        a_turned = k.sem(f"a_turned_{name}")
        a_saved = k.sem(f"a_saved_{name}")
        a_stored = k.sem(f"a_stored_{name}")
        block = ctx.enter_context(nc.Block(f"project_{name}"))

        def turned(slot):
            at = slot * KB * BANK
            return k.psum[:, at:at + KB * BANK].rearrange("p (b c) -> p b c", b=KB)[:, :, 0:4 * P]

        def halves(x, slot):
            return x[:, slot].rearrange("p (b c) n -> p b (c n)", b=KB)

        def h_bank(slot, m):
            at = (2 * KB + slot * MB + m) * BANK
            return k.psum[0:P, at:at + BANK]

        a_bank = k.psum[0:H, 7 * BANK:7 * BANK + P]

        @block.sync
        def _(sp):
            if relu:
                sp.dma_start(bias_rows[:], row_bias.rearrange("(o c) -> o c", o=1).to_broadcast([P, K * 128])
                             ).then_inc(bias_loaded, 16)
            sp.dma_start(w_f32[:], w.rearrange("(c p) m -> p c m", p=128)).then_inc(w_loaded, 16)

            def step(s):
                if not s.live():
                    return
                wait_item(sp, x_turned, s, ago=2)
                sp.dma_start(x_rows[:, s.slot], rows[bass.ds(s.item * P, P), :]).then_inc(x_loaded[s.slot], 16)
                if s.first():
                    for i, v in enumerate((att_src, att_dst)):
                        sp.dma_start(att[:, i], v.rearrange("(o h) c -> o (h c)", o=1).to_broadcast([P, M])
                                     ).then_inc(att_loaded, 16)

            run_steps(sp, T, 0, step)
            sp.wait_ge(a_saved, T)
            sp.dma_start(a_src_rows, a_src_t[:]).then_inc(a_stored, 16)
            sp.wait_ge(a_stored, 16)

        @block.tensor
        def _(pe):
            def step(s):
                if s.live():
                    if relu:
                        wait_item(pe, x_biased, s)
                    else:
                        wait_loaded(pe, x_loaded, s)
                    wait_item(pe, x_low_done, s, ago=2)
                    for c in range(K):
                        block_t = pe.transpose(turned(s.slot)[:, c // 4, (c % 4) * P:(c % 4 + 1) * P],
                                               x_rows[:, s.slot, c * 128:(c + 1) * 128], k.ident[0:P, 0:P])
                    block_t.then_inc(x_turned, 1)
                s = s.back(1)
                if s.live():
                    if s.first():
                        pe.wait_ge(w_low_done, 1)
                    wait_item(pe, x_low_done, s)
                    wait_item(pe, h_saved, s, ago=2)
                    for m in range(MB):
                        cols = slice(m * BANK, (m + 1) * BANK)
                        for c in range(K):
                            for i, (x, v) in enumerate(((x_high, w_high), (x_high, w_low), (x_low, w_high))):
                                product = pe.matmul(h_bank(s.slot, m), x[:, s.slot, c], v[:, c, cols],
                                                    start=c == 0 and i == 0, stop=c == K - 1 and i == 2)
                    product.then_inc(h_summed, 1)
                s = s.back(2)
                if s.live():
                    wait_item(pe, a_reduced, s)
                    wait_item(pe, a_saved, s, ago=1)
                    pe.transpose(a_bank, a_src[:, s.slot], k.ident[0:P, 0:P]).then_inc(a_turned, 1)

            run_steps(pe, T, 3, step)

        @block.scalar
        def _(act):
            act.wait_ge(w_loaded, 16)
            act.copy(w_high[:], w_f32[:]).then_inc(w_high_done, 1)

            def step(s):
                if s.live():
                    wait_item(act, x_turned, s)
                    wait_item(act, h_summed, s, ago=2)
                    act.activation(halves(x_high, s.slot), turned(s.slot), ACT.Relu if relu else ACT.Copy).then_inc(x_high_done, 1)
                s = s.back(1)
                if s.live():
                    wait_item(act, h_summed, s)
                    for m in range(MB):
                        saved = act.copy(h_sb[:, s.item, m * BANK:(m + 1) * BANK], h_bank(s.slot, m))
                    saved.then_inc(h_saved, 1)

            run_steps(act, T, 1, step)

        @block.gpsimd
        def _(pool):
            pool.wait_ge(att_loaded, 32)
            if relu:
                pool.wait_ge(bias_loaded, 16)

            def step(s):
                if s.live() and relu:
                    wait_loaded(pool, x_loaded, s)
                    pool.tensor_tensor(x_rows[:, s.slot], x_rows[:, s.slot], bias_rows[:], ALU.add).then_inc(x_biased, 1)
                s = s.back(2)
                if s.live():
                    wait_item(pool, h_saved, s)
                    wait_item(pool, a_reduced, s, ago=2)
                    for i in range(2):
                        made = pool.tensor_tensor(h_att[:, s.slot, i], h_sb[:, s.item, :], att[:, i], ALU.mult)
                    made.then_inc(att_multiplied, 1)

            run_steps(pool, T, 2, step)

        @block.vector
        def _(dve):
            dve.wait_ge(w_high_done, 1)
            dve.tensor_tensor(w_low[:], w_f32[:], w_high[:].bitcast(F32), ALU.subtract).then_inc(w_low_done, 1)

            def step(s):
                if s.live():
                    wait_item(dve, x_high_done, s)
                    if relu:
                        cut = dve.scalar_tensor_tensor(halves(x_low, s.slot), turned(s.slot), 0.0,
                                                       halves(x_high, s.slot).bitcast(F32), ALU.max, ALU.subtract)
                    else:
                        cut = dve.tensor_tensor(halves(x_low, s.slot), turned(s.slot), halves(x_high, s.slot).bitcast(F32),
                                                ALU.subtract)
                    cut.then_inc(x_low_done, 1)
                s = s.back(2)
                if s.live():
                    wait_item(dve, att_multiplied, s)
                    wait_item(dve, a_turned, s, ago=2)
                    for i, a in enumerate((a_src[:, s.slot], a_dst[:, s.item, :])):
                        total = dve.tensor_reduce(a, h_att[:, s.slot, i].rearrange("p (h c) -> p h c", h=H), AX_X, ALU.add)
                    total.then_inc(a_reduced, 1)
                s = s.back(1)
                if s.live():
                    wait_item(dve, a_turned, s)
                    dve.tensor_copy(a_src_t[:, bass.ds(s.item * P, P)], a_bank).then_inc(a_saved, 1)

            run_steps(dve, T, 3, step)


def stage_gat_attend(k, name, h_sb, a_dst, a_src_rows, out_rows):
    nc, P, T, N, H = k.nc, k.P, k.T, k.N, k.H
    CH = h_sb.shape[2] // H
    B = T // 2
    HALF = BANK // 2
    with k.stage("stage_gat_attend") as ctx:
        def sb(what, shape, dt=F32):
            return ctx.enter_context(nc.sbuf_tensor(f"{what}_{name}", shape, dt))

        a_src = sb("a_src_all", [P, H, N])
        probs = sb("probs", [P, B, N])
        base = sb("base", [P, 2, N])
        minus_a_dst = sb("minus_a_dst", [P, T, H])
        probs_t = sb("probs_t", [P, B, T, P])
        neg_max, sums, sums_safe, inverse = (sb(what, [P, T]) for what in ("neg_max", "sums", "sums_safe", "inverse"))
        final = sb("final", [P, 2, T // 2, CH])
        a_loaded = k.sem(f"a_loaded_{name}")
        a_rest_loaded = k.sem(f"a_rest_loaded_{name}")
        ramp_done = k.sem(f"ramp_done_{name}")
        negated = k.sem(f"negated_{name}")
        base_free = k.sem(f"base_free_{name}")
        base_done = k.sem(f"base_done_{name}")
        masked = k.sem(f"masked_{name}")
        exp_done = k.sem(f"exp_done_{name}")
        sum_safe = k.sem(f"sum_safe_{name}")
        inverted = k.sem(f"inverted_{name}")
        probs_turned = k.sem(f"probs_turned_{name}")
        probs_saved = k.sem(f"probs_saved_{name}")
        summed = k.sem(f"summed_{name}")
        final_done = k.sem(f"final_done_{name}")
        stored = [k.sem(f"stored{i}_{name}") for i in range(2)]
        block = ctx.enter_context(nc.Block(f"attend_{name}"))

        def turned(u):
            at = (u % 2) * 3 * BANK
            return k.psum[0:P, at:at + T // 2 * HALF].rearrange("p (b c) -> p b c", c=HALF)[:, :, 0:2 * P]

        def out_bank(u):
            at = (6 + u % 2) * BANK
            return k.psum[0:P, at:at + CH]

        @block.sync
        def _(sp):
            for h in range(H):
                sp.dma_start(a_src[:, h], a_src_rows[h:h + 1, :].to_broadcast([P, N])
                             ).then_inc(a_rest_loaded if h else a_loaded, 16)

            def step(n):
                if n.live() and n.tile % B == B - 1:
                    half = n.tile // B
                    wait_unit(sp, final_done, n)
                    sp.dma_start(out_rows.rearrange("(t p) m -> p t m", p=P)[:, half * B:(half + 1) * B, bass.ds(n.head * CH, CH)],
                                 final[:, half]).then_inc(stored[half], 16)

            run_units(sp, H, T, step)
            for half in range(2):
                sp.wait_ge(stored[half], 16 * H)

        @block.scalar
        def _(act):
            act.preload_act_table_set(EXP_LN)

            def step(n):
                if n.live():
                    wait_unit(act, masked, n)
                    act.activation(probs[:, n.tile % B], probs[:, n.tile % B], ACT.Exp, scale=-1.0,
                                   bias=neg_max[:, n.tile:n.tile + 1],
                                   accum_out=sums[:, n.tile:n.tile + 1]).then_inc(exp_done, 1)
                n = n.shift(-1)
                if n.live():
                    wait_unit(act, probs_turned, n)
                    wait_unit(act, summed, n, ago=B)
                    act.copy(probs_t[:, n.tile % B].rearrange("p (b c) n -> p b (c n)", c=2), turned(n.tile)
                             ).then_inc(probs_saved, 1)
                n = n.shift(-2)
                if n.live():
                    wait_unit(act, summed, n)
                    wait_unit(act, inverted, n)
                    half, t = n.tile // B, n.tile % B
                    if t == 0 and not (isinstance(n.head, int) and n.head == 0):
                        act.wait_ge(stored[half], n.head * 16)
                    act.activation(final[:, half, t], out_bank(n.tile), ACT.Copy,
                                   scale=inverse[:, n.tile:n.tile + 1]).then_inc(final_done, 1)

            run_units(act, H, T, step)

        @block.vector
        def _(dve):
            dve.tensor_scalar(minus_a_dst[:], a_dst[:], -1.0, None, ALU.mult).then_inc(negated, 1)
            dve.wait_ge(negated, 1)

            def ramp(n):
                if n.live():
                    if n.starts(0):
                        dve.wait_ge(a_loaded, 16)
                    if n.starts(1):
                        dve.wait_ge(a_rest_loaded, 16 * (H - 1))
                    wait_unit(dve, probs_turned, n, ago=B)
                    dve.tensor_scalar(probs[:, n.tile % B], a_src[:, n.head, :], minus_a_dst[:, n.tile, bass.ds(n.head, 1)],
                                      GAIN - 1, ALU.max, ALU.mult).then_inc(ramp_done, 1)

            def wait_mask(n):
                if n.live():
                    wait_unit(dve, base_done, n)
                    wait_unit(dve, ramp_done, n)

            def mask(n):
                if n.live():
                    dve.tensor_tensor_reduce(probs[:, n.tile % B], probs[:, n.tile % B], base[:, n.tile % 2],
                                             -NEG_SLOPE, -FLOOR, ALU.add, ALU.min,
                                             neg_max[:, n.tile:n.tile + 1]).then_inc(masked, 1)

            def step(n):
                ramp(n.shift(2))
                wait_mask(n.shift(1))
                last = n.shift(-1)
                if last.live():
                    wait_unit(dve, exp_done, last)
                    dve.tensor_scalar(sums_safe[:, last.tile:last.tile + 1], sums[:, last.tile:last.tile + 1],
                                      TINY, None, ALU.add).then_inc(sum_safe, 1)
                mask(n.shift(1))
                n = last
                if n.live():
                    wait_unit(dve, sum_safe, n)
                    dve.reciprocal(inverse[:, n.tile:n.tile + 1], sums_safe[:, n.tile:n.tile + 1]
                                   ).then_inc(inverted, 1)

            for u in range(2):
                ramp(Unit(0, u, H, T))
            wait_mask(Unit(0, 0, H, T))
            mask(Unit(0, 0, H, T))
            run_units(dve, H, T, step)

        @block.tensor
        def _(pe):
            def step(n):
                if n.live():
                    wait_unit(pe, exp_done, n)
                    wait_unit(pe, probs_saved, n, ago=2)
                    for i in range(T):
                        block_t = pe.transpose(turned(n.tile)[:, i // 2, (i % 2) * P:(i % 2 + 1) * P],
                                               probs[:, n.tile % B, i * P:(i + 1) * P], k.ident[0:P, 0:P])
                    block_t.then_inc(probs_turned, 1)
                n = n.shift(-2)
                if n.live():
                    wait_unit(pe, probs_saved, n)
                    wait_unit(pe, final_done, n, ago=2)
                    for i in range(T):
                        total = pe.matmul(out_bank(n.tile), probs_t[:, n.tile % B, i],
                                          h_sb[:, i, bass.ds(n.head * CH, CH)], start=i == 0, stop=i == T - 1)
                    total.then_inc(summed, 1)

            run_units(pe, H, T, step)

        @block.gpsimd
        def _(pool):
            def step(n):
                if n.live():
                    if isinstance(n.head, int) and n.head == 0:
                        pool.wait_ge(a_loaded, 16)
                    else:
                        pool.wait_ge(a_rest_loaded, 16 * (H - 1))
                    wait_unit(pool, masked, n, ago=2)
                    pool.sem_inc(base_free, 1)
                    pool.tensor_tensor(base[:, n.tile % 2], k.log_counts[:, n.tile, :], a_src[:, n.head, :], ALU.add
                                       ).then_inc(base_done, 1)

            run_units(pool, H, T, step)


def stage_gat_finish(k, gat_rows, bias, x, x_rows, x_cols):
    nc, P, T, N, D = k.nc, k.P, k.T, k.N, k.D
    C = D // 128
    with k.stage("stage_gat_finish") as ctx:
        def sb(what, shape, dt=F32):
            return ctx.enter_context(nc.sbuf_tensor(f"{what}_gf", shape, dt))

        g = sb("g", [P, T, D])
        y = sb("y", [P, T, D])
        e = sb("e", [P, 2, D])
        normal = sb("normal", [P, 2, D])
        cols = sb("cols", [128, 2, C, P])
        neg_max, sums, shift = sb("neg_max", [P, T]), sb("sums", [P, T]), sb("shift", [P, T])
        logs = sb("logs", [P, T])
        stats = sb("stats", [P, T, 6])
        moments = sb("moments", [P, T, 2])
        spread, deviation, inverse = sb("spread", [P, T]), sb("deviation", [P, T]), sb("inverse", [P, T])
        bias_rows = sb("bias_rows", [P, D])
        bias_loaded, g_biased = k.sem("bias_loaded_gf"), k.sem("g_biased_gf")
        g_loaded, x_loaded = k.sem("g_loaded"), k.sem("x_loaded_gf")
        max_done, exp_done, logs_done = k.sem("max_done_gf"), k.sem("exp_done_gf"), k.sem("logs_done_gf")
        shift_done, added, stats_done = k.sem("shift_done_gf"), k.sem("added_gf"), k.sem("stats_done_gf")
        moments_done, spread_done = k.sem("moments_done_gf"), k.sem("spread_done_gf")
        deviation_done, inverse_done = k.sem("deviation_done_gf"), k.sem("inverse_done_gf")
        normed, turned, cols_saved = k.sem("normed_gf"), k.sem("turned_gf"), k.sem("cols_saved_gf")
        rows_stored = [k.sem(f"rows_stored{i}_gf") for i in range(2)]
        cols_stored = [k.sem(f"cols_stored{i}_gf") for i in range(2)]
        block = ctx.enter_context(nc.Block("gat_finish"))

        def bank(slot):
            return k.psum[:, slot * BANK:slot * BANK + C * P]

        @block.sync
        def _(sp):
            sp.dma_start(bias_rows[:], bias.rearrange("(o c) -> o c", o=1).to_broadcast([P, D])).then_inc(bias_loaded, 16)
            sp.dma_start(g[:], gat_rows.rearrange("(t p) d -> p t d", p=P)).then_inc(g_loaded, 16)
            sp.dma_start(y[:], x.rearrange("(t p) d -> p t d", p=P)).then_inc(x_loaded, 16)

            def step(s):
                wait_item(sp, normed, s)
                sp.dma_start(x_rows[bass.ds(s.item * P, P), :], normal[:, s.slot]).then_inc(rows_stored[s.slot], 16)

            run_steps(sp, T, 0, step)
            for i in range(2):
                sp.wait_ge(rows_stored[i], 16 * T // 2)
                sp.wait_ge(cols_stored[i], 16 * T // 2)

        @block.gpsimd
        def _(pool):
            pool.wait_ge(bias_loaded, 16)
            pool.wait_ge(g_loaded, 16)
            with pool.Fori(0, T) as t:
                pool.tensor_tensor(g[:, t, :], g[:, t, :], bias_rows[:], ALU.add).then_inc(g_biased, 1)

        @block.vector
        def _(dve):
            with dve.Fori(0, T) as t:
                dve.wait_ge(g_biased, t + 1)
                dve.tensor_reduce(neg_max[:, bass.ds(t, 1)], g[:, t, :], AX_X, ALU.max, negate=True).then_inc(max_done, 1)
            dve.wait_ge(logs_done, 1)
            dve.wait_ge(max_done, T)
            dve.tensor_tensor(shift[:], neg_max[:], logs[:], ALU.subtract).then_inc(shift_done, 1)
            dve.wait_ge(shift_done, 1)
            dve.wait_ge(x_loaded, 16)
            with dve.Fori(0, T) as t:
                dve.scalar_tensor_tensor(y[:, t, :], g[:, t, :], shift[:, bass.ds(t, 1)], y[:, t, :],
                                         ALU.add, ALU.add).then_inc(added, 1)
                dve.wait_ge(added, t + 1)
                dve.bn_stats(stats[:, t, :], y[:, t, :]).then_inc(stats_done, 1)
            dve.wait_ge(stats_done, T)
            for t in range(T):
                dve.bn_aggr(moments[:, t], stats[:, t]).then_inc(moments_done, 1)
            dve.wait_ge(moments_done, T)
            dve.tensor_scalar(spread[:], moments[:, :, 1], EPS, None, ALU.add).then_inc(spread_done, 1)
            dve.wait_ge(deviation_done, 1)
            dve.reciprocal(inverse[:], deviation[:]).then_inc(inverse_done, 1)
            dve.wait_ge(inverse_done, 1)

            def norm(s):
                wait_stored(dve, rows_stored, s)
                wait_item(dve, turned, s, ago=2)
                dve.tensor_scalar(normal[:, s.slot], y[:, s.item, :], moments[:, s.item, 0:1],
                                  inverse[:, bass.ds(s.item, 1)], ALU.subtract, ALU.mult).then_inc(normed, 1)

            run_steps(dve, T, 0, norm)

        @block.scalar
        def _(act):
            act.preload_act_table_set(EXP_LN)

            def softmax(s):
                wait_item(act, max_done, s)
                wait_item(act, exp_done, s, ago=2)
                act.activation(e[:, s.slot], g[:, s.item, :], ACT.Exp, bias=neg_max[:, bass.ds(s.item, 1)],
                               accum_out=sums[:, bass.ds(s.item, 1)]).then_inc(exp_done, 1)

            run_steps(act, T, 0, softmax)
            act.wait_ge(exp_done, T)
            act.activation(logs[:], sums[:], ACT.Ln).then_inc(logs_done, 1)
            act.wait_ge(spread_done, 1)
            act.activation(deviation[:], spread[:], ACT.Sqrt).then_inc(deviation_done, 1)

            def save(s):
                wait_item(act, turned, s)
                wait_stored(act, cols_stored, s)
                act.copy(cols[:, s.slot].rearrange("p c n -> p (c n)"), bank(s.slot)).then_inc(cols_saved, 1)
                wait_item(act, cols_saved, s)
                act.dma_start(x_cols.rearrange("(c p) n -> p c n", p=128)[:, :, bass.ds(s.item * P, P)],
                             cols[:, s.slot]).then_inc(cols_stored[s.slot], 16)

            run_steps(act, T, 0, save)

        @block.tensor
        def _(pe):
            def step(s):
                wait_item(pe, normed, s)
                wait_item(pe, cols_saved, s, ago=2)
                for c in range(C):
                    block_t = pe.transpose(bank(s.slot)[:, c * P:(c + 1) * P], normal[:, s.slot, c * 128:(c + 1) * 128],
                                           k.ident[0:P, 0:P])
                block_t.then_inc(turned, 1)

            run_steps(pe, T, 0, step)


def stage_plain_counts(k):
    nc, P, T = k.nc, k.P, k.T
    with k.stage("stage_plain_counts") as ctx:
        scaled = k.sem("mask_scaled")
        block = ctx.enter_context(nc.Block("plain_counts"))

        @block.vector
        def _(dve):
            with dve.Fori(0, T) as t:
                dve.tensor_scalar(k.log_counts[:, t, :], k.log_counts[:, t, :], NEG_SLOPE, None, ALU.mult).then_inc(scaled, 1)
                dve.wait_ge(scaled, t + 1)
                dve.tensor_copy(k.log_counts[:, t, bass.ds(t * P, P)], k.plain_diag[:, t, :])


def stage_turn_weights(k, name, jobs):
    nc = k.nc
    parts = [(w, high, low, o) for w, high, low in jobs for o in range(w.shape[0] // 128)]
    widest = max(w.shape[1] for w, _, _ in jobs)
    total = len(parts)
    assert total % 2 == 0
    with k.stage("stage_turn_weights") as ctx:
        rows = ctx.enter_context(nc.sbuf_tensor(f"w_rows_{name}", [128, total, widest], F32))
        loaded = [k.sem(f"w_rows_loaded{i}_{name}") for i in range(2)]
        turned, high_done, low_done = (k.sem(f"w_{what}_{name}") for what in ("turned", "high_done", "low_done"))
        block = ctx.enter_context(nc.Block(f"weights_{name}"))

        def bank(j, width):
            return k.psum[:, (j % 4) * BANK:(j % 4) * BANK + width]

        def part_of(j, half):
            w, high, low, o = parts[j]
            return (low if half else high)[:, :, o * 128:(o + 1) * 128]

        def blocks(j, width):
            return bank(j, width).rearrange("p (c o) -> p c o", o=128)

        @block.sync
        def _(sp):
            for j, (w, _, _, o) in enumerate(parts):
                sp.dma_start(rows[:, j, 0:w.shape[1]], w[o * 128:(o + 1) * 128, :]).then_inc(loaded[j * 2 // total], 16)

        @block.tensor
        def _(pe):
            for j, (w, _, _, o) in enumerate(parts):
                if j * 2 % total == 0:
                    pe.wait_ge(loaded[j * 2 // total], 8 * total)
                if j >= 4:
                    pe.wait_ge(low_done, j - 3)
                for c in range(w.shape[1] // 128):
                    block_t = pe.transpose(bank(j, w.shape[1])[:, c * 128:(c + 1) * 128],
                                           rows[:, j, c * 128:(c + 1) * 128], k.ident[:])
                block_t.then_inc(turned, 1)

        @block.scalar
        def _(act):
            for j, (w, _, _, o) in enumerate(parts):
                act.wait_ge(turned, j + 1)
                act.copy(part_of(j, 0), blocks(j, w.shape[1])).then_inc(high_done, 1)

        @block.vector
        def _(dve):
            for j, (w, _, _, o) in enumerate(parts):
                dve.wait_ge(high_done, j + 1)
                dve.tensor_tensor(part_of(j, 1), blocks(j, w.shape[1]), part_of(j, 0).bitcast(F32), ALU.subtract
                                  ).then_inc(low_done, 1)


def halves(nc, ctx, name, ins, outs):
    return [ctx.enter_context(nc.sbuf_tensor(f"{name}_{half}", [128, ins, outs], F32R)) for half in ("high", "low")]


def three_passes(pe, out, x_high, x_low, w_high, w_low, first, last):
    pe.matmul(out, w_high, x_high, start=first, stop=False)
    pe.matmul(out, w_high, x_low, start=False, stop=False)
    return pe.matmul(out, w_low, x_high, start=False, stop=last)


def stage_qkv(k, x_cols, wq, wk, wv, bq, q_halves, k_halves, v_rows):
    nc, P, T, N, D, H = k.nc, k.P, k.T, k.N, k.D, k.H
    C, CH = D // 128, D // H
    W, CHUNKS = 2 * P, T // 2
    SCALE = float(CH) ** -0.5
    with k.stage("stage_qkv") as ctx:
        def sb(what, shape, dt=F32):
            return ctx.enter_context(nc.sbuf_tensor(f"{what}_qkv", shape, dt))

        x = sb("x", [128, 2, C, W])
        x_high, x_low = sb("x_high", [128, 2, C, W], F32R), sb("x_low", [128, 2, C, W], F32R)
        q = sb("q", [128, C, W])
        q_out = sb("q_out", [128, 2, C, W], F32R)
        k_low = sb("k_low", [128, 2, C, W], F32R)
        bias, scaled_bias = sb("bias", [128, C]), sb("scaled_bias", [128, C])
        bias_loaded, bias_scaled, high_done, low_done, q_summed, k_summed, v_summed, q_saved, q_high_done, \
            q_low_done, q_stored, k_high_done, k_low_done, v_saved = (
                k.sem(f"{what}_qkv") for what in ("bias_loaded", "bias_scaled", "high_done", "low_done", "q_summed",
                                                  "k_summed", "v_summed", "q_saved", "q_high_done", "q_low_done",
                                                  "q_stored", "k_high_done", "k_low_done", "v_saved"))
        x_loaded, k_stored = ([k.sem(f"{what}{slot}_qkv") for slot in range(2)] for what in ("x_loaded", "k_stored"))
        block = ctx.enter_context(nc.Block("qkv"))

        def by_feature(i):
            return k.psum[:, i * 2 * BANK:(i + 1) * 2 * BANK].rearrange("p (b c) -> p b c", b=C // 2)[:, :, 0:2 * W].rearrange(
                "p b (c n) -> p b c n", c=2)

        def product(i, o):
            at = (i * 2 + o // 2) * BANK + o % 2 * W
            return k.psum[:, at:at + W]

        def v_bank(t):
            return k.psum[0:P, (4 + t) * BANK:(5 + t) * BANK]

        def like_banks(v):
            return v.rearrange("p (b c) n -> p b c n", c=2)

        def own(odd):
            return slice(odd * CH, (odd + 1) * CH)

        def k_at(rows, odd, s):
            return k_halves[own(rows)].rearrange("p (c odd) n -> p odd c n", odd=2)[:, odd][:, :, bass.ds(s.item * W, W)]

        @block.sync
        def _(sp):
            sp.dma_start(bias[:], bq.rearrange("(c p) -> p c", p=128), allow_slow_non_contiguous=True).then_inc(bias_loaded, 16)

            def step(s):
                nodes = bass.ds(s.item * W, W)
                if s.live():
                    wait_item(sp, low_done, s, ago=2)
                    sp.dma_start(x[:, s.slot], x_cols.rearrange("(c p) n -> p c n", p=128)[:, :, nodes]
                                 ).then_inc(x_loaded[s.slot], 16)
                s = s.back(1)
                if s.live():
                    nodes = bass.ds(s.item * W, W)
                    wait_item(sp, q_low_done, s)
                    for half, part in enumerate((q_out[:, 0], q_out[:, 1])):
                        sp.dma_start(q_halves.rearrange("(c p) half n -> half p c n", p=128)[half][:, :, nodes],
                                     part.bitcast(F32)).then_inc(q_stored, 16)
                    wait_item(sp, k_low_done, s)
                    for odd in range(2):
                        sp.dma_start(k_at(1 - odd, odd, s).bitcast(F32), k_low[own(odd), s.slot].bitcast(F32)
                                     ).then_inc(k_stored[s.slot], 16)

            run_steps(sp, CHUNKS, 1, step)
            sp.wait_ge(q_stored, 32 * CHUNKS)
            sp.wait_ge(k_stored[0], 32 * ((CHUNKS + 1) // 2))
            sp.wait_ge(k_stored[1], 32 * (CHUNKS // 2))

        @block.tensor
        def _(pe):
            def step(s):
                wait_item(pe, low_done, s)
                for i, (w, summed, saved) in enumerate(((wq, q_summed, q_saved), (wk, k_summed, k_low_done))):
                    wait_item(pe, saved, s, ago=1)
                    for o in range(C):
                        for c in range(C):
                            total = three_passes(pe, product(i, o), x_high[:, s.slot, c], x_low[:, s.slot, c],
                                                 w[0][:, c, o * 128:(o + 1) * 128], w[1][:, c, o * 128:(o + 1) * 128],
                                                 c == 0, c == C - 1)
                    total.then_inc(summed, 1)
                wait_item(pe, v_saved, s, ago=1)
                for t in range(2):
                    for c in range(C):
                        xh, xl = (v[:, s.slot, c, t * P:(t + 1) * P] for v in (x_high, x_low))
                        for i, (v, w) in enumerate(((xh, wv[0]), (xh, wv[1]), (xl, wv[0]))):
                            total = pe.matmul(v_bank(t), v, w[:, c, :], start=c == 0 and i == 0, stop=c == C - 1 and i == 2)
                total.then_inc(v_summed, 1)

            run_steps(pe, CHUNKS, 0, step)

        @block.scalar
        def _(act):
            act.wait_ge(bias_scaled, 1)

            def step(s):
                if s.live():
                    wait_loaded(act, x_loaded, s)
                    wait_item(act, v_summed, s, ago=2)
                    act.copy(x_high[:, s.slot], x[:, s.slot]).then_inc(high_done, 1)
                s = s.back(1)
                if s.live():
                    wait_item(act, q_summed, s)
                    wait_item(act, q_low_done, s, ago=1)
                    for o in range(C):
                        saved = act.activation(q[:, o], product(0, o), ACT.Identity,
                                               bias=scaled_bias[:, o:o + 1], scale=SCALE)
                    saved.then_inc(q_saved, 1)
                    wait_item(act, q_saved, s)
                    if not s.first():
                        act.wait_ge(q_stored, s.item * 32)
                    act.copy(q_out[:, 0], q[:]).then_inc(q_high_done, 1)
                    wait_item(act, k_summed, s)
                    for odd in range(2):
                        saved = act.copy(like_banks(k_at(odd, odd, s)), by_feature(1)[own(odd)])
                    saved.then_inc(k_high_done, 1)
                    wait_item(act, v_summed, s)
                    for t in range(2):
                        saved = act.copy(v_rows[:, s.item * 2 + t, :], v_bank(t))
                    saved.then_inc(v_saved, 1)

            run_steps(act, CHUNKS, 1, step)

        @block.vector
        def _(dve):
            dve.wait_ge(bias_loaded, 16)
            dve.tensor_scalar(scaled_bias[:], bias[:], SCALE, None, ALU.mult).then_inc(bias_scaled, 1)

            def step(s):
                if s.live():
                    wait_item(dve, high_done, s)
                    dve.tensor_tensor(x_low[:, s.slot], x[:, s.slot], x_high[:, s.slot].bitcast(F32), ALU.subtract
                                      ).then_inc(low_done, 1)
                s = s.back(1)
                if s.live():
                    wait_item(dve, q_high_done, s)
                    dve.tensor_tensor(q_out[:, 1], q[:], q_out[:, 0].bitcast(F32), ALU.subtract).then_inc(q_low_done, 1)
                    wait_item(dve, k_high_done, s)
                    wait_stored(dve, k_stored, s, 2)
                    for odd in range(2):
                        cut = dve.tensor_tensor(like_banks(k_low[own(odd), s.slot]), by_feature(1)[own(odd)],
                                                like_banks(k_at(odd, odd, s).bitcast(F32)), ALU.subtract)
                    cut.then_inc(k_low_done, 1)

            run_steps(dve, CHUNKS, 1, step)


def stage_attend(k, q_halves, k_halves, v_rows, out_rows):
    nc, P, T, N, D, H = k.nc, k.P, k.T, k.N, k.D, k.H
    CH = D // H
    B = T // 2
    HALF = BANK // 2
    with k.stage("stage_attend") as ctx:
        def sb(what, shape, dt=F32):
            return ctx.enter_context(nc.sbuf_tensor(f"{what}_att", shape, dt))

        q = sb("q", [128, 2, N], F32R)
        probs = sb("probs", [P, B, N])
        probs_t = sb("probs_t", [P, B, T, P])
        neg_max, sums, sums_safe, inverse = (sb(what, [P, T]) for what in ("neg_max", "sums", "sums_safe", "inverse"))
        final = sb("final", [P, 2, B, CH])
        q_loaded = [k.sem(f"q_loaded{i}_att") for i in range(2)]
        stored = [k.sem(f"stored{i}_att") for i in range(2)]
        scored, masked, exp_done, sum_safe, inverted, probs_turned, probs_saved, summed, final_done = (
            k.sem(f"{what}_att") for what in ("scored", "masked", "exp_done", "sum_safe", "inverted", "probs_turned",
                                              "probs_saved", "summed", "final_done"))
        block = ctx.enter_context(nc.Block("attend"))

        scores = k.psum[0:P, 0:N]

        def turned():
            return k.psum[0:P, 3 * BANK:3 * BANK + T // 2 * HALF].rearrange("p (b c) -> p b c", c=HALF)[:, :, 0:2 * P]

        def out_bank(u):
            at = (6 + u % 2) * BANK
            return k.psum[0:P, at:at + CH]

        def units(eng, emit):
            run_units(eng, H, T, emit)

        @block.sync
        def _(sp):
            def load(n):
                if n.live():
                    wait_unit(sp, scored, n, ago=T - B + 1)
                    for copy in range(2):
                        sp.dma_start(q[copy * CH:(copy + 1) * CH, :, n.tile * P:(n.tile + B) * P].bitcast(F32),
                                     q_halves[bass.ds(n.head * CH, CH), :, n.tile * P:(n.tile + B) * P]
                                     ).then_inc(q_loaded[n.tile // B], 16)

            def step(n):
                if n.tile % B == 2:
                    load(n.shift(B - 2 + B))
                if n.tile % B == 1:
                    n = n.shift(-2)
                    if n.live():
                        half = n.tile // B
                        wait_unit(sp, final_done, n)
                        sp.dma_start(out_rows.rearrange("(t p) m -> p t m", p=P)[:, half * B:(half + 1) * B, bass.ds(n.head * CH, CH)],
                                     final[:, half]).then_inc(stored[half], 16)

            for half in range(2):
                load(Unit(0, half * B, H, T))
            units(sp, step)
            for half in range(2):
                sp.wait_ge(stored[half], 16 * H)

        @block.tensor
        def _(pe):
            def score(n):
                if n.live():
                    if n.tile % B == 0:
                        pe.wait_ge(q_loaded[n.tile // B], (n.head + 1) * 32)
                    wait_unit(pe, masked, n, ago=1)
                    for a, width in pieces(N):
                        for half in range(2):
                            total = pe.matmul(scores[:, a:a + width], q[:, half, n.tile * P:(n.tile + 1) * P], k_halves[:, n.head, a:a + width],
                                              start=half == 0, stop=half == 1)
                    total.then_inc(scored, 1)

            def step(n):
                if n.live():
                    wait_unit(pe, exp_done, n)
                    wait_unit(pe, probs_saved, n, ago=1)
                    for i in range(T):
                        block_t = pe.transpose(turned()[:, i // 2, (i % 2) * P:(i % 2 + 1) * P],
                                               probs[:, n.tile % B, i * P:(i + 1) * P], k.ident[0:P, 0:P])
                    block_t.then_inc(probs_turned, 1)
                m = n.shift(-2)
                if m.live():
                    wait_unit(pe, probs_saved, m)
                    wait_unit(pe, final_done, m, ago=2)
                    for i in range(T):
                        total = pe.matmul(out_bank(m.tile), probs_t[:, m.tile % B, i], v_rows[:, i, bass.ds(m.head * CH, CH)],
                                          start=i == 0, stop=i == T - 1)
                    total.then_inc(summed, 1)
                score(n.shift(3))

            for u in range(3):
                score(Unit(0, u, H, T))
            units(pe, step)

        @block.scalar
        def _(act):
            act.preload_act_table_set(EXP_LN)

            def exponential(n):
                if n.live():
                    wait_unit(act, masked, n)
                    act.activation(probs[:, n.tile % B], probs[:, n.tile % B], ACT.Exp, scale=-1.0,
                                   bias=neg_max[:, n.tile:n.tile + 1],
                                   accum_out=sums[:, n.tile:n.tile + 1]).then_inc(exp_done, 1)

            def step(n):
                if n.live():
                    wait_unit(act, probs_turned, n)
                    wait_unit(act, summed, n, ago=B)
                    act.copy(probs_t[:, n.tile % B].rearrange("p (b c) n -> p b (c n)", c=2), turned()
                             ).then_inc(probs_saved, 1)
                exponential(n.shift(2))
                n = n.shift(-2)
                if n.live():
                    wait_unit(act, summed, n)
                    wait_unit(act, inverted, n)
                    half, t = n.tile // B, n.tile % B
                    if t == 0 and not (isinstance(n.head, int) and n.head == 0):
                        act.wait_ge(stored[half], n.head * 16)
                    act.activation(final[:, half, t], out_bank(n.tile), ACT.Copy,
                                   scale=inverse[:, n.tile:n.tile + 1]).then_inc(final_done, 1)

            for u in range(2):
                exponential(Unit(0, u, H, T))
            units(act, step)

        @block.vector
        def _(dve):
            def invert(n):
                if n.live():
                    wait_unit(dve, sum_safe, n)
                    dve.reciprocal(inverse[:, n.tile:n.tile + 1], sums_safe[:, n.tile:n.tile + 1]).then_inc(inverted, 1)

            def wait_mask(n):
                if n.live():
                    wait_unit(dve, scored, n)
                    wait_unit(dve, probs_turned, n, ago=B)

            def mask(n):
                if n.live():
                    dve.tensor_tensor_reduce(probs[:, n.tile % B], scores, k.log_counts[:, n.tile, :],
                                             -1.0, -FLOOR, ALU.add, ALU.min, neg_max[:, n.tile:n.tile + 1]).then_inc(masked, 1)

            def step(n):
                wait_mask(n.shift(2))
                invert(n.shift(-1))
                mask(n.shift(2))
                if n.live():
                    wait_unit(dve, exp_done, n)
                    dve.tensor_scalar(sums_safe[:, n.tile:n.tile + 1], sums[:, n.tile:n.tile + 1],
                                      TINY, None, ALU.add).then_inc(sum_safe, 1)

            for u in range(2):
                wait_mask(Unit(0, u, H, T))
                mask(Unit(0, u, H, T))
            units(dve, step)


def stage_out(k, rows, x_cols, w, bo, y):
    nc, P, T, N, D = k.nc, k.P, k.T, k.N, k.D
    C = D // 128
    W, CHUNKS = 2 * P, T // 2
    with k.stage("stage_out") as ctx:
        def sb(what, shape, dt=F32):
            return ctx.enter_context(nc.sbuf_tensor(f"{what}_out", shape, dt))

        a_rows = sb("a_rows", [P, 2, 2, D])
        a_high, a_low = sb("a_high", [128, 2, C, W], F32R), sb("a_low", [128, 2, C, W], F32R)
        bias = sb("bias", [128, C])
        bias_loaded, x_loaded, turned_done, high_done, low_done, summed, added = (
            k.sem(f"{what}_out") for what in ("bias_loaded", "x_loaded", "turned_done", "high_done", "low_done",
                                              "summed", "added"))
        a_loaded = [k.sem(f"a_loaded{slot}_out") for slot in range(2)]
        block = ctx.enter_context(nc.Block("out"))

        def banks(first, slot):
            at = (first + slot * 2) * BANK
            return k.psum[:, at:at + C // 2 * BANK].rearrange("p (b c) -> p b c", b=C // 2)[:, :, 0:2 * W]

        def chunk(first, slot, c):
            return banks(first, slot)[:, c // 2, c % 2 * W:(c % 2 + 1) * W]

        def pairs(v, slot):
            return v[:, slot].rearrange("p (b c) n -> p b (c n)", c=2)

        @block.sync
        def _(sp):
            sp.dma_start(bias[:], bo.rearrange("(c p) -> p c", p=128), allow_slow_non_contiguous=True).then_inc(bias_loaded, 16)

            def step(s):
                wait_item(sp, turned_done, s, ago=2)
                sp.dma_start(a_rows[:, s.slot], rows[bass.ds(s.item * W, W), :].rearrange("(t p) d -> p t d", p=P)
                             ).then_inc(a_loaded[s.slot], 16)
                if s.first():
                    sp.dma_start(y[:], x_cols.rearrange("(c p) n -> p c n", p=128)).then_inc(x_loaded, 16)

            run_steps(sp, CHUNKS, 0, step)

        @block.tensor
        def _(pe):
            def step(s):
                if s.live():
                    wait_loaded(pe, a_loaded, s)
                    wait_item(pe, low_done, s, ago=2)
                    for c in range(C):
                        for t in range(2):
                            block_t = pe.transpose(chunk(0, s.slot, c)[:, t * P:(t + 1) * P],
                                                   a_rows[:, s.slot, t, c * 128:(c + 1) * 128], k.ident[0:P, 0:P])
                    block_t.then_inc(turned_done, 1)
                s = s.back(1)
                if s.live():
                    wait_item(pe, low_done, s)
                    wait_item(pe, added, s, ago=2)
                    for o in range(C):
                        for c in range(C):
                            total = three_passes(pe, chunk(4, s.slot, o), a_high[:, s.slot, c], a_low[:, s.slot, c],
                                                 w[0][:, c, o * 128:(o + 1) * 128], w[1][:, c, o * 128:(o + 1) * 128],
                                                 c == 0, c == C - 1)
                    total.then_inc(summed, 1)

            run_steps(pe, CHUNKS, 1, step)

        @block.scalar
        def _(act):
            def step(s):
                wait_item(act, turned_done, s)
                wait_item(act, summed, s, ago=2)
                act.copy(pairs(a_high, s.slot), banks(0, s.slot)).then_inc(high_done, 1)

            run_steps(act, CHUNKS, 0, step)

        @block.vector
        def _(dve):
            dve.wait_ge(bias_loaded, 16)
            dve.wait_ge(x_loaded, 16)

            def step(s):
                if s.live():
                    wait_item(dve, high_done, s)
                    dve.tensor_tensor(pairs(a_low, s.slot), banks(0, s.slot), pairs(a_high, s.slot).bitcast(F32),
                                      ALU.subtract).then_inc(low_done, 1)
                s = s.back(2)
                if s.live():
                    wait_item(dve, summed, s)
                    for c in range(C):
                        cols = y[:, c, bass.ds(s.item * W, W)]
                        made = dve.scalar_tensor_tensor(cols, chunk(4, s.slot, c), bias[:, c:c + 1], cols, ALU.add, ALU.add)
                    made.then_inc(added, 1)

            run_steps(dve, CHUNKS, 2, step)


def stage_feed_forward(k, w1, b1, w2, b2, y):
    nc, P, T, N, D = k.nc, k.P, k.T, k.N, k.D
    C, F = D // 128, b1.shape[0] // 128
    W, CHUNKS = 2 * P, T // 2
    with k.stage("stage_feed_forward") as ctx:
        def sb(what, shape, dt=F32):
            return ctx.enter_context(nc.sbuf_tensor(f"{what}_ff", shape, dt))

        x_high, x_low = sb("x_high", [128, 2, C, W], F32R), sb("x_low", [128, 2, C, W], F32R)
        f, f_high, f_low = sb("f", [128, 2, F, W]), sb("f_high", [128, 2, F, W], F32R), sb("f_low", [128, 2, F, W], F32R)
        bias1, bias2 = sb("bias1", [128, F]), sb("bias2", [128, C])
        bias_loaded, x_high_done, x_low_done, f_summed, f_saved, f_high_done, f_low_done, summed, added = (
            k.sem(f"{what}_ff") for what in ("bias_loaded", "x_high_done", "x_low_done", "f_summed",
                                             "f_saved", "f_high_done", "f_low_done", "summed", "added"))
        block = ctx.enter_context(nc.Block("feed_forward"))

        def hidden(slot, c):
            return k.psum[:, slot * BANK + c * W:slot * BANK + (c + 1) * W]

        def result(slot, c):
            at = (4 + slot * 2 + c // 2) * BANK + c % 2 * W
            return k.psum[:, at:at + W]

        @block.sync
        def _(sp):
            sp.dma_start(bias1[:], b1.rearrange("(c p) -> p c", p=128), allow_slow_non_contiguous=True).then_inc(bias_loaded, 16)
            sp.dma_start(bias2[:], b2.rearrange("(c p) -> p c", p=128), allow_slow_non_contiguous=True).then_inc(bias_loaded, 16)

        @block.tensor
        def _(pe):
            def step(s):
                if s.live():
                    wait_item(pe, x_low_done, s)
                    wait_item(pe, f_saved, s, ago=2)
                    for o in range(F):
                        for c in range(C):
                            total = three_passes(pe, hidden(s.slot, o), x_high[:, s.slot, c], x_low[:, s.slot, c],
                                                 w1[0][:, c, o * 128:(o + 1) * 128], w1[1][:, c, o * 128:(o + 1) * 128],
                                                 c == 0, c == C - 1)
                    total.then_inc(f_summed, 1)
                s = s.back(1)
                if s.live():
                    wait_item(pe, f_low_done, s)
                    wait_item(pe, added, s, ago=2)
                    for o in range(C):
                        for c in range(F):
                            total = three_passes(pe, result(s.slot, o), f_high[:, s.slot, c], f_low[:, s.slot, c],
                                                 w2[0][:, c, o * 128:(o + 1) * 128], w2[1][:, c, o * 128:(o + 1) * 128],
                                                 c == 0, c == F - 1)
                    total.then_inc(summed, 1)

            run_steps(pe, CHUNKS, 1, step)

        @block.scalar
        def _(act):
            act.wait_ge(bias_loaded, 32)

            def step(s):
                if s.live():
                    wait_item(act, f_summed, s, ago=2)
                    act.copy(x_high[:, s.slot], y[:, :, bass.ds(s.item * W, W)]).then_inc(x_high_done, 1)
                s = s.back(1)
                if s.live():
                    wait_item(act, f_summed, s)
                    wait_item(act, f_low_done, s, ago=2)
                    for c in range(F):
                        saved = act.activation(f[:, s.slot, c], hidden(s.slot, c), ACT.Relu, bias=bias1[:, c:c + 1])
                    saved.then_inc(f_saved, 1)
                    wait_item(act, f_saved, s)
                    wait_item(act, summed, s, ago=2)
                    act.copy(f_high[:, s.slot], f[:, s.slot]).then_inc(f_high_done, 1)

            run_steps(act, CHUNKS, 1, step)

        @block.vector
        def _(dve):
            dve.wait_ge(bias_loaded, 32)

            def step(s):
                if s.live():
                    wait_item(dve, x_high_done, s)
                    dve.tensor_tensor(x_low[:, s.slot], y[:, :, bass.ds(s.item * W, W)], x_high[:, s.slot].bitcast(F32),
                                      ALU.subtract).then_inc(x_low_done, 1)
                s = s.back(1)
                if s.live():
                    wait_item(dve, f_high_done, s)
                    dve.tensor_tensor(f_low[:, s.slot], f[:, s.slot], f_high[:, s.slot].bitcast(F32), ALU.subtract
                                      ).then_inc(f_low_done, 1)
                s = s.back(1)
                if s.live():
                    wait_item(dve, summed, s)
                    for c in range(C):
                        cols = y[:, c, bass.ds(s.item * W, W)]
                        made = dve.scalar_tensor_tensor(cols, result(s.slot, c), bias2[:, c:c + 1], cols, ALU.add, ALU.add)
                    made.then_inc(added, 1)

            run_steps(dve, CHUNKS, 2, step)


def stage_batch_norm(k, name, gamma, beta, y, x_cols):
    nc, N, D = k.nc, k.N, k.D
    C = D // 128
    parts = -(-N // BANK)
    cuts = [N * i // parts for i in range(parts + 1)]
    with k.stage("stage_batch_norm") as ctx:
        def sb(what, shape, dt=F32):
            return ctx.enter_context(nc.sbuf_tensor(f"{what}_{name}", shape, dt))

        g, b = sb("g", [128, C]), sb("b", [128, C])
        stats, moments = sb("stats", [128, C, parts * 6]), sb("moments", [128, C, 2])
        spread, deviation, inverse = sb("spread", [128, C]), sb("deviation", [128, C]), sb("inverse", [128, C])
        scale, moved, shift = sb("scale", [128, C]), sb("moved", [128, C]), sb("shift", [128, C])
        loaded, stats_done, moments_done, spread_done, deviation_done, inverse_done, scale_done, moved_done, shift_done, \
            normed, stored = (
                k.sem(f"{what}_{name}") for what in ("loaded", "stats_done", "moments_done", "spread_done", "deviation_done",
                                                     "inverse_done", "scale_done", "moved_done", "shift_done", "normed",
                                                     "stored"))
        block = ctx.enter_context(nc.Block(name))

        @block.sync
        def _(sp):
            sp.dma_start(g[:], gamma.rearrange("(c p) -> p c", p=128), allow_slow_non_contiguous=True).then_inc(loaded, 16)
            sp.dma_start(b[:], beta.rearrange("(c p) -> p c", p=128), allow_slow_non_contiguous=True).then_inc(loaded, 16)
            if x_cols is not None:
                for c in range(C):
                    sp.wait_ge(normed, c + 1)
                    sp.dma_start(x_cols[c * 128:(c + 1) * 128, :], y[:, c]).then_inc(stored, 16)
                sp.wait_ge(stored, (16 * C))

        @block.vector
        def _(dve):
            for c in range(C):
                for i in range(parts):
                    done = dve.bn_stats(stats[:, c, 6 * i:6 * i + 6], y[:, c, cuts[i]:cuts[i + 1]])
            done.then_inc(stats_done, 1)
            dve.wait_ge(stats_done, 1)
            for c in range(C):
                done = dve.bn_aggr(moments[:, c], stats[:, c])
            done.then_inc(moments_done, 1)
            dve.wait_ge(moments_done, 1)
            dve.tensor_scalar(spread[:], moments[:, :, 1], EPS, None, ALU.add).then_inc(spread_done, 1)
            dve.wait_ge(deviation_done, 1)
            dve.reciprocal(inverse[:], deviation[:]).then_inc(inverse_done, 1)
            dve.wait_ge(inverse_done, 1)
            dve.wait_ge(loaded, 32)
            dve.tensor_tensor(scale[:], inverse[:], g[:], ALU.mult).then_inc(scale_done, 1)
            dve.wait_ge(scale_done, 1)
            dve.tensor_tensor(moved[:], moments[:, :, 0], scale[:], ALU.mult).then_inc(moved_done, 1)
            dve.wait_ge(moved_done, 1)
            dve.tensor_tensor(shift[:], b[:], moved[:], ALU.subtract).then_inc(shift_done, 1)
            dve.wait_ge(shift_done, 1)
            for c in range(C):
                dve.tensor_scalar(y[:, c], y[:, c], scale[:, c:c + 1], shift[:, c:c + 1], ALU.mult, ALU.add
                                  ).then_inc(normed, 1)

        @block.scalar
        def _(act):
            act.wait_ge(spread_done, 1)
            act.activation(deviation[:], spread[:], ACT.Sqrt).then_inc(deviation_done, 1)


def stage_final(k, x_cols, ln_g, ln_b, x_rows, out):
    nc, P, T, N, D = k.nc, k.P, k.T, k.N, k.D
    C = D // 128
    with k.stage("stage_final") as ctx:
        def sb(what, shape, dt=F32):
            return ctx.enter_context(nc.sbuf_tensor(f"{what}_fin", shape, dt))

        cols = sb("cols", [128, 2, C, P])
        z, x1 = sb("z", [P, T, D]), sb("x1", [P, T, D])
        g, b = sb("g", [P, D]), sb("b", [P, D])
        stats, moments = sb("stats", [P, T, 6]), [sb(f"moments{r}", [P, T, 2]) for r in range(2)]
        spread, deviation = [[sb(f"{what}{r}", [P, T]) for r in range(2)] for what in ("spread", "deviation")]
        inverse = [sb(f"inverse{r}", [P, T]) for r in range(2)]
        cols_loaded = [k.sem(f"cols_loaded{i}_fin") for i in range(2)]
        x1_loaded, gb_loaded, turned, saved, stats_done, moments_done, spread_done, deviation_done, \
            inverse_done, normed, gained, shifted, added, out_stored = (
                k.sem(f"{what}_fin") for what in ("x1_loaded", "gb_loaded", "turned", "saved", "stats_done",
                                                  "moments_done", "spread_done", "deviation_done", "inverse_done",
                                                  "normed", "gained", "shifted", "added", "out_stored"))
        block = ctx.enter_context(nc.Block("final"))

        def bank(slot):
            return k.psum[0:P, slot * BANK:(slot + 1) * BANK]

        @block.sync
        def _(sp):
            def load(s):
                wait_item(sp, turned, s, ago=2)
                sp.dma_start(cols[:, s.slot], x_cols.rearrange("(c p) n -> p c n", p=128)[:, :, bass.ds(s.item * P, P)]
                             ).then_inc(cols_loaded[s.slot], 16)

            run_steps(sp, T, 0, load)
            sp.dma_start(x1[:], x_rows.rearrange("(t p) d -> p t d", p=P)).then_inc(x1_loaded, 16)
            for v, w in ((g, ln_g), (b, ln_b)):
                sp.dma_start(v[:], w.rearrange("(o d) -> o d", o=1).to_broadcast([P, D])).then_inc(gb_loaded, 16)
            with sp.Fori(0, T) as t:
                sp.wait_ge(normed, T + t + 1)
                sp.dma_start(out[bass.ds(t * P, P), :], z[:, t, :]).then_inc(out_stored, 16)
            sp.wait_ge(out_stored, 16 * T)

        @block.tensor
        def _(pe):
            def step(s):
                wait_loaded(pe, cols_loaded, s)
                wait_item(pe, saved, s, ago=2)
                for c in range(C):
                    block_t = pe.transpose(bank(s.slot)[:, c * 128:(c + 1) * 128], cols[:, s.slot, c], k.ident[:])
                block_t.then_inc(turned, 1)

            run_steps(pe, T, 0, step)

        @block.scalar
        def _(act):
            def step(s):
                wait_item(act, turned, s)
                act.copy(z[:, s.item, :], bank(s.slot)).then_inc(saved, 1)

            run_steps(act, T, 0, step)
            for r in range(2):
                act.wait_ge(spread_done, r + 1)
                act.activation(deviation[r][:], spread[r][:], ACT.Sqrt).then_inc(deviation_done, 1)

        @block.gpsimd
        def _(pool):
            pool.wait_ge(gb_loaded, 32)
            with pool.Fori(0, T) as t:
                pool.wait_ge(gained, t + 1)
                pool.tensor_tensor(z[:, t, :], z[:, t, :], b[:], ALU.add).then_inc(shifted, 1)

        @block.vector
        def _(dve):
            def stats_of(t):
                dve.bn_stats(stats[:, t, :], z[:, t, :]).then_inc(stats_done, 1)

            def invert(r):
                dve.wait_ge(stats_done, (r + 1) * T)
                for t in range(T):
                    dve.bn_aggr(moments[r][:, t], stats[:, t]).then_inc(moments_done, 1)
                dve.wait_ge(moments_done, (r + 1) * T)
                dve.tensor_scalar(spread[r][:], moments[r][:, :, 1], EPS, None, ALU.add).then_inc(spread_done, 1)
                dve.wait_ge(deviation_done, r + 1)
                dve.reciprocal(inverse[r][:], deviation[r][:]).then_inc(inverse_done, 1)
                dve.wait_ge(inverse_done, r + 1)

            def norm(r, t):
                return dve.tensor_scalar(z[:, t, :], z[:, t, :], moments[r][:, t, 0:1], inverse[r][:, bass.ds(t, 1)],
                                         ALU.subtract, ALU.mult).then_inc(normed, 1)

            with dve.Fori(0, T) as t:
                dve.wait_ge(saved, t + 1)
                stats_of(t)
            invert(0)
            dve.wait_ge(gb_loaded, 32)
            with dve.Fori(0, T) as t:
                norm(0, t)
                dve.wait_ge(normed, t + 1)
                dve.tensor_tensor(z[:, t, :], z[:, t, :], g[:], ALU.mult).then_inc(gained, 1)
            dve.wait_ge(x1_loaded, 16)
            with dve.Fori(0, T) as t:
                dve.wait_ge(shifted, t + 1)
                dve.tensor_tensor(z[:, t, :], z[:, t, :], x1[:, t, :], ALU.add).then_inc(added, 1)
                dve.wait_ge(added, t + 1)
                stats_of(t)
            invert(1)
            with dve.Fori(0, T) as t:
                norm(1, t)


def build(nc, **a):
    src, dst, x = a["src"], a["dst"], a["x"]
    k = Kernel(nc, x, src)
    P, T, N, D, H = k.P, k.T, k.N, k.D, k.H
    with k.ctx:
        k.psum = k.ctx.enter_context(nc.psum_tensor("banks", [128, 8 * BANK], F32))
        k.ident = k.sb("ident", [128, 128])
        k.ones = k.sb("ones", [128, 1])
        k.edges_found = k.sb("edges_found", [1, 1], I32)
        k.log_counts = k.sb("log_counts", [P, T, N])
        diag_ctx = k.ctx.enter_context(ExitStack())
        k.plain_diag = diag_ctx.enter_context(nc.sbuf_tensor("plain_diag", [P, T, P], F32))

        with ExitStack() as edge_ctx:
            share = k.chunks // T
            window = -(-(share + 4) // 3) * 3
            k.pad_left = (window - share) // 2
            k.node_row = edge_ctx.enter_context(nc.sbuf_tensor("node_row", [128, N], F16))
            k.end_cols = edge_ctx.enter_context(
                nc.sbuf_tensor("end_cols", [P, 2, k.chunks + window - share], F32))
            stage_edges(k, src, dst)
            stage_count(k, "count_windows", lambda t: t * share, window, window // 3, verify=True)
            found = nc.values_load(k.edges_found[0:1, 0:1], min_val=0, max_val=k.E)
            with nc.If(found < k.E):
                nc.gpsimd.nop()
                nc.sync.nop()
                stage_count(k, "count_all", lambda t: k.pad_left, k.chunks, divisor(k.chunks, 8), verify=False)
            stage_logs(k)
        hidden = H * a["L0_gnn_att_src1"].shape[1]
        classes = H * a["L0_gnn_att_src2"].shape[1]
        gat1_rows = k.dram("gat1_rows", [N, hidden])
        gat2_rows = k.dram("gat2_rows", [N, classes])
        a_src_rows = k.dram("a_src_rows", [H, N])
        for name, rows, width, w, att_src, att_dst, row_bias, out_rows in (
                ("gat1", x, hidden, a["L0_gnn_W1"], a["L0_gnn_att_src1"], a["L0_gnn_att_dst1"], None, gat1_rows),
                ("gat2", gat1_rows, classes, a["L0_gnn_W2"], a["L0_gnn_att_src2"], a["L0_gnn_att_dst2"], a["L0_gnn_b1"], gat2_rows)):
            with ExitStack() as gat_ctx:
                h_sb = gat_ctx.enter_context(nc.sbuf_tensor(f"h_{name}", [P, T, width], F32))
                a_dst = gat_ctx.enter_context(nc.sbuf_tensor(f"a_dst_{name}", [P, T, H], F32))
                stage_gat_project(k, name, rows, row_bias, w, att_src, att_dst, h_sb, a_dst, a_src_rows)
                stage_gat_attend(k, name, h_sb, a_dst, a_src_rows, out_rows)
        x_rows = k.dram("x_rows", [N, D])
        x_cols = k.dram("x_cols", [D, N])
        stage_gat_finish(k, gat2_rows, a["L0_gnn_b2"], x, x_rows, x_cols)
        stage_plain_counts(k)
        diag_ctx.close()
        w = {name: a[f"L1_gnn_{name}"] for name in ("Wq", "Wk", "Wv", "Wo", "W1", "W2", "bq", "bo", "b1", "b2",
                                                    "g1", "beta1", "g2", "beta2")}
        C, F, CH = D // 128, w["W1"].shape[1] // 128, D // H
        q_halves = k.dram("q_halves", [D, 2, N])
        att_rows = k.dram("att_rows", [N, D])
        with nc.Fori(0, w["Wq"].shape[0]) as layer:
            with ExitStack() as ctx:
                k_halves = ctx.enter_context(nc.sbuf_tensor("k_halves", [2 * CH, H, N], F32R))
                v_rows = ctx.enter_context(nc.sbuf_tensor("v_rows", [P, T, D], F32))
                with ExitStack() as w_ctx:
                    wq, wk, wv = (halves(nc, w_ctx, name, C, D) for name in ("wq", "wk", "wv"))
                    stage_turn_weights(k, "qkv", [(w["Wq"][layer], *wq), (w["Wk"][layer], *wk), (w["Wv"][layer], *wv)])
                    stage_qkv(k, x_cols, wq, wk, wv, w["bq"][layer], q_halves, k_halves, v_rows)
                stage_attend(k, q_halves, k_halves, v_rows, att_rows)
            with ExitStack() as w_ctx:
                y = w_ctx.enter_context(nc.sbuf_tensor("y", [128, C, N], F32))
                wo, w1, w2 = (halves(nc, w_ctx, *v) for v in (("wo", C, D), ("w1", C, F * 128), ("w2", F, D)))
                stage_turn_weights(k, "rest", [(w["Wo"][layer], *wo), (w["W1"][layer], *w1), (w["W2"][layer], *w2)])
                stage_out(k, att_rows, x_cols, wo, w["bo"][layer], y)
                stage_batch_norm(k, "norm1", w["g1"][layer], w["beta1"][layer], y, None)
                stage_feed_forward(k, w1, w["b1"][layer], w2, w["b2"][layer], y)
                stage_batch_norm(k, "norm2", w["g2"][layer], w["beta2"][layer], y, x_cols)
        stage_final(k, x_cols, a["L1_gnn_ln_g"], a["L1_gnn_ln_b"], x_rows, a["out"])



INPUTS = ("x", "src", "dst") + tuple(f"L0_gnn_{name}" for name in (
    "W1", "att_src1", "att_dst1", "b1", "W2", "att_src2", "att_dst2", "b2")) + tuple(f"L1_gnn_{name}" for name in (
        "Wq", "bq", "Wk", "Wv", "Wo", "bo", "W1", "b1", "W2", "b2", "g1", "beta1", "g2", "beta2", "ln_g", "ln_b"))


def kernel(**inputs):
    import numpy as np
    import concourse.bacc as bacc
    from concourse.bass_utils import run_bass_kernel_spmd

    nc = bacc.Bacc("TRN2", target_bir_lowering=False, num_devices=1)
    arrays, args = {}, {}
    for name in INPUTS:
        array = np.ascontiguousarray(inputs[name])
        arrays[f"in_{name}_dram"] = array
        args[name] = nc.dram_tensor(f"in_{name}_dram", array.shape, mybir.dt.from_np(array.dtype), kind="ExternalInput").ap()
    args["out"] = nc.dram_tensor("out_0_dram", inputs["x"].shape, F32, kind="ExternalOutput").ap()
    build(nc, **args)
    result = run_bass_kernel_spmd(nc, [arrays], core_ids=[0])
    return result.results[0]["out_0_dram"]
```

```python
from contextlib import ExitStack, contextmanager

import concourse.bass as bass
from concourse import mybir

ALU = mybir.AluOpType
ACT = mybir.ActivationFunctionType
AX_X = mybir.AxisListType.X
F32 = mybir.dt.float32
F32R = mybir.dt.float32r
F16 = mybir.dt.float16
BF16 = mybir.dt.bfloat16
I32 = mybir.dt.int32

BANK = 512
NEG_SLOPE = 0.2
GAIN = 1 / NEG_SLOPE
EPS = 1e-5
TINY = 1e-16
NO_EDGE = -1e30
FLOOR = -1e29
LEAST_COUNT = 2.0 ** -64
EXP_LN = "natural_log_exp_and_others"


def pieces(width):
    return [(a, min(BANK, width - a)) for a in range(0, width, BANK)]


def divisor(n, limit=128):
    return max(p for p in range(1, limit + 1) if n % p == 0)


class Step:

    def __init__(self, item, slot, turn, total):
        self.item, self.slot, self.turn, self.total = item, slot, turn, total

    def back(self, d):
        return Step(self.item - d, (self.slot - d) % 2, self.turn + (self.slot - d) // 2, self.total)

    def live(self):
        return not isinstance(self.item, int) or 0 <= self.item < self.total

    def first(self):
        return isinstance(self.item, int) and self.item == 0


def run_steps(eng, total, lag, emit):
    head = 2 * ((lag + 1) // 2) + 2
    if (total - head) // 2 < 2:
        head = total + lag
    for s in range(head):
        emit(Step(s, s % 2, s // 2, total))
    pairs = max(0, (total - head) // 2)
    if pairs > 0:
        with eng.Fori(0, pairs) as i:
            for slot in range(2):
                emit(Step(i * 2 + (head + slot), slot, i + head // 2, total))
    for s in range(head + 2 * pairs, total + lag):
        emit(Step(s, s % 2, s // 2, total))


def wait_item(eng, sem, step, ago=0):
    count = step.item - ago + 1
    if not isinstance(count, int) or count > 0:
        eng.wait_ge(sem, count)


def wait_loaded(eng, sems, step):
    eng.wait_ge(sems[step.slot], (step.turn + 1) * 16)


def wait_stored(eng, sems, step, dmas=1):
    last = step.back(2)
    if last.live():
        eng.wait_ge(sems[step.slot], (last.turn + 1) * (16 * dmas))


class Unit:

    def __init__(self, head, tile, heads, tiles):
        self.head, self.tile, self.heads, self.tiles = head, tile, heads, tiles

    def shift(self, d):
        v = self.tile + d
        return Unit(self.head + v // self.tiles, v % self.tiles, self.heads, self.tiles)

    def live(self):
        return not isinstance(self.head, int) or 0 <= self.head < self.heads

    def number(self):
        return self.head * self.tiles + self.tile

    def starts(self, head):
        return isinstance(self.head, int) and self.head == head and self.tile == 0


def run_units(eng, heads, tiles, emit):
    for t in range(tiles):
        emit(Unit(0, t, heads, tiles))
    with eng.Fori(1, heads - 1) as h:
        for t in range(tiles):
            emit(Unit(h, t, heads, tiles))
    for h in (heads - 1, heads):
        for t in range(tiles):
            emit(Unit(h, t, heads, tiles))


def wait_unit(eng, sem, unit, ago=0):
    count = unit.number() - ago + 1
    if not isinstance(count, int) or count > 0:
        eng.wait_ge(sem, count)


class Kernel:

    def __init__(self, nc, x, src):
        self.nc = nc
        self.N, self.D = x.shape
        self.P = divisor(self.N)
        self.T = self.N // self.P
        self.H = 8
        self.E = src.shape[0]
        self.chunks = self.E // self.P
        self.chunk_rows = divisor(self.chunks)
        self.ctx = ExitStack()

    def sb(self, name, shape, dt=F32):
        return self.ctx.enter_context(self.nc.sbuf_tensor(name, shape, dt))

    def sem(self, name):
        self.stage_sems.append(self.nc.alloc_semaphore(name))
        return self.stage_sems[-1]

    @contextmanager
    def stage(self, name):
        self.stage_sems = []
        with ExitStack() as buffers:
            yield buffers
        self.nc.clear_and_free_semaphores(self.stage_sems)
        self.nc.all_engine_barrier()

    def dram(self, name, shape, dt=F32):
        return self.nc.dram_tensor(name, shape, dt, kind="Internal").ap()




def stage_edges(k, src, dst):
    nc, P, N = k.nc, k.P, k.N
    rows, parts = k.chunk_rows, k.chunks // k.chunk_rows
    with k.stage("stage_edges") as ctx:
        ends_int = ctx.enter_context(nc.sbuf_tensor("ends_int", [rows, 2, parts, P], I32))
        ends_f32 = ctx.enter_context(nc.sbuf_tensor("ends_f32", [rows, 2, parts, P], F32))
        ends_loaded = k.sem("ends_loaded")
        ends_cast = k.sem("ends_cast")
        ends_turned = k.sem("ends_turned")
        zeroed = k.sem("zeroed")
        padded = k.sem("padded")
        ident_made = k.sem("ident_made")
        cols_saved = k.sem("cols_saved")
        block = ctx.enter_context(nc.Block("edges"))

        @block.sync
        def _(sp):
            for i, ends in enumerate((src, dst)):
                sp.dma_start(ends_int[:, i], ends.rearrange("(a p e) -> p a e", a=parts, p=rows)).then_inc(ends_loaded, 16)

        @block.gpsimd
        def _(pool):
            pool.memset(k.ident[:], 0.0).then_inc(zeroed, 1)
            pool.wait_ge(zeroed, 1)
            pool.affine_select(out=k.ident[:], in_=k.ident[:], compare_op=ALU.not_equal, fill=1.0,
                               base=0, pattern=[[-1, 128]], channel_multiplier=1).then_inc(ident_made, 1)
            pool.iota(k.node_row[:], [[1, N]], base=0, channel_multiplier=0,
                      allow_small_or_imprecise_dtypes=True)
            pool.memset(k.ones[:], 1.0)

        @block.vector
        def _(dve):
            dve.memset(k.end_cols[:], -1.0).then_inc(padded, 1)
            dve.wait_ge(ends_loaded, 32)
            dve.tensor_copy(ends_f32[:], ends_int[:]).then_inc(ends_cast, 1)
            dve.wait_ge(padded, 1)
            for i in range(2):
                dve.wait_ge(ends_turned, i + 1)
                dve.tensor_copy(k.end_cols[:, i, k.pad_left:k.pad_left + k.chunks],
                                k.psum[0:P, i * BANK:i * BANK + k.chunks]).then_inc(cols_saved, 1)
            dve.wait_ge(cols_saved, 2)
            dve.tensor_scalar(k.minus_targets[:], k.end_cols[:, 1], -1.0, None, ALU.mult)

        @block.tensor
        def _(pe):
            pe.wait_ge(ident_made, 1)
            pe.wait_ge(ends_cast, 1)
            for i in range(2):
                for a in range(parts):
                    turned = pe.transpose(k.psum[0:P, i * BANK + a * rows:i * BANK + (a + 1) * rows],
                                          ends_f32[:, i, a], k.ident[0:rows, 0:rows])
                turned.then_inc(ends_turned, 1)


def stage_count(k, name, first_chunk, chunks, R, verify):
    nc, P, T, N = k.nc, k.P, k.T, k.N
    assert chunks % R == 0
    groups = chunks // R
    batches = [(R * b // 3, R * (b + 1) // 3) for b in range(3)]
    with k.stage("stage_count") as ctx:
        src_hot = ctx.enter_context(nc.sbuf_tensor(f"src_hot_{name}", [P, R, N], BF16))
        distance = ctx.enter_context(nc.sbuf_tensor(f"distance_{name}", [P, R, P], F32))
        dst_hot = ctx.enter_context(nc.sbuf_tensor(f"dst_hot_{name}", [P, R, P], BF16))
        row_total = ctx.enter_context(nc.sbuf_tensor(f"row_total_{name}", [P, T], F32))
        col_total = ctx.enter_context(nc.sbuf_tensor(f"col_total_{name}", [P, 1], F32))
        src_ready = k.sem(f"src_ready_{name}")
        distance_done = k.sem(f"distance_done_{name}")
        dst_ready = k.sem(f"dst_ready_{name}")
        hot_free = k.sem(f"hot_free_{name}")
        sums_free = k.sem(f"sums_free_{name}")
        total_step = k.sem(f"total_step_{name}")
        block = ctx.enter_context(nc.Block(name))

        def sums(slot, a, n):
            return k.psum[0:P, 3 * BANK * slot + a:3 * BANK * slot + a + n]

        @block.vector
        def _(dve):
            dve.sem_inc(hot_free, R)
            with dve.Fori(0, T) as t:
                with dve.Fori(0, groups) as g:
                    for r in range(R):
                        c = first_chunk(t) + g * R + r
                        dve.wait_ge(hot_free, (t * groups + g) * R + r + 1)
                        dve.tensor_scalar(src_hot[:, r], k.node_row[0:P, :], k.end_cols[:, 0, bass.ds(c, 1)], None,
                                          ALU.is_equal).then_inc(src_ready, 1)
            if verify:
                dve.wait_ge(sums_free, T + 2)
                dve.tensor_reduce(col_total[:], row_total[:], AX_X, ALU.add).then_inc(total_step, 1)
                dve.wait_ge(total_step, 2)
                dve.tensor_copy(k.edges_found[:], k.psum[0:1, 6 * BANK:6 * BANK + 1])

        @block.tensor
        def _(pe):
            def group(t, slot, g, first, last):
                for r in range(R):
                    pe.wait_ge(src_ready, (t * groups + g) * R + r + 1)
                    pe.wait_ge(dst_ready, (t * groups + g) * R + r + 1)
                    for a, n in pieces(N):
                        product = pe.matmul(sums(slot, a, n), dst_hot[:, r], src_hot[:, r, a:a + n],
                                            start=first and r == 0, stop=last and r == R - 1)
                    product.then_inc(hot_free, 1)

            def tile(t, slot):
                pe.wait_ge(sums_free, t + 1)
                group(t, slot, 0, True, False)
                with pe.Fori(1, groups - 1) as g:
                    group(t, slot, g, False, False)
                group(t, slot, groups - 1, False, True)

            with pe.Fori(0, T // 2) as i:
                tile(i * 2, 0)
                tile(i * 2 + 1, 1)
            if verify:
                pe.wait_ge(total_step, 1)
                pe.matmul(k.psum[0:1, 6 * BANK:6 * BANK + 1], col_total[:], k.ones[0:P, 0:1],
                          start=True, stop=True).then_inc(total_step, 1)

        @block.scalar
        def _(act):
            act.sem_inc(sums_free, 2)

            def group(t, g):
                done = (t * groups + g) * R
                for b in range(len(batches) + 1):
                    if b < len(batches):
                        lo, hi = batches[b]
                        for r in range(lo, hi):
                            act.activation(distance[:, r], k.node_row[0:P, bass.ds(t * P, P)], ACT.Abs,
                                           bias=k.minus_targets[:, bass.ds(first_chunk(t) + g * R + r, 1)]).then_inc(distance_done, 1)
                    if b > 0:
                        lo, hi = batches[b - 1]
                        act.wait_ge(distance_done, done + hi)
                        act.wait_ge(hot_free, done + hi)
                        later = b + 1 - len(batches)
                        used = done + batches[later][1] - (R if later < 0 else 0)
                        if not isinstance(used, int) or used > 0:
                            act.wait_ge(dst_ready, used)
                        act.activation(dst_hot[:, lo:hi], distance[:, lo:hi], ACT.Relu, scale=-1.0, bias=k.ones[0:P, :]
                                       ).then_inc(dst_ready, hi - lo)

            def save(t, slot):
                act.wait_ge(hot_free, (t + 1) * groups * R + R)
                act.activation(k.log_counts[:, t, :], sums(slot, 0, N), ACT.Copy,
                               accum_out=row_total[:, bass.ds(t, 1)]).then_inc(sums_free, 1)

            def tile(t, slot, first):
                group(t, 0)
                if not first:
                    save(t - 1, 1 - slot)
                with act.Fori(1, groups) as g:
                    group(t, g)

            tile(0, 0, True)
            tile(1, 1, False)
            with act.Fori(1, T // 2) as i:
                tile(i * 2, 0, False)
                tile(i * 2 + 1, 1, False)
            save(T - 1, 1)


def stage_logs(k):
    nc, P, T, N = k.nc, k.P, k.T, k.N
    with k.stage("stage_logs") as ctx:
        logs = ctx.enter_context(nc.sbuf_tensor("logs", [P, 2, N], F32))
        fence = ctx.enter_context(nc.sbuf_tensor("fence", [P, 2, N], F32))
        loop_counts = ctx.enter_context(nc.sbuf_tensor("loop_counts", [P, 2, P], F32))
        loop_logs = ctx.enter_context(nc.sbuf_tensor("loop_logs", [P, 2, P], F32))
        loop_fence = ctx.enter_context(nc.sbuf_tensor("loop_fence", [P, 2, P], F32))
        least = ctx.enter_context(nc.sbuf_tensor("least", [P, 1], F32))
        least_set = k.sem("least_set")
        loops_added = k.sem("loops_added")
        fences_ready = k.sem("fences_ready")
        logs_ready = k.sem("logs_ready")
        tile_done = k.sem("tile_done")
        rows_done = k.sem("rows_done")
        block = ctx.enter_context(nc.Block("logs"))

        def diag(t):
            return k.log_counts[:, t, bass.ds(t * P, P)]

        @block.gpsimd
        def _(pool):
            pool.memset(least[:], LEAST_COUNT).then_inc(least_set, 1)
            pool.sem_inc(tile_done, 2)
            with pool.Fori(0, T // 2) as i:
                for slot in range(2):
                    t = i * 2 + slot
                    pool.wait_ge(tile_done, t + 1)
                    pool.tensor_tensor(loop_counts[:, slot], diag(t), k.ident[0:P, 0:P], ALU.add).then_inc(loops_added, 1)

        @block.scalar
        def _(act):
            act.preload_act_table_set(EXP_LN)
            act.wait_ge(least_set, 1)

            def step(s):
                wait_item(act, rows_done, s, ago=2)
                act.activation(logs[:, s.slot], k.log_counts[:, s.item, :], ACT.Ln, bias=least[:])
                act.wait_ge(tile_done, s.item + 1)
                wait_item(act, loops_added, s)
                act.activation(loop_logs[:, s.slot], loop_counts[:, s.slot], ACT.Ln, bias=least[:]).then_inc(logs_ready, 1)

            run_steps(act, T, 0, step)

        @block.vector
        def _(dve):
            def step(s):
                last = s.back(2)
                if last.live():
                    wait_item(dve, rows_done, last)
                    dve.scalar_tensor_tensor(diag(last.item), loop_logs[:, last.slot], GAIN, loop_fence[:, last.slot],
                                             ALU.mult, ALU.min).then_inc(tile_done, 1)
                if s.live():
                    dve.tensor_scalar(fence[:, s.slot], k.log_counts[:, s.item, :], -0.5, -2 * NO_EDGE, ALU.add, ALU.mult)
                m = s.back(1)
                if m.live():
                    wait_item(dve, fences_ready, m)
                    wait_item(dve, logs_ready, m)
                    block_at = bass.ds(m.item * P, P)
                    dve.tensor_tensor(k.plain_diag[:, m.item, :], logs[:, m.slot, block_at], fence[:, m.slot, block_at], ALU.min)
                    dve.scalar_tensor_tensor(k.log_counts[:, m.item, :], logs[:, m.slot], GAIN, fence[:, m.slot],
                                             ALU.mult, ALU.min).then_inc(rows_done, 1)
                if s.live():
                    wait_item(dve, loops_added, s)
                    dve.tensor_scalar(loop_fence[:, s.slot], loop_counts[:, s.slot], -0.5, -2 * NO_EDGE, ALU.add, ALU.mult
                                      ).then_inc(fences_ready, 1)

            run_steps(dve, T, 2, step)


def stage_gat_project(k, name, rows, row_bias, w, att_src, att_dst, h_sb, a_dst, a_src_rows):
    nc, P, T, N, H = k.nc, k.P, k.T, k.N, k.H
    relu = row_bias is not None
    K = w.shape[0] // 128
    M = w.shape[1]
    KB = -(-K // 4)
    MB = M // BANK
    with k.stage("stage_gat_project") as ctx:
        def sb(what, shape, dt=F32):
            return ctx.enter_context(nc.sbuf_tensor(f"{what}_{name}", shape, dt))

        w_f32 = sb("w_f32", [128, K, M])
        w_high = sb("w_high", [128, K, M], F32R)
        w_low = sb("w_low", [128, K, M], F32R)
        att = sb("att", [P, 2, M])
        x_rows = sb("x_rows", [P, 2, K * 128])
        x_high = sb("x_high", [128, 2, K, P], F32R)
        x_low = sb("x_low", [128, 2, K, P], F32R)
        h_att = sb("h_att", [P, 2, 2, M])
        a_src = sb("a_src", [P, 2, H])
        a_src_t = sb("a_src_t", [H, N])
        if relu:
            bias_rows = sb("bias_rows", [P, K * 128])
            bias_loaded = k.sem(f"bias_loaded_{name}")
            x_biased = k.sem(f"x_biased_{name}")
        w_loaded = [k.sem(f"w_loaded{c}_{name}") for c in range(K)]
        att_loaded = k.sem(f"att_loaded_{name}")
        x_loaded = [k.sem(f"x_loaded{i}_{name}") for i in range(2)]
        w_high_done = k.sem(f"w_high_done_{name}")
        w_low_done = k.sem(f"w_low_done_{name}")
        x_turned = k.sem(f"x_turned_{name}")
        x_high_done = k.sem(f"x_high_done_{name}")
        x_low_done = k.sem(f"x_low_done_{name}")
        h_summed = k.sem(f"h_summed_{name}")
        h_saved = k.sem(f"h_saved_{name}")
        att_multiplied = k.sem(f"att_multiplied_{name}")
        a_reduced = k.sem(f"a_reduced_{name}")
        a_turned = k.sem(f"a_turned_{name}")
        a_saved = k.sem(f"a_saved_{name}")
        a_stored = k.sem(f"a_stored_{name}")
        block = ctx.enter_context(nc.Block(f"project_{name}"))

        def turned(slot):
            at = slot * KB * BANK
            return k.psum[:, at:at + KB * BANK].rearrange("p (b c) -> p b c", b=KB)[:, :, 0:4 * P]

        def halves(x, slot):
            return x[:, slot].rearrange("p (b c) n -> p b (c n)", b=KB)

        def h_bank(slot, m):
            at = (2 * KB + slot * MB + m) * BANK
            return k.psum[0:P, at:at + BANK]

        a_bank = k.psum[0:H, 7 * BANK:7 * BANK + P]

        @block.sync
        def _(sp):
            if relu:
                sp.dma_start(bias_rows[:], row_bias.rearrange("(o c) -> o c", o=1).to_broadcast([P, K * 128])
                             ).then_inc(bias_loaded, 16)

            def step(s):
                if not s.live():
                    return
                wait_item(sp, x_turned, s, ago=2)
                sp.dma_start(x_rows[:, s.slot], rows[bass.ds(s.item * P, P), :]).then_inc(x_loaded[s.slot], 16)
                if s.first():
                    for c in range(K):
                        sp.dma_start(w_f32[:, c], w[c * 128:(c + 1) * 128, :]).then_inc(w_loaded[c], 16)
                    for i, v in enumerate((att_src, att_dst)):
                        sp.dma_start(att[:, i], v.rearrange("(o h) c -> o (h c)", o=1).to_broadcast([P, M])
                                     ).then_inc(att_loaded, 16)

            run_steps(sp, T, 0, step)
            sp.wait_ge(a_saved, T)
            sp.dma_start(a_src_rows, a_src_t[:]).then_inc(a_stored, 16)
            sp.wait_ge(a_stored, 16)

        @block.tensor
        def _(pe):
            def step(s):
                if s.live():
                    if relu:
                        wait_item(pe, x_biased, s)
                    else:
                        wait_loaded(pe, x_loaded, s)
                    wait_item(pe, x_low_done, s, ago=2)
                    for c in range(K):
                        block_t = pe.transpose(turned(s.slot)[:, c // 4, (c % 4) * P:(c % 4 + 1) * P],
                                               x_rows[:, s.slot, c * 128:(c + 1) * 128], k.ident[0:P, 0:P])
                    block_t.then_inc(x_turned, 1)
                s = s.back(1)
                if s.live():
                    if s.first():
                        pe.wait_ge(w_low_done, K)
                    wait_item(pe, x_low_done, s)
                    wait_item(pe, h_saved, s, ago=2)
                    for m in range(MB):
                        cols = slice(m * BANK, (m + 1) * BANK)
                        for c in range(K):
                            for i, (x, v) in enumerate(((x_high, w_high), (x_high, w_low), (x_low, w_high))):
                                product = pe.matmul(h_bank(s.slot, m), x[:, s.slot, c], v[:, c, cols],
                                                    start=c == 0 and i == 0, stop=c == K - 1 and i == 2)
                    product.then_inc(h_summed, 1)
                s = s.back(2)
                if s.live():
                    wait_item(pe, a_reduced, s)
                    wait_item(pe, a_saved, s, ago=1)
                    pe.transpose(a_bank, a_src[:, s.slot], k.ident[0:P, 0:P]).then_inc(a_turned, 1)

            run_steps(pe, T, 3, step)

        @block.scalar
        def _(act):
            for c in range(K):
                act.wait_ge(w_loaded[c], 16)
                act.copy(w_high[:, c], w_f32[:, c]).then_inc(w_high_done, 1)

            def step(s):
                if s.live():
                    wait_item(act, x_turned, s)
                    wait_item(act, h_summed, s, ago=2)
                    act.activation(halves(x_high, s.slot), turned(s.slot), ACT.Relu if relu else ACT.Copy).then_inc(x_high_done, 1)
                s = s.back(1)
                if s.live():
                    wait_item(act, h_summed, s)
                    for m in range(MB):
                        saved = act.copy(h_sb[:, s.item, m * BANK:(m + 1) * BANK], h_bank(s.slot, m))
                    saved.then_inc(h_saved, 1)

            run_steps(act, T, 1, step)

        @block.gpsimd
        def _(pool):
            if relu:
                pool.wait_ge(bias_loaded, 16)

            def step(s):
                if s.live() and relu:
                    wait_loaded(pool, x_loaded, s)
                    pool.tensor_tensor(x_rows[:, s.slot], x_rows[:, s.slot], bias_rows[:], ALU.add).then_inc(x_biased, 1)
                s = s.back(2)
                if s.live():
                    if s.first():
                        pool.wait_ge(att_loaded, 32)
                    wait_item(pool, h_saved, s)
                    wait_item(pool, a_reduced, s, ago=2)
                    for i in range(2):
                        made = pool.tensor_tensor(h_att[:, s.slot, i], h_sb[:, s.item, :], att[:, i], ALU.mult)
                    made.then_inc(att_multiplied, 1)

            run_steps(pool, T, 2, step)

        @block.vector
        def _(dve):
            for c in range(K):
                dve.wait_ge(w_high_done, c + 1)
                dve.tensor_tensor(w_low[:, c], w_f32[:, c], w_high[:, c].bitcast(F32), ALU.subtract).then_inc(w_low_done, 1)

            def step(s):
                if s.live():
                    wait_item(dve, x_high_done, s)
                    if relu:
                        cut = dve.scalar_tensor_tensor(halves(x_low, s.slot), turned(s.slot), 0.0,
                                                       halves(x_high, s.slot).bitcast(F32), ALU.max, ALU.subtract)
                    else:
                        cut = dve.tensor_tensor(halves(x_low, s.slot), turned(s.slot), halves(x_high, s.slot).bitcast(F32),
                                                ALU.subtract)
                    cut.then_inc(x_low_done, 1)
                s = s.back(2)
                if s.live():
                    wait_item(dve, att_multiplied, s)
                    wait_item(dve, a_turned, s, ago=2)
                    for i, a in enumerate((a_src[:, s.slot], a_dst[:, s.item, :])):
                        total = dve.tensor_reduce(a, h_att[:, s.slot, i].rearrange("p (h c) -> p h c", h=H), AX_X, ALU.add)
                    total.then_inc(a_reduced, 1)
                s = s.back(1)
                if s.live():
                    wait_item(dve, a_turned, s)
                    dve.tensor_copy(a_src_t[:, bass.ds(s.item * P, P)], a_bank).then_inc(a_saved, 1)

            run_steps(dve, T, 3, step)


def stage_gat_attend(k, name, h_sb, a_dst, a_src_rows, out_rows):
    nc, P, T, N, H = k.nc, k.P, k.T, k.N, k.H
    CH = h_sb.shape[2] // H
    B = T // 2
    HALF = BANK // 2
    with k.stage("stage_gat_attend") as ctx:
        def sb(what, shape, dt=F32):
            return ctx.enter_context(nc.sbuf_tensor(f"{what}_{name}", shape, dt))

        a_src = sb("a_src_all", [P, H, N])
        probs = sb("probs", [P, B, N])
        base = sb("base", [P, 2, N])
        minus_a_dst = sb("minus_a_dst", [P, T, H])
        probs_t = sb("probs_t", [P, B, T, P])
        neg_max, sums, sums_safe, inverse = (sb(what, [P, T]) for what in ("neg_max", "sums", "sums_safe", "inverse"))
        final = sb("final", [P, 2, T // 2, CH])
        a_loaded = k.sem(f"a_loaded_{name}")
        a_rest_loaded = k.sem(f"a_rest_loaded_{name}")
        ramp_done = k.sem(f"ramp_done_{name}")
        negated = k.sem(f"negated_{name}")
        base_free = k.sem(f"base_free_{name}")
        base_done = k.sem(f"base_done_{name}")
        masked = k.sem(f"masked_{name}")
        exp_done = k.sem(f"exp_done_{name}")
        sum_safe = k.sem(f"sum_safe_{name}")
        inverted = k.sem(f"inverted_{name}")
        probs_turned = k.sem(f"probs_turned_{name}")
        probs_saved = k.sem(f"probs_saved_{name}")
        summed = k.sem(f"summed_{name}")
        final_done = k.sem(f"final_done_{name}")
        stored = [k.sem(f"stored{i}_{name}") for i in range(2)]
        block = ctx.enter_context(nc.Block(f"attend_{name}"))

        def turned(u):
            at = (u % 2) * 3 * BANK
            return k.psum[0:P, at:at + T // 2 * HALF].rearrange("p (b c) -> p b c", c=HALF)[:, :, 0:2 * P]

        def out_bank(u):
            at = (6 + u % 2) * BANK
            return k.psum[0:P, at:at + CH]

        @block.sync
        def _(sp):
            for h in range(H):
                sp.dma_start(a_src[:, h], a_src_rows[h:h + 1, :].to_broadcast([P, N])
                             ).then_inc(a_rest_loaded if h else a_loaded, 16)

            def step(n):
                if n.live() and n.tile % B == B - 1:
                    half = n.tile // B
                    wait_unit(sp, final_done, n)
                    sp.dma_start(out_rows.rearrange("(t p) m -> p t m", p=P)[:, half * B:(half + 1) * B, bass.ds(n.head * CH, CH)],
                                 final[:, half]).then_inc(stored[half], 16)

            run_units(sp, H, T, step)
            for half in range(2):
                sp.wait_ge(stored[half], 16 * H)

        @block.scalar
        def _(act):
            act.preload_act_table_set(EXP_LN)

            def step(n):
                if n.live():
                    wait_unit(act, masked, n)
                    act.activation(probs[:, n.tile % B], probs[:, n.tile % B], ACT.Exp, scale=-1.0,
                                   bias=neg_max[:, n.tile:n.tile + 1],
                                   accum_out=sums[:, n.tile:n.tile + 1]).then_inc(exp_done, 1)
                n = n.shift(-1)
                if n.live():
                    wait_unit(act, probs_turned, n)
                    wait_unit(act, summed, n, ago=B)
                    act.copy(probs_t[:, n.tile % B].rearrange("p (b c) n -> p b (c n)", c=2), turned(n.tile)
                             ).then_inc(probs_saved, 1)
                n = n.shift(-2)
                if n.live():
                    wait_unit(act, summed, n)
                    wait_unit(act, inverted, n)
                    half, t = n.tile // B, n.tile % B
                    if t == 0 and not (isinstance(n.head, int) and n.head == 0):
                        act.wait_ge(stored[half], n.head * 16)
                    act.activation(final[:, half, t], out_bank(n.tile), ACT.Copy,
                                   scale=inverse[:, n.tile:n.tile + 1]).then_inc(final_done, 1)

            run_units(act, H, T, step)

        @block.vector
        def _(dve):
            dve.tensor_scalar(minus_a_dst[:], a_dst[:], -1.0, None, ALU.mult).then_inc(negated, 1)
            dve.wait_ge(negated, 1)

            def ramp(n):
                if n.live():
                    if n.starts(0):
                        dve.wait_ge(a_loaded, 16)
                    if n.starts(1):
                        dve.wait_ge(a_rest_loaded, 16 * (H - 1))
                    wait_unit(dve, probs_turned, n, ago=B)
                    dve.tensor_scalar(probs[:, n.tile % B], a_src[:, n.head, :], minus_a_dst[:, n.tile, bass.ds(n.head, 1)],
                                      GAIN - 1, ALU.max, ALU.mult).then_inc(ramp_done, 1)

            def wait_mask(n):
                if n.live():
                    wait_unit(dve, base_done, n)
                    wait_unit(dve, ramp_done, n)

            def mask(n):
                if n.live():
                    dve.tensor_tensor_reduce(probs[:, n.tile % B], probs[:, n.tile % B], base[:, n.tile % 2],
                                             -NEG_SLOPE, -FLOOR, ALU.add, ALU.min,
                                             neg_max[:, n.tile:n.tile + 1]).then_inc(masked, 1)

            def step(n):
                ramp(n.shift(2))
                wait_mask(n.shift(1))
                last = n.shift(-1)
                if last.live():
                    wait_unit(dve, exp_done, last)
                    dve.tensor_scalar(sums_safe[:, last.tile:last.tile + 1], sums[:, last.tile:last.tile + 1],
                                      TINY, None, ALU.add).then_inc(sum_safe, 1)
                mask(n.shift(1))
                n = last
                if n.live():
                    wait_unit(dve, sum_safe, n)
                    dve.reciprocal(inverse[:, n.tile:n.tile + 1], sums_safe[:, n.tile:n.tile + 1]
                                   ).then_inc(inverted, 1)

            for u in range(2):
                ramp(Unit(0, u, H, T))
            wait_mask(Unit(0, 0, H, T))
            mask(Unit(0, 0, H, T))
            run_units(dve, H, T, step)

        @block.tensor
        def _(pe):
            def step(n):
                if n.live():
                    wait_unit(pe, exp_done, n)
                    wait_unit(pe, probs_saved, n, ago=2)
                    for i in range(T):
                        block_t = pe.transpose(turned(n.tile)[:, i // 2, (i % 2) * P:(i % 2 + 1) * P],
                                               probs[:, n.tile % B, i * P:(i + 1) * P], k.ident[0:P, 0:P])
                    block_t.then_inc(probs_turned, 1)
                n = n.shift(-2)
                if n.live():
                    wait_unit(pe, probs_saved, n)
                    wait_unit(pe, final_done, n, ago=2)
                    for i in range(T):
                        total = pe.matmul(out_bank(n.tile), probs_t[:, n.tile % B, i],
                                          h_sb[:, i, bass.ds(n.head * CH, CH)], start=i == 0, stop=i == T - 1)
                    total.then_inc(summed, 1)

            run_units(pe, H, T, step)

        @block.gpsimd
        def _(pool):
            def step(n):
                if n.live():
                    if isinstance(n.head, int) and n.head == 0:
                        pool.wait_ge(a_loaded, 16)
                    else:
                        pool.wait_ge(a_rest_loaded, 16 * (H - 1))
                    wait_unit(pool, masked, n, ago=2)
                    pool.sem_inc(base_free, 1)
                    pool.tensor_tensor(base[:, n.tile % 2], k.log_counts[:, n.tile, :], a_src[:, n.head, :], ALU.add
                                       ).then_inc(base_done, 1)

            run_units(pool, H, T, step)


def stage_gat_finish(k, gat_rows, bias, x, x_rows, x_cols):
    nc, P, T, N, D = k.nc, k.P, k.T, k.N, k.D
    C = D // 128
    with k.stage("stage_gat_finish") as ctx:
        def sb(what, shape, dt=F32):
            return ctx.enter_context(nc.sbuf_tensor(f"{what}_gf", shape, dt))

        g = sb("g", [P, T, D])
        y = sb("y", [P, T, D])
        e = sb("e", [P, 2, D])
        normal = sb("normal", [P, T, D])
        cols = sb("cols", [128, C, N])
        neg_max, sums, shift = sb("neg_max", [P, T]), sb("sums", [P, T]), sb("shift", [P, T])
        logs = sb("logs", [P, T])
        stats = sb("stats", [P, T, 6])
        moments = sb("moments", [P, T, 2])
        spread, deviation, inverse = sb("spread", [P, T]), sb("deviation", [P, T]), sb("inverse", [P, T])
        bias_rows = sb("bias_rows", [P, D])
        bias_loaded, g_biased, mask_scaled = k.sem("bias_loaded_gf"), k.sem("g_biased_gf"), k.sem("mask_scaled_gf")
        max_done, exp_done, logs_done = k.sem("max_done_gf"), k.sem("exp_done_gf"), k.sem("logs_done_gf")
        shift_done, added, stats_done = k.sem("shift_done_gf"), k.sem("added_gf"), k.sem("stats_done_gf")
        moments_done, spread_done = k.sem("moments_done_gf"), k.sem("spread_done_gf")
        deviation_done, inverse_done = k.sem("deviation_done_gf"), k.sem("inverse_done_gf")
        normed, turned, cols_saved, stored = k.sem("normed_gf"), k.sem("turned_gf"), k.sem("cols_saved_gf"), k.sem("stored_gf")
        PARTS = 5
        g_loaded = [k.sem(f"g_loaded{i}_gf") for i in range(PARTS)]
        x_loaded = k.sem("x_loaded_gf")
        block = ctx.enter_context(nc.Block("gat_finish"))

        def bank(slot):
            return k.psum[:, slot * BANK:slot * BANK + C * P]

        @block.sync
        def _(sp):
            sp.dma_start(bias_rows[:], bias.rearrange("(o c) -> o c", o=1).to_broadcast([P, D])).then_inc(bias_loaded, 16)
            for i in range(PARTS):
                tiles = slice(i * T // PARTS, (i + 1) * T // PARTS)
                sp.dma_start(g[:, tiles], gat_rows.rearrange("(t p) d -> p t d", p=P)[:, tiles]).then_inc(g_loaded[i], 16)
            sp.dma_start(y[:], x.rearrange("(t p) d -> p t d", p=P)).then_inc(x_loaded, 16)
            with sp.Fori(0, T) as t:
                sp.wait_ge(normed, t + 1)
                sp.dma_start(x_rows[bass.ds(t * P, P), :], normal[:, t, :]).then_inc(stored, 16)
            for half in range(2):
                tiles = T // 2 * (half + 1)
                nodes = slice(half * N // 2, (half + 1) * N // 2)
                sp.wait_ge(cols_saved, tiles)
                sp.dma_start(x_cols.rearrange("(c p) n -> p c n", p=128)[:, :, nodes], cols[:, :, nodes]).then_inc(stored, 16)
            sp.wait_ge(stored, 16 * (T + 2))

        @block.gpsimd
        def _(pool):
            pool.wait_ge(bias_loaded, 16)
            for t in range(T):
                pool.wait_ge(g_loaded[t * PARTS // T], 16)
                pool.tensor_tensor(g[:, t], g[:, t], bias_rows[:], ALU.add).then_inc(g_biased, 1)

        @block.vector
        def _(dve):
            for t in range(T):
                dve.tensor_scalar(k.log_counts[:, t], k.log_counts[:, t], NEG_SLOPE, None, ALU.mult).then_inc(mask_scaled, 1)
                dve.wait_ge(g_biased, t + 1)
                dve.tensor_reduce(neg_max[:, t:t + 1], g[:, t], AX_X, ALU.max, negate=True).then_inc(max_done, 1)
                dve.wait_ge(mask_scaled, t + 1)
                dve.tensor_copy(k.log_counts[:, t, t * P:(t + 1) * P], k.plain_diag[:, t])
            dve.wait_ge(logs_done, 1)
            dve.wait_ge(max_done, T)
            dve.tensor_tensor(shift[:], neg_max[:], logs[:], ALU.subtract).then_inc(shift_done, 1)
            dve.wait_ge(shift_done, 1)
            dve.wait_ge(x_loaded, 16)

            def add(s):
                if s.live():
                    dve.scalar_tensor_tensor(y[:, s.item, :], g[:, s.item, :], shift[:, bass.ds(s.item, 1)], y[:, s.item, :],
                                             ALU.add, ALU.add).then_inc(added, 1)
                s = s.back(1)
                if s.live():
                    wait_item(dve, added, s)
                    dve.bn_stats(stats[:, s.item, :], y[:, s.item, :]).then_inc(stats_done, 1)

            run_steps(dve, T, 1, add)
            dve.wait_ge(stats_done, T)
            for t in range(T):
                dve.bn_aggr(moments[:, t], stats[:, t]).then_inc(moments_done, 1)
            dve.wait_ge(moments_done, T)
            dve.tensor_scalar(spread[:], moments[:, :, 1], EPS, None, ALU.add).then_inc(spread_done, 1)
            dve.wait_ge(deviation_done, 1)
            dve.reciprocal(inverse[:], deviation[:]).then_inc(inverse_done, 1)
            dve.wait_ge(inverse_done, 1)
            for t in range(T):
                dve.tensor_scalar(normal[:, t], y[:, t], moments[:, t, 0:1], inverse[:, t:t + 1], ALU.subtract, ALU.mult
                                  ).then_inc(normed, 1)

        @block.scalar
        def _(act):
            act.preload_act_table_set(EXP_LN)

            def softmax(s):
                wait_item(act, max_done, s)
                wait_item(act, exp_done, s, ago=2)
                act.activation(e[:, s.slot], g[:, s.item, :], ACT.Exp, bias=neg_max[:, bass.ds(s.item, 1)],
                               accum_out=sums[:, bass.ds(s.item, 1)]).then_inc(exp_done, 1)

            run_steps(act, T, 0, softmax)
            act.wait_ge(exp_done, T)
            act.activation(logs[:], sums[:], ACT.Ln).then_inc(logs_done, 1)
            act.preload_act_table_set("sqrt_and_others")
            act.wait_ge(spread_done, 1)
            act.activation(deviation[:], spread[:], ACT.Sqrt).then_inc(deviation_done, 1)

            def save(s):
                wait_item(act, turned, s)
                act.copy(cols[:, :, bass.ds(s.item * P, P)], bank(s.slot).rearrange("p (c n) -> p c n", n=P)
                         ).then_inc(cols_saved, 1)

            run_steps(act, T, 0, save)

        @block.tensor
        def _(pe):
            for t in range(T):
                pe.wait_ge(normed, t + 1)
                if t >= 2:
                    pe.wait_ge(cols_saved, t - 1)
                for c in range(C):
                    block_t = pe.transpose(bank(t % 2)[:, c * P:(c + 1) * P], normal[:, t, c * 128:(c + 1) * 128],
                                           k.ident[0:P, 0:P])
                block_t.then_inc(turned, 1)


def weight_rows(k, ctx, name, weights):
    parts = [(w, o) for w in weights for o in range(w.shape[0] // 128)]
    rows = ctx.enter_context(k.nc.sbuf_tensor(f"w_rows_{name}", [128, len(parts), max(w.shape[1] for w in weights)], F32))
    return rows, [(rows[:, j, 0:w.shape[1]], w[o * 128:(o + 1) * 128, :]) for j, (w, o) in enumerate(parts)]


def stage_turn_weights(k, name, rows, loads, jobs):
    nc = k.nc
    parts = [(w, high, low, o) for w, high, low in jobs for o in range(w.shape[0] // 128)]
    total = len(parts)
    assert total % 2 == 0
    with k.stage("stage_turn_weights") as ctx:
        loaded = [k.sem(f"w_rows_loaded{i}_{name}") for i in range(2)]
        turned, high_done, low_done = (k.sem(f"w_{what}_{name}") for what in ("turned", "high_done", "low_done"))
        block = ctx.enter_context(nc.Block(f"weights_{name}"))

        def bank(j, width):
            return k.psum[:, (j % 4) * BANK:(j % 4) * BANK + width]

        def part_of(j, half):
            w, high, low, o = parts[j]
            return (low if half else high)[:, :, o * 128:(o + 1) * 128]

        def blocks(j, width):
            return bank(j, width).rearrange("p (c o) -> p c o", o=128)

        @block.sync
        def _(sp):
            for j, (buffer, source) in enumerate(loads):
                sp.dma_start(buffer, source).then_inc(loaded[j * 2 // total], 16)

        @block.tensor
        def _(pe):
            for j, (w, _, _, o) in enumerate(parts):
                if loads and j * 2 % total == 0:
                    pe.wait_ge(loaded[j * 2 // total], 8 * total)
                if j >= 4:
                    pe.wait_ge(low_done, j - 3)
                for c in range(w.shape[1] // 128):
                    block_t = pe.transpose(bank(j, w.shape[1])[:, c * 128:(c + 1) * 128],
                                           rows[:, j, c * 128:(c + 1) * 128], k.ident[:])
                block_t.then_inc(turned, 1)

        @block.scalar
        def _(act):
            for j, (w, _, _, o) in enumerate(parts):
                act.wait_ge(turned, j + 1)
                act.copy(part_of(j, 0), blocks(j, w.shape[1])).then_inc(high_done, 1)

        @block.vector
        def _(dve):
            for j, (w, _, _, o) in enumerate(parts):
                dve.wait_ge(high_done, j + 1)
                dve.tensor_tensor(part_of(j, 1), blocks(j, w.shape[1]), part_of(j, 0).bitcast(F32), ALU.subtract
                                  ).then_inc(low_done, 1)


def halves(nc, ctx, name, ins, outs):
    return [ctx.enter_context(nc.sbuf_tensor(f"{name}_{half}", [128, ins, outs], F32R)) for half in ("high", "low")]


def three_passes(pe, out, x_high, x_low, w_high, w_low, first, last):
    pe.matmul(out, w_high, x_high, start=first, stop=False)
    pe.matmul(out, w_high, x_low, start=False, stop=False)
    return pe.matmul(out, w_low, x_high, start=False, stop=last)


def stage_qkv(k, x_cols, wq, wk, wv, bq, q_halves, k_halves, v_rows):
    nc, P, T, N, D, H = k.nc, k.P, k.T, k.N, k.D, k.H
    C, CH = D // 128, D // H
    W, CHUNKS = 2 * P, T // 2
    SCALE = float(CH) ** -0.5
    with k.stage("stage_qkv") as ctx:
        def sb(what, shape, dt=F32):
            return ctx.enter_context(nc.sbuf_tensor(f"{what}_qkv", shape, dt))

        x = sb("x", [128, 2, C, W])
        x_high, x_low = sb("x_high", [128, 2, C, W], F32R), sb("x_low", [128, 2, C, W], F32R)
        q = sb("q", [128, C, W])
        q_out = sb("q_out", [128, 2, C, W], F32R)
        k_low = sb("k_low", [128, 2, C, W], F32R)
        bias, scaled_bias = sb("bias", [128, C]), sb("scaled_bias", [128, C])
        bias_loaded, bias_scaled, high_done, low_done, q_summed, k_summed, v_summed, q_saved, q_high_done, \
            q_low_done, q_stored, k_high_done, k_low_done, v_saved = (
                k.sem(f"{what}_qkv") for what in ("bias_loaded", "bias_scaled", "high_done", "low_done", "q_summed",
                                                  "k_summed", "v_summed", "q_saved", "q_high_done", "q_low_done",
                                                  "q_stored", "k_high_done", "k_low_done", "v_saved"))
        x_loaded, k_stored = ([k.sem(f"{what}{slot}_qkv") for slot in range(2)] for what in ("x_loaded", "k_stored"))
        block = ctx.enter_context(nc.Block("qkv"))

        def by_feature(i):
            return k.psum[:, i * 2 * BANK:(i + 1) * 2 * BANK].rearrange("p (b c) -> p b c", b=C // 2)[:, :, 0:2 * W].rearrange(
                "p b (c n) -> p b c n", c=2)

        def product(i, o):
            at = (i * 2 + o // 2) * BANK + o % 2 * W
            return k.psum[:, at:at + W]

        def v_bank(t):
            return k.psum[0:P, (4 + t) * BANK:(5 + t) * BANK]

        def like_banks(v):
            return v.rearrange("p (b c) n -> p b c n", c=2)

        def own(odd):
            return slice(odd * CH, (odd + 1) * CH)

        def k_at(rows, odd, s):
            return k_halves[own(rows)].rearrange("p (c odd) n -> p odd c n", odd=2)[:, odd][:, :, bass.ds(s.item * W, W)]

        @block.sync
        def _(sp):
            sp.dma_start(bias[:], bq.rearrange("(c p) -> p c", p=128), allow_slow_non_contiguous=True).then_inc(bias_loaded, 16)

            def step(s):
                nodes = bass.ds(s.item * W, W)
                if s.live():
                    wait_item(sp, low_done, s, ago=2)
                    sp.dma_start(x[:, s.slot], x_cols.rearrange("(c p) n -> p c n", p=128)[:, :, nodes]
                                 ).then_inc(x_loaded[s.slot], 16)
                s = s.back(1)
                if s.live():
                    nodes = bass.ds(s.item * W, W)
                    wait_item(sp, q_low_done, s)
                    for half, part in enumerate((q_out[:, 0], q_out[:, 1])):
                        sp.dma_start(q_halves.rearrange("(c p) half n -> half p c n", p=128)[half][:, :, nodes],
                                     part.bitcast(F32)).then_inc(q_stored, 16)
                    wait_item(sp, k_low_done, s)
                    for odd in range(2):
                        sp.dma_start(k_at(1 - odd, odd, s).bitcast(F32), k_low[own(odd), s.slot].bitcast(F32)
                                     ).then_inc(k_stored[s.slot], 16)

            run_steps(sp, CHUNKS, 1, step)
            sp.wait_ge(q_stored, 32 * CHUNKS)
            sp.wait_ge(k_stored[0], 32 * ((CHUNKS + 1) // 2))
            sp.wait_ge(k_stored[1], 32 * (CHUNKS // 2))

        @block.tensor
        def _(pe):
            def step(s):
                wait_item(pe, low_done, s)
                for i, (w, summed, saved) in enumerate(((wq, q_summed, q_saved), (wk, k_summed, k_low_done))):
                    wait_item(pe, saved, s, ago=1)
                    for o in range(C):
                        for c in range(C):
                            total = three_passes(pe, product(i, o), x_high[:, s.slot, c], x_low[:, s.slot, c],
                                                 w[0][:, c, o * 128:(o + 1) * 128], w[1][:, c, o * 128:(o + 1) * 128],
                                                 c == 0, c == C - 1)
                    total.then_inc(summed, 1)
                wait_item(pe, v_saved, s, ago=1)
                for t in range(2):
                    for c in range(C):
                        xh, xl = (v[:, s.slot, c, t * P:(t + 1) * P] for v in (x_high, x_low))
                        for i, (v, w) in enumerate(((xh, wv[0]), (xh, wv[1]), (xl, wv[0]))):
                            total = pe.matmul(v_bank(t), v, w[:, c, :], start=c == 0 and i == 0, stop=c == C - 1 and i == 2)
                total.then_inc(v_summed, 1)

            run_steps(pe, CHUNKS, 0, step)

        @block.scalar
        def _(act):
            act.wait_ge(bias_scaled, 1)

            def step(s):
                if s.live():
                    wait_loaded(act, x_loaded, s)
                    wait_item(act, v_summed, s, ago=2)
                    act.copy(x_high[:, s.slot], x[:, s.slot]).then_inc(high_done, 1)
                s = s.back(1)
                if s.live():
                    wait_item(act, q_summed, s)
                    wait_item(act, q_low_done, s, ago=1)
                    for o in range(C):
                        saved = act.activation(q[:, o], product(0, o), ACT.Identity,
                                               bias=scaled_bias[:, o:o + 1], scale=SCALE)
                    saved.then_inc(q_saved, 1)
                    wait_item(act, q_saved, s)
                    if not s.first():
                        act.wait_ge(q_stored, s.item * 32)
                    act.copy(q_out[:, 0], q[:]).then_inc(q_high_done, 1)
                    wait_item(act, k_summed, s)
                    for odd in range(2):
                        saved = act.copy(like_banks(k_at(odd, odd, s)), by_feature(1)[own(odd)])
                    saved.then_inc(k_high_done, 1)
                    wait_item(act, v_summed, s)
                    for t in range(2):
                        saved = act.copy(v_rows[:, s.item * 2 + t, :], v_bank(t))
                    saved.then_inc(v_saved, 1)

            run_steps(act, CHUNKS, 1, step)

        @block.vector
        def _(dve):
            dve.wait_ge(bias_loaded, 16)
            dve.tensor_scalar(scaled_bias[:], bias[:], SCALE, None, ALU.mult).then_inc(bias_scaled, 1)

            def step(s):
                if s.live():
                    wait_item(dve, high_done, s)
                    dve.tensor_tensor(x_low[:, s.slot], x[:, s.slot], x_high[:, s.slot].bitcast(F32), ALU.subtract
                                      ).then_inc(low_done, 1)
                s = s.back(1)
                if s.live():
                    wait_item(dve, q_high_done, s)
                    dve.tensor_tensor(q_out[:, 1], q[:], q_out[:, 0].bitcast(F32), ALU.subtract).then_inc(q_low_done, 1)
                    wait_item(dve, k_high_done, s)
                    wait_stored(dve, k_stored, s, 2)
                    for odd in range(2):
                        cut = dve.tensor_tensor(like_banks(k_low[own(odd), s.slot]), by_feature(1)[own(odd)],
                                                like_banks(k_at(odd, odd, s).bitcast(F32)), ALU.subtract)
                    cut.then_inc(k_low_done, 1)

            run_steps(dve, CHUNKS, 1, step)


def stage_attend(k, q_halves, k_halves, v_rows, out_cols, loads):
    nc, P, T, N, D, H = k.nc, k.P, k.T, k.N, k.D, k.H
    CH = D // H
    B = T // 2
    U = 2 * T
    HALF = BANK // 2
    with k.stage("stage_attend") as ctx:
        def sb(what, shape, dt=F32):
            return ctx.enter_context(nc.sbuf_tensor(f"{what}_att", shape, dt))

        q = sb("q", [128, 2, 2, N], F32R)
        probs = sb("probs", [P, B, N])
        probs_t = sb("probs_t", [P, B, T, P])
        neg_max, sums, sums_safe, inverse = (sb(what, [P, U]) for what in ("neg_max", "sums", "sums_safe", "inverse"))
        final = sb("final", [128, 2, B * P])
        v_pair = sb("v_pair", [P, T, 2 * CH])
        q_loaded = [k.sem(f"q_loaded{i}_att") for i in range(2)]
        stored = [k.sem(f"stored{i}_att") for i in range(2)]
        v_copied, v_free, half_summed = (k.sem(f"{what}_att") for what in ("v_copied", "v_free", "half_summed"))
        loaded = k.sem("loaded_att")
        scored, masked, exp_done, sum_safe, inverted, divided, probs_turned, probs_saved, summed, final_done = (
            k.sem(f"{what}_att") for what in ("scored", "masked", "exp_done", "sum_safe", "inverted", "divided",
                                              "probs_turned", "probs_saved", "summed", "final_done"))
        block = ctx.enter_context(nc.Block("attend"))

        scores = k.psum[0:P, 0:N]

        def turned():
            return k.psum[0:P, 3 * BANK:3 * BANK + T // 2 * HALF].rearrange("p (b c) -> p b c", c=HALF)[:, :, 0:2 * P]

        def out_bank(t):
            at = (6 + t % 2) * BANK
            return k.psum[:, at:at + P]

        def tile_of(n):
            return Unit(n.head, n.tile // 2, H // 2, T)

        def column(n):
            return slice(n.tile, n.tile + 1)

        def units(eng, emit):
            run_units(eng, H // 2, U, emit)

        @block.sync
        def _(sp):
            def load(n):
                if n.live():
                    group = n.tile // (2 * B)
                    nodes = slice(group * B * P, (group + 1) * B * P)
                    wait_unit(sp, scored, n, ago=U - 2 * B + 1)
                    for odd in range(2):
                        for copy in range(2):
                            sp.dma_start(q[copy * CH:(copy + 1) * CH, odd, :, nodes].bitcast(F32),
                                         q_halves[bass.ds(n.head * 2 * CH + odd * CH, CH), :, nodes]
                                         ).then_inc(q_loaded[group], 16)

            def store(n):
                if n.live():
                    group = n.tile // (2 * B)
                    wait_unit(sp, final_done, tile_of(n))
                    sp.dma_start(out_cols[bass.ds(n.head * 128, 128), group * B * P:(group + 1) * B * P], final[:, group]
                                 ).then_inc(stored[group], 16)

            def step(n):
                if n.tile % (2 * B) == 3:
                    store(n.shift(-4))
                if n.tile % (2 * B) == 4:
                    load(n.shift(4 * B - 4))

            for group in range(2):
                load(Unit(0, group * 2 * B, H // 2, U))
            for buffer, source in loads:
                sp.dma_start(buffer, source).then_inc(loaded, 16)
            units(sp, step)
            sp.wait_ge(loaded, 16 * len(loads))
            for group in range(2):
                sp.wait_ge(stored[group], 16 * H // 2)

        @block.tensor
        def _(pe):
            def score(n):
                if n.live():
                    t, odd = n.tile // 2, n.tile % 2
                    if t % B == 0 and odd == 0:
                        pe.wait_ge(q_loaded[t // B], (n.head + 1) * 64)
                    wait_unit(pe, masked, n, ago=1)
                    for half in range(2):
                        for a, width in pieces(N):
                            total = pe.matmul(scores[:, a:a + width], q[:, odd, half, t * P:(t + 1) * P],
                                              k_halves[:, n.head * 2 + odd, a:a + width], start=half == 0, stop=half == 1)
                    total.then_inc(scored, 1)

            def weigh(n, part):
                if n.live():
                    tile, both = tile_of(n), (n.shift(-1), n)
                    if tile.tile == 0:
                        pe.wait_ge(v_copied, n.head * 2 + part + 1)
                    if part == 0:
                        wait_unit(pe, probs_saved, n)
                        wait_unit(pe, final_done, tile, ago=2)
                    for i in range(part * B, (part + 1) * B):
                        for odd, m in enumerate(both):
                            total = pe.matmul(out_bank(tile.tile)[odd * CH:(odd + 1) * CH],
                                              v_pair[:, i, odd * CH:(odd + 1) * CH],
                                              probs_t[:, m.tile % B, i], start=i == 0, stop=i == T - 1)
                    total.then_inc((half_summed, summed)[part], 1)

            def step(n):
                if n.live():
                    wait_unit(pe, divided, n)
                    wait_unit(pe, probs_saved, n, ago=1)
                    for i in range(T):
                        block_t = pe.transpose(turned()[:, i // 2, (i % 2) * P:(i % 2 + 1) * P],
                                               probs[:, n.tile % B, i * P:(i + 1) * P], k.ident[0:P, 0:P])
                    block_t.then_inc(probs_turned, 1)
                if n.tile % 2:
                    weigh(n.shift(-2), 0)
                else:
                    weigh(n.shift(-3), 1)
                score(n.shift(3))

            for u in range(3):
                score(Unit(0, u, H // 2, U))
            units(pe, step)

        @block.scalar
        def _(act):
            act.preload_act_table_set(EXP_LN)

            def exponential(n):
                if n.live():
                    wait_unit(act, masked, n)
                    act.activation(probs[:, n.tile % B], probs[:, n.tile % B], ACT.Exp, scale=-1.0,
                                   bias=neg_max[:, column(n)], accum_out=sums[:, column(n)]).then_inc(exp_done, 1)

            def step(n):
                if n.live():
                    wait_unit(act, probs_turned, n)
                    if n.shift(-B).live():
                        wait_unit(act, summed, tile_of(n.shift(-B)))
                    act.copy(probs_t[:, n.tile % B].rearrange("p (b c) n -> p b (c n)", c=2), turned()
                             ).then_inc(probs_saved, 1)
                exponential(n.shift(2))
                if n.tile % 2 == 0 and n.shift(-5).live():
                    tile = tile_of(n.shift(-5))
                    group, t = tile.tile // B, tile.tile % B
                    wait_unit(act, summed, tile)
                    if t == 0 and not (isinstance(tile.head, int) and tile.head == 0):
                        act.wait_ge(stored[group], tile.head * 16)
                    act.copy(final[:, group, t * P:(t + 1) * P], out_bank(tile.tile)).then_inc(final_done, 1)

            for u in range(2):
                exponential(Unit(0, u, H // 2, U))
            units(act, step)

        @block.vector
        def _(dve):
            def wait_mask(n):
                if n.live():
                    wait_unit(dve, scored, n)
                    wait_unit(dve, probs_turned, n, ago=B)

            def mask(n):
                if n.live():
                    dve.tensor_tensor_reduce(probs[:, n.tile % B], scores, k.log_counts[:, n.tile // 2, :],
                                             -1.0, -FLOOR, ALU.add, ALU.min, neg_max[:, column(n)]).then_inc(masked, 1)

            def safe(n):
                if n.live():
                    wait_unit(dve, exp_done, n)
                    dve.tensor_scalar(sums_safe[:, column(n)], sums[:, column(n)], TINY, None, ALU.add).then_inc(sum_safe, 1)

            def divide(n):
                if n.live():
                    wait_unit(dve, sum_safe, n)
                    dve.reciprocal(inverse[:, column(n)], sums_safe[:, column(n)]).then_inc(inverted, 1)
                    wait_unit(dve, inverted, n)
                    dve.tensor_scalar(probs[:, n.tile % B], probs[:, n.tile % B], inverse[:, column(n)], None, ALU.mult
                                      ).then_inc(divided, 1)

            def step(n):
                wait_mask(n.shift(2))
                safe(n.shift(1))
                mask(n.shift(2))
                divide(n.shift(1))

            for u in range(2):
                wait_mask(Unit(0, u, H // 2, U))
                mask(Unit(0, u, H // 2, U))
            safe(Unit(0, 0, H // 2, U))
            divide(Unit(0, 0, H // 2, U))
            units(dve, step)

        @block.gpsimd
        def _(pool):
            def copy_v(pair, part):
                sources = slice(part * B, (part + 1) * B)
                pool.tensor_copy(v_pair[:, sources], v_rows[:, sources, bass.ds(pair * 2 * CH, 2 * CH)]).then_inc(v_copied, 1)

            for part in range(2):
                copy_v(0, part)
            with pool.Fori(1, H // 2) as pair:
                for part, done in enumerate((half_summed, summed)):
                    pool.wait_ge(done, pair * T)
                    pool.sem_inc(v_free, 1)
                    copy_v(pair, part)


def stage_out(k, a_cols, x_cols, w, bo, y, stats):
    nc, P, T, D = k.nc, k.P, k.T, k.D
    C = D // 128
    W, CHUNKS = 2 * P, T // 2
    with k.stage("stage_out") as ctx:
        def sb(what, shape, dt=F32):
            return ctx.enter_context(nc.sbuf_tensor(f"{what}_out", shape, dt))

        a = sb("a", [128, 2, C, W])
        a_high, a_low = sb("a_high", [128, 2, C, W], F32R), sb("a_low", [128, 2, C, W], F32R)
        bias = sb("bias", [128, C])
        bias_loaded, x_loaded, high_done, low_done, summed, added = (
            k.sem(f"{what}_out") for what in ("bias_loaded", "x_loaded", "high_done", "low_done",
                                              "summed", "added"))
        a_loaded = [k.sem(f"a_loaded{slot}_out") for slot in range(2)]
        block = ctx.enter_context(nc.Block("out"))

        def result(slot, c):
            at = (slot * 2 + c // 2) * BANK + c % 2 * W
            return k.psum[:, at:at + W]

        @block.sync
        def _(sp):
            sp.dma_start(bias[:], bo.rearrange("(c p) -> p c", p=128), allow_slow_non_contiguous=True).then_inc(bias_loaded, 16)

            def step(s):
                wait_item(sp, low_done, s, ago=2)
                sp.dma_start(a[:, s.slot], a_cols.rearrange("(c p) n -> p c n", p=128)[:, :, bass.ds(s.item * W, W)]
                             ).then_inc(a_loaded[s.slot], 16)
                if s.item == 1:
                    sp.dma_start(y[:], x_cols.rearrange("(c p) n -> p c n", p=128)).then_inc(x_loaded, 16)

            run_steps(sp, CHUNKS, 0, step)

        @block.tensor
        def _(pe):
            def step(s):
                wait_item(pe, low_done, s)
                wait_item(pe, added, s, ago=2)
                for o in range(C):
                    for c in range(C):
                        total = three_passes(pe, result(s.slot, o), a_high[:, s.slot, c], a_low[:, s.slot, c],
                                             w[0][:, c, o * 128:(o + 1) * 128], w[1][:, c, o * 128:(o + 1) * 128],
                                             c == 0, c == C - 1)
                total.then_inc(summed, 1)

            run_steps(pe, CHUNKS, 0, step)

        @block.scalar
        def _(act):
            def step(s):
                wait_loaded(act, a_loaded, s)
                wait_item(act, summed, s, ago=2)
                act.copy(a_high[:, s.slot], a[:, s.slot]).then_inc(high_done, 1)

            run_steps(act, CHUNKS, 0, step)

        @block.vector
        def _(dve):
            dve.wait_ge(bias_loaded, 16)

            def step(s):
                if s.live():
                    wait_item(dve, high_done, s)
                    dve.tensor_tensor(a_low[:, s.slot], a[:, s.slot], a_high[:, s.slot].bitcast(F32), ALU.subtract).then_inc(low_done, 1)
                last = s.back(3)
                if last.live():
                    wait_item(dve, added, last)
                    for c in range(C):
                        dve.bn_stats(stats[:, c, last.item, :], y[:, c, bass.ds(last.item * W, W)])
                s = s.back(2)
                if s.live():
                    if s.first():
                        dve.wait_ge(x_loaded, 16)
                    wait_item(dve, summed, s)
                    for c in range(C):
                        cols = y[:, c, bass.ds(s.item * W, W)]
                        made = dve.scalar_tensor_tensor(cols, result(s.slot, c), bias[:, c:c + 1], cols, ALU.add, ALU.add)
                    made.then_inc(added, 1)

            run_steps(dve, CHUNKS, 3, step)


def stage_feed_forward(k, w1, b1, w2, b2, y, stats):
    nc, P, T, D = k.nc, k.P, k.T, k.D
    C, F = D // 128, b1.shape[0] // 128
    W, CHUNKS = 2 * P, T // 2
    with k.stage("stage_feed_forward") as ctx:
        def sb(what, shape, dt=F32):
            return ctx.enter_context(nc.sbuf_tensor(f"{what}_ff", shape, dt))

        x_high, x_low = sb("x_high", [128, 2, C, W], F32R), sb("x_low", [128, 2, C, W], F32R)
        f, f_high, f_low = sb("f", [128, F, W]), sb("f_high", [128, 2, F, W], F32R), sb("f_low", [128, 2, F, W], F32R)
        bias1, bias2 = sb("bias1", [128, F]), sb("bias2", [128, C])
        bias_loaded, x_high_done, x_low_done, f_summed, f_saved, f_high_done, f_low_done, summed, added = (
            k.sem(f"{what}_ff") for what in ("bias_loaded", "x_high_done", "x_low_done", "f_summed",
                                             "f_saved", "f_high_done", "f_low_done", "summed", "added"))
        block = ctx.enter_context(nc.Block("feed_forward"))

        def hidden(slot, c):
            return k.psum[:, slot * BANK + c * W:slot * BANK + (c + 1) * W]

        def result(slot, c):
            at = (4 + slot * 2 + c // 2) * BANK + c % 2 * W
            return k.psum[:, at:at + W]

        @block.sync
        def _(sp):
            sp.dma_start(bias1[:], b1.rearrange("(c p) -> p c", p=128), allow_slow_non_contiguous=True).then_inc(bias_loaded, 16)
            sp.dma_start(bias2[:], b2.rearrange("(c p) -> p c", p=128), allow_slow_non_contiguous=True).then_inc(bias_loaded, 16)

        @block.tensor
        def _(pe):
            def step(s):
                if s.live():
                    wait_item(pe, x_low_done, s)
                    wait_item(pe, f_saved, s, ago=2)
                    for o in range(F):
                        for c in range(C):
                            total = three_passes(pe, hidden(s.slot, o), x_high[:, s.slot, c], x_low[:, s.slot, c],
                                                 w1[0][:, c, o * 128:(o + 1) * 128], w1[1][:, c, o * 128:(o + 1) * 128],
                                                 c == 0, c == C - 1)
                    total.then_inc(f_summed, 1)
                s = s.back(1)
                if s.live():
                    wait_item(pe, f_low_done, s)
                    wait_item(pe, added, s, ago=2)
                    for o in range(C):
                        for c in range(F):
                            total = three_passes(pe, result(s.slot, o), f_high[:, s.slot, c], f_low[:, s.slot, c],
                                                 w2[0][:, c, o * 128:(o + 1) * 128], w2[1][:, c, o * 128:(o + 1) * 128],
                                                 c == 0, c == F - 1)
                    total.then_inc(summed, 1)

            run_steps(pe, CHUNKS, 1, step)

        @block.scalar
        def _(act):
            act.wait_ge(bias_loaded, 32)

            def step(s):
                if s.live():
                    wait_item(act, f_summed, s, ago=2)
                    act.copy(x_high[:, s.slot], y[:, :, bass.ds(s.item * W, W)]).then_inc(x_high_done, 1)
                s = s.back(1)
                if s.live():
                    wait_item(act, f_summed, s)
                    wait_item(act, f_low_done, s, ago=1)
                    for c in range(F):
                        saved = act.activation(f[:, c], hidden(s.slot, c), ACT.Relu, bias=bias1[:, c:c + 1])
                    saved.then_inc(f_saved, 1)
                    wait_item(act, f_saved, s)
                    wait_item(act, summed, s, ago=2)
                    act.copy(f_high[:, s.slot], f[:]).then_inc(f_high_done, 1)

            run_steps(act, CHUNKS, 1, step)

        @block.vector
        def _(dve):
            dve.wait_ge(bias_loaded, 32)

            def step(s):
                if s.live():
                    wait_item(dve, x_high_done, s)
                    dve.tensor_tensor(x_low[:, s.slot], y[:, :, bass.ds(s.item * W, W)], x_high[:, s.slot].bitcast(F32),
                                      ALU.subtract).then_inc(x_low_done, 1)
                s = s.back(1)
                if s.live():
                    wait_item(dve, f_high_done, s)
                    dve.tensor_tensor(f_low[:, s.slot], f[:], f_high[:, s.slot].bitcast(F32), ALU.subtract
                                      ).then_inc(f_low_done, 1)
                last = s.back(2)
                if last.live():
                    wait_item(dve, added, last)
                    for c in range(C):
                        dve.bn_stats(stats[:, c, last.item, :], y[:, c, bass.ds(last.item * W, W)])
                s = s.back(1)
                if s.live():
                    wait_item(dve, summed, s)
                    for c in range(C):
                        cols = y[:, c, bass.ds(s.item * W, W)]
                        made = dve.scalar_tensor_tensor(cols, result(s.slot, c), bias2[:, c:c + 1], cols, ALU.add, ALU.add)
                    made.then_inc(added, 1)

            run_steps(dve, CHUNKS, 3, step)


def stage_batch_norm(k, name, gamma, beta, stats, y, x_cols):
    nc, D = k.nc, k.D
    C = D // 128
    with k.stage("stage_batch_norm") as ctx:
        def sb(what, shape, dt=F32):
            return ctx.enter_context(nc.sbuf_tensor(f"{what}_{name}", shape, dt))

        g, b = sb("g", [128, C]), sb("b", [128, C])
        moments = sb("moments", [128, C, 2])
        spread, deviation, inverse = sb("spread", [128, C]), sb("deviation", [128, C]), sb("inverse", [128, C])
        scale, moved, shift = sb("scale", [128, C]), sb("moved", [128, C]), sb("shift", [128, C])
        loaded, moments_done, spread_done, deviation_done, inverse_done, scale_done, moved_done, shift_done, \
            normed, stored = (
                k.sem(f"{what}_{name}") for what in ("loaded", "moments_done", "spread_done", "deviation_done",
                                                     "inverse_done", "scale_done", "moved_done", "shift_done", "normed",
                                                     "stored"))
        block = ctx.enter_context(nc.Block(name))

        @block.sync
        def _(sp):
            sp.dma_start(g[:], gamma.rearrange("(c p) -> p c", p=128), allow_slow_non_contiguous=True).then_inc(loaded, 16)
            sp.dma_start(b[:], beta.rearrange("(c p) -> p c", p=128), allow_slow_non_contiguous=True).then_inc(loaded, 16)
            if x_cols is not None:
                for c in range(C):
                    sp.wait_ge(normed, c + 1)
                    sp.dma_start(x_cols[c * 128:(c + 1) * 128, :], y[:, c]).then_inc(stored, 16)
                sp.wait_ge(stored, (16 * C))

        @block.vector
        def _(dve):
            for c in range(C):
                done = dve.bn_aggr(moments[:, c], stats[:, c].rearrange("p i v -> p (i v)"))
            done.then_inc(moments_done, 1)
            dve.wait_ge(moments_done, 1)
            dve.tensor_scalar(spread[:], moments[:, :, 1], EPS, None, ALU.add).then_inc(spread_done, 1)
            dve.wait_ge(deviation_done, 1)
            dve.reciprocal(inverse[:], deviation[:]).then_inc(inverse_done, 1)
            dve.wait_ge(inverse_done, 1)
            dve.wait_ge(loaded, 32)
            dve.tensor_tensor(scale[:], inverse[:], g[:], ALU.mult).then_inc(scale_done, 1)
            dve.wait_ge(scale_done, 1)
            dve.tensor_tensor(moved[:], moments[:, :, 0], scale[:], ALU.mult).then_inc(moved_done, 1)
            dve.wait_ge(moved_done, 1)
            dve.tensor_tensor(shift[:], b[:], moved[:], ALU.subtract).then_inc(shift_done, 1)
            dve.wait_ge(shift_done, 1)
            for c in range(C):
                dve.tensor_scalar(y[:, c], y[:, c], scale[:, c:c + 1], shift[:, c:c + 1], ALU.mult, ALU.add
                                  ).then_inc(normed, 1)

        @block.scalar
        def _(act):
            act.preload_act_table_set("sqrt_and_others")
            act.wait_ge(spread_done, 1)
            act.activation(deviation[:], spread[:], ACT.Sqrt).then_inc(deviation_done, 1)


def stage_final(k, x_cols, ln_g, ln_b, x_rows, out):
    nc, P, T, N, D = k.nc, k.P, k.T, k.N, k.D
    C = D // 128
    with k.stage("stage_final") as ctx:
        def sb(what, shape, dt=F32):
            return ctx.enter_context(nc.sbuf_tensor(f"{what}_fin", shape, dt))

        cols = sb("cols", [128, C, N])
        z, x1 = sb("z", [P, T, D]), sb("x1", [P, T, D])
        g, b = sb("g", [P, D]), sb("b", [P, D])
        stats, moments = sb("stats", [P, T, 6]), [sb(f"moments{r}", [P, T, 2]) for r in range(2)]
        spread, deviation = [[sb(f"{what}{r}", [P, T]) for r in range(2)] for what in ("spread", "deviation")]
        inverse = [sb(f"inverse{r}", [P, T]) for r in range(2)]
        x1_loaded, gb_loaded, turned, saved, stats_done, moments_done, spread_done, deviation_done, \
            inverse_done, normed, gained, shifted, added, out_stored = (
                k.sem(f"{what}_fin") for what in ("x1_loaded", "gb_loaded", "turned", "saved", "stats_done",
                                                  "moments_done", "spread_done", "deviation_done", "inverse_done",
                                                  "normed", "gained", "shifted", "added", "out_stored"))
        PARTS = 5
        cols_loaded = [k.sem(f"cols_loaded{i}_fin") for i in range(PARTS)]
        block = ctx.enter_context(nc.Block("final"))

        def bank(slot):
            return k.psum[0:P, slot * BANK:(slot + 1) * BANK]

        @block.sync
        def _(sp):
            for i in range(PARTS):
                nodes = slice(i * N // PARTS, (i + 1) * N // PARTS)
                sp.dma_start(cols[:, :, nodes], x_cols.rearrange("(c p) n -> p c n", p=128)[:, :, nodes]).then_inc(cols_loaded[i], 16)
            for v, w in ((g, ln_g), (b, ln_b)):
                sp.dma_start(v[:], w.rearrange("(o d) -> o d", o=1).to_broadcast([P, D])).then_inc(gb_loaded, 16)
            sp.dma_start(x1[:], x_rows.rearrange("(t p) d -> p t d", p=P)).then_inc(x1_loaded, 16)
            with sp.Fori(0, T) as t:
                sp.wait_ge(normed, t + 1)
                sp.dma_start(out[bass.ds(t * P, P), :], z[:, t, :]).then_inc(out_stored, 16)
            sp.wait_ge(out_stored, 16 * T)

        @block.tensor
        def _(pe):
            for t in range(T):
                pe.wait_ge(cols_loaded[t * PARTS // T], 16)
                if t >= 2:
                    pe.wait_ge(saved, t - 1)
                for c in range(C):
                    block_t = pe.transpose(bank(t % 2)[:, c * 128:(c + 1) * 128], cols[:, c, t * P:(t + 1) * P], k.ident[:])
                block_t.then_inc(turned, 1)

        @block.scalar
        def _(act):
            act.preload_act_table_set("sqrt_and_others")

            def step(s):
                wait_item(act, turned, s)
                act.copy(z[:, s.item, :], bank(s.slot)).then_inc(saved, 1)

            run_steps(act, T, 0, step)
            for r in range(2):
                act.wait_ge(spread_done, r + 1)
                act.activation(deviation[r][:], spread[r][:], ACT.Sqrt).then_inc(deviation_done, 1)

        @block.gpsimd
        def _(pool):
            pool.wait_ge(gb_loaded, 32)
            pool.wait_ge(x1_loaded, 16)
            for t in range(T):
                pool.tensor_tensor(x1[:, t], x1[:, t], b[:], ALU.add).then_inc(shifted, 1)

        @block.vector
        def _(dve):
            def invert(r):
                dve.wait_ge(stats_done, (r + 1) * T)
                for t in range(T):
                    dve.bn_aggr(moments[r][:, t], stats[:, t]).then_inc(moments_done, 1)
                dve.wait_ge(moments_done, (r + 1) * T)
                dve.tensor_scalar(spread[r][:], moments[r][:, :, 1], EPS, None, ALU.add).then_inc(spread_done, 1)
                dve.wait_ge(deviation_done, r + 1)
                dve.reciprocal(inverse[r][:], deviation[r][:]).then_inc(inverse_done, 1)
                dve.wait_ge(inverse_done, r + 1)

            with dve.Fori(0, T) as t:
                dve.wait_ge(saved, t + 1)
                dve.bn_stats(stats[:, t, :], z[:, t, :]).then_inc(stats_done, 1)
            invert(0)
            dve.wait_ge(gb_loaded, 32)

            def step(s):
                if s.live():
                    dve.scalar_tensor_tensor(z[:, s.item, :], z[:, s.item, :], moments[0][:, s.item, 0:1], g[:],
                                             ALU.subtract, ALU.mult).then_inc(gained, 1)
                s = s.back(1)
                if s.live():
                    wait_item(dve, gained, s)
                    wait_item(dve, shifted, s)
                    dve.scalar_tensor_tensor(z[:, s.item, :], z[:, s.item, :], inverse[0][:, bass.ds(s.item, 1)], x1[:, s.item, :],
                                             ALU.mult, ALU.add).then_inc(added, 1)
                s = s.back(1)
                if s.live():
                    wait_item(dve, added, s)
                    dve.bn_stats(stats[:, s.item, :], z[:, s.item, :]).then_inc(stats_done, 1)

            run_steps(dve, T, 2, step)
            invert(1)
            for t in range(T):
                dve.tensor_scalar(z[:, t], z[:, t], moments[1][:, t, 0:1], inverse[1][:, t:t + 1], ALU.subtract, ALU.mult
                                  ).then_inc(normed, 1)


def build(nc, **a):
    src, dst, x = a["src"], a["dst"], a["x"]
    k = Kernel(nc, x, src)
    P, T, N, D, H = k.P, k.T, k.N, k.D, k.H
    with k.ctx:
        k.psum = k.ctx.enter_context(nc.psum_tensor("banks", [128, 8 * BANK], F32))
        k.ident = k.sb("ident", [128, 128])
        k.ones = k.sb("ones", [128, 1])
        k.edges_found = k.sb("edges_found", [1, 1], I32)
        k.log_counts = k.sb("log_counts", [P, T, N])
        diag_ctx = k.ctx.enter_context(ExitStack())
        k.plain_diag = diag_ctx.enter_context(nc.sbuf_tensor("plain_diag", [P, T, P], F32))

        with ExitStack() as edge_ctx:
            share = k.chunks // T
            window = -(-(share + 4) // 3) * 3
            k.pad_left = (window - share) // 2
            k.node_row = edge_ctx.enter_context(nc.sbuf_tensor("node_row", [128, N], F16))
            k.minus_targets = edge_ctx.enter_context(
                nc.sbuf_tensor("minus_targets", [P, k.chunks + window - share], F32))
            k.end_cols = edge_ctx.enter_context(
                nc.sbuf_tensor("end_cols", [P, 2, k.chunks + window - share], F32))
            stage_edges(k, src, dst)
            stage_count(k, "count_windows", lambda t: t * share, window, window // 3, verify=True)
            found = nc.values_load(k.edges_found[0:1, 0:1], min_val=0, max_val=k.E)
            with nc.If(found < k.E):
                nc.gpsimd.nop()
                nc.sync.nop()
                stage_count(k, "count_all", lambda t: k.pad_left, k.chunks, divisor(k.chunks, 8), verify=False)
            stage_logs(k)
        hidden = H * a["L0_gnn_att_src1"].shape[1]
        classes = H * a["L0_gnn_att_src2"].shape[1]
        gat1_rows = k.dram("gat1_rows", [N, hidden])
        gat2_rows = k.dram("gat2_rows", [N, classes])
        a_src_rows = k.dram("a_src_rows", [H, N])
        for name, rows, width, w, att_src, att_dst, row_bias, out_rows in (
                ("gat1", x, hidden, a["L0_gnn_W1"], a["L0_gnn_att_src1"], a["L0_gnn_att_dst1"], None, gat1_rows),
                ("gat2", gat1_rows, classes, a["L0_gnn_W2"], a["L0_gnn_att_src2"], a["L0_gnn_att_dst2"], a["L0_gnn_b1"], gat2_rows)):
            with ExitStack() as gat_ctx:
                h_sb = gat_ctx.enter_context(nc.sbuf_tensor(f"h_{name}", [P, T, width], F32))
                a_dst = gat_ctx.enter_context(nc.sbuf_tensor(f"a_dst_{name}", [P, T, H], F32))
                stage_gat_project(k, name, rows, row_bias, w, att_src, att_dst, h_sb, a_dst, a_src_rows)
                stage_gat_attend(k, name, h_sb, a_dst, a_src_rows, out_rows)
        x_rows = k.dram("x_rows", [N, D])
        x_cols = k.dram("x_cols", [D, N])
        stage_gat_finish(k, gat2_rows, a["L0_gnn_b2"], x, x_rows, x_cols)
        diag_ctx.close()
        w = {name: a[f"L1_gnn_{name}"] for name in ("Wq", "Wk", "Wv", "Wo", "W1", "W2", "bq", "bo", "b1", "b2",
                                                    "g1", "beta1", "g2", "beta2")}
        C, F, CH = D // 128, w["W1"].shape[1] // 128, D // H
        q_halves = k.dram("q_halves", [D, 2, N])
        att_cols = k.dram("att_cols", [D, N])
        with nc.Fori(0, w["Wq"].shape[0]) as layer, ExitStack() as ctx:
            Wq, Wk, Wv, Wo, W1, W2 = (w[name][layer] for name in ("Wq", "Wk", "Wv", "Wo", "W1", "W2"))
            k_halves = ctx.enter_context(nc.sbuf_tensor("k_halves", [2 * CH, H, N], F32R))
            v_rows = ctx.enter_context(nc.sbuf_tensor("v_rows", [P, T, D], F32))
            with ExitStack() as w_ctx:
                wq, wk, wv = (halves(nc, w_ctx, name, C, D) for name in ("wq", "wk", "wv"))
                with ExitStack() as rows_ctx:
                    rows, loads = weight_rows(k, rows_ctx, "qkv", (Wq, Wk, Wv))
                    stage_turn_weights(k, "qkv", rows, loads, [(Wq, *wq), (Wk, *wk), (Wv, *wv)])
                stage_qkv(k, x_cols, wq, wk, wv, w["bq"][layer], q_halves, k_halves, v_rows)
            rows, loads = weight_rows(k, ctx, "rest", (Wo, W1, W2))
            stage_attend(k, q_halves, k_halves, v_rows, att_cols, loads)
            y = ctx.enter_context(nc.sbuf_tensor("y", [128, C, N], F32))
            stats = ctx.enter_context(nc.sbuf_tensor("chunk_stats", [128, C, T // 2, 6], F32))
            wo, w1, w2 = (halves(nc, ctx, *v) for v in (("wo", C, D), ("w1", C, F * 128), ("w2", F, D)))
            stage_turn_weights(k, "rest", rows, (), [(Wo, *wo), (W1, *w1), (W2, *w2)])
            stage_out(k, att_cols, x_cols, wo, w["bo"][layer], y, stats)
            stage_batch_norm(k, "norm1", w["g1"][layer], w["beta1"][layer], stats, y, None)
            stage_feed_forward(k, w1, w["b1"][layer], w2, w["b2"][layer], y, stats)
            stage_batch_norm(k, "norm2", w["g2"][layer], w["beta2"][layer], stats, y, x_cols)
        stage_final(k, x_cols, a["L1_gnn_ln_g"], a["L1_gnn_ln_b"], x_rows, a["out"])



INPUTS = ("x", "src", "dst") + tuple(f"L0_gnn_{name}" for name in (
    "W1", "att_src1", "att_dst1", "b1", "W2", "att_src2", "att_dst2", "b2")) + tuple(f"L1_gnn_{name}" for name in (
        "Wq", "bq", "Wk", "Wv", "Wo", "bo", "W1", "b1", "W2", "b2", "g1", "beta1", "g2", "beta2", "ln_g", "ln_b"))


def kernel(**inputs):
    import numpy as np
    import concourse.bacc as bacc
    from concourse.bass_utils import run_bass_kernel_spmd

    nc = bacc.Bacc("TRN2", target_bir_lowering=False, num_devices=1)
    arrays, args = {}, {}
    for name in INPUTS:
        array = np.ascontiguousarray(inputs[name])
        arrays[f"in_{name}_dram"] = array
        args[name] = nc.dram_tensor(f"in_{name}_dram", array.shape, mybir.dt.from_np(array.dtype), kind="ExternalInput").ap()
    args["out"] = nc.dram_tensor("out_0_dram", inputs["x"].shape, F32, kind="ExternalOutput").ap()
    build(nc, **args)
    result = run_bass_kernel_spmd(nc, [arrays], core_ids=[0])
    return result.results[0]["out_0_dram"]
```
